# Optimizing a Trainium2 kernel written in Bass

```python
import numpy as np
import jax
import jax.numpy as jnp

def _softmax(x, axis=-1):
    return jax.nn.softmax(x, axis=axis)

def _gelu(x):
    return jax.nn.gelu(x, approximate=True)

def _silu(x):
    return jax.nn.silu(x)

def _sigmoid(x):
    return jax.nn.sigmoid(x)

def _layernorm(x, axis=-1, eps=1e-05):
    m = jnp.mean(x, axis=axis, keepdims=True)
    v = jnp.var(x, axis=axis, keepdims=True)
    return (x - m) / jnp.sqrt(v + eps)

def _scatter_add(tgt, idx, src, axis=0):
    return tgt.at[idx].add(src)

def _segment_sum(src, seg, n):
    return jax.ops.segment_sum(src, seg, n)
kernel_name = 'mk_flamingo_gated_d2_seqx_r4_e4fdab'

def setup_inputs(seed: int=0):
    np.random.seed(seed)
    _w = jnp.asarray

    def _rec_inputs():
        import jax
        import jax.numpy as jnp
        _rk = jax.random.key(seed)
        x = -0.0002928 + 1 * jax.random.normal(jax.random.fold_in(_rk, 1), (4, 1024, 256), jnp.float32)
        _lenS = 1024 - jax.random.randint(jax.random.fold_in(_rk, 7), (4,), 0, max(1, 1024 // 4) + 1, jnp.int32)
        _lenS2 = 77 - jax.random.randint(jax.random.fold_in(_rk, 8), (4,), 0, max(1, 77 // 4) + 1, jnp.int32)
        _ctx_1024P = jax.random.normal(jax.random.fold_in(_rk, 11), (4, 16, 256), jnp.float32)
        _ctx_1024c = jax.random.dirichlet(jax.random.fold_in(_rk, 511), 0.3 * jnp.ones((16,), jnp.float32), (4, 77))
        _ctx_1024t = jnp.einsum('bsk,bkd->bsd', _ctx_1024c, _ctx_1024P)
        _ctx_1024t = _ctx_1024t * jax.lax.rsqrt(jnp.mean(jnp.square(_ctx_1024t)) + 1e-12) * 0.953939
        ctx_1024 = -1.39393e-06 + 0.999914 * (_ctx_1024t + 0.3 * jax.random.normal(jax.random.fold_in(_rk, 611), (4, 77, 256), jnp.float32))
        _g = jax.random.normal(jax.random.fold_in(_rk, 9001), (2, 2), jnp.float32)
        _g = jnp.sign(_g) * jnp.maximum(jnp.abs(_g), 1.0) + (_g == 0) * 1.0
        g_xattn = _g[0]
        g_ffn = _g[1]
        return (x, ctx_1024, g_xattn, g_ffn)
    x, ctx_1024, g_xattn, g_ffn = _rec_inputs()

    def _L0_xattn_setup():
        import jax, jax.numpy as jnp
        import numpy as np
        B, NQ, NK = (2, 512, 512)
        DIM_Q = DIM_KV = DIM_E = DIM_O = 256
        H = 16
        HD = DIM_E // H
        SCALE = HD ** (-0.5)
        key = jax.random.key(seed)
        ks = jax.random.split(key, 8)
        inp = {'query': jax.random.normal(ks[0], (B, NQ, DIM_Q), dtype=jnp.float32), 'key': jax.random.normal(ks[1], (B, NK, DIM_KV), dtype=jnp.float32), 'value': jax.random.normal(ks[2], (B, NK, DIM_KV), dtype=jnp.float32), 'Wq': jax.random.normal(ks[3], (DIM_Q, DIM_E), dtype=jnp.float32) * DIM_Q ** (-0.5), 'Wk': jax.random.normal(ks[4], (DIM_KV, DIM_E), dtype=jnp.float32) * DIM_KV ** (-0.5), 'Wv': jax.random.normal(ks[5], (DIM_KV, DIM_E), dtype=jnp.float32) * DIM_KV ** (-0.5), 'Wo': jax.random.normal(ks[6], (DIM_E, DIM_O), dtype=jnp.float32) * DIM_E ** (-0.5), 'bo': jax.random.normal(ks[7], (DIM_O,), dtype=jnp.float32) * 0.01}
        return inp
    _L0_xattn_all = _L0_xattn_setup()
    _L0_xattn_in = {k: v for k, v in _L0_xattn_all.items() if k in ('Wq', 'Wk', 'Wv', 'Wo', 'bo')}
    del _L0_xattn_all

    def _L0_ffn_setup():
        import jax, jax.numpy as jnp
        import numpy as np
        EPS = 1e-05

        def rmsnorm(x):
            var = jnp.mean(jnp.square(x), axis=-1, keepdims=True)
            return x * jax.lax.rsqrt(var + 1e-06)

        def activation_quant(x):
            scale = 127.0 / jnp.clip(jnp.max(jnp.abs(x), axis=-1, keepdims=True), EPS, None)
            return jnp.clip(jnp.round(x * scale), -128, 127) / scale

        def weight_quant(w):
            scale = 1.0 / jnp.clip(jnp.mean(jnp.abs(w)), EPS, None)
            return jnp.clip(jnp.round(w * scale), -1, 1) / scale

        def bitlinear(x, w, b):
            xn = rmsnorm(x)
            xq = xn + jax.lax.stop_gradient(activation_quant(xn) - xn)
            wq = w + jax.lax.stop_gradient(weight_quant(w) - w)
            return jnp.einsum('bsi,oi->bso', xq, wq) + b
        key = jax.random.key(seed)
        k1, k2, k3 = jax.random.split(key, 3)
        B, S, D, H = (4, 512, 256, 1024)
        x = jax.random.normal(k1, (B, S, D), dtype=jnp.float32)
        w1 = jax.random.normal(k2, (H, D), dtype=jnp.float32) * D ** (-0.5)
        b1 = jnp.zeros((H,), dtype=jnp.float32)
        w2 = jax.random.normal(k3, (D, H), dtype=jnp.float32) * H ** (-0.5)
        b2 = jnp.zeros((D,), dtype=jnp.float32)
        return {'x': x, 'w1': w1, 'b1': b1, 'w2': w2, 'b2': b2}
    _L0_ffn_all = _L0_ffn_setup()
    _L0_ffn_in = {k: v for k, v in _L0_ffn_all.items() if k in ('w1', 'b1', 'w2', 'b2')}
    del _L0_ffn_all

    def _L1_xattn_setup():
        import jax, jax.numpy as jnp
        import numpy as np
        D_MODEL = 256
        NUM_HEADS = 16
        D_K = D_MODEL // NUM_HEADS

        def _split_heads(x):
            B, S, _ = x.shape
            return x.reshape(B, S, NUM_HEADS, D_K).transpose(0, 2, 1, 3)
        key = jax.random.key(seed)
        ks = jax.random.split(key, 11)
        B, S = (2, 512)
        scale = 1.0 / np.sqrt(D_MODEL)
        inp = {'q': jax.random.normal(ks[0], (B, S, D_MODEL), jnp.float32), 'k': jax.random.normal(ks[1], (B, S, D_MODEL), jnp.float32), 'v': jax.random.normal(ks[2], (B, S, D_MODEL), jnp.float32), 'Wq': jax.random.normal(ks[3], (D_MODEL, D_MODEL), jnp.float32) * scale, 'bq': jnp.zeros((D_MODEL,), jnp.float32), 'Wk': jax.random.normal(ks[4], (D_MODEL, D_MODEL), jnp.float32) * scale, 'bk': jnp.zeros((D_MODEL,), jnp.float32), 'Wv': jax.random.normal(ks[5], (D_MODEL, D_MODEL), jnp.float32) * scale, 'bv': jnp.zeros((D_MODEL,), jnp.float32), 'Wo': jax.random.normal(ks[6], (D_MODEL, D_MODEL), jnp.float32) * scale, 'bo': jnp.zeros((D_MODEL,), jnp.float32)}
        return inp
    _L1_xattn_all = _L1_xattn_setup()
    _L1_xattn_in = {k: v for k, v in _L1_xattn_all.items() if k in ('Wq', 'bq', 'Wk', 'bk', 'Wv', 'bv', 'Wo', 'bo')}
    del _L1_xattn_all

    def _L1_ffn_setup():
        import jax, jax.numpy as jnp
        import numpy as np
        B, S, H, M, E, K = (4, 512, 256, 1024, 8, 2)
        key = jax.random.key(seed)
        ks = jax.random.split(key, 6)
        x = jax.random.normal(ks[0], (B, S, H), dtype=jnp.float32)
        Wr = jax.random.normal(ks[1], (E, H), dtype=jnp.float32) * (1.0 / np.sqrt(H))
        W1 = jax.random.normal(ks[2], (E, M, H), dtype=jnp.float32) * np.sqrt(2.0 / (H + M))
        b1 = jax.random.normal(ks[3], (E, M), dtype=jnp.float32) * 1e-06
        W2 = jax.random.normal(ks[4], (E, H, M), dtype=jnp.float32) * np.sqrt(2.0 / (H + M))
        b2 = jax.random.normal(ks[5], (E, H), dtype=jnp.float32) * 1e-06
        return {'x': x, 'Wr': Wr, 'W1': W1, 'b1': b1, 'W2': W2, 'b2': b2}
    _L1_ffn_all = _L1_ffn_setup()
    _L1_ffn_in = {k: v for k, v in _L1_ffn_all.items() if k in ('Wr', 'W1', 'b1', 'W2', 'b2')}
    del _L1_ffn_all
    return {'x': x, 'ctx_1024': ctx_1024, 'g_xattn': g_xattn, 'g_ffn': g_ffn, 'L0_xattn_Wq': _L0_xattn_in['Wq'], 'L0_xattn_Wk': _L0_xattn_in['Wk'], 'L0_xattn_Wv': _L0_xattn_in['Wv'], 'L0_xattn_Wo': _L0_xattn_in['Wo'], 'L0_xattn_bo': _L0_xattn_in['bo'], 'L0_ffn_w1': _L0_ffn_in['w1'], 'L0_ffn_b1': _L0_ffn_in['b1'], 'L0_ffn_w2': _L0_ffn_in['w2'], 'L0_ffn_b2': _L0_ffn_in['b2'], 'L1_xattn_Wq': _L1_xattn_in['Wq'], 'L1_xattn_bq': _L1_xattn_in['bq'], 'L1_xattn_Wk': _L1_xattn_in['Wk'], 'L1_xattn_bk': _L1_xattn_in['bk'], 'L1_xattn_Wv': _L1_xattn_in['Wv'], 'L1_xattn_bv': _L1_xattn_in['bv'], 'L1_xattn_Wo': _L1_xattn_in['Wo'], 'L1_xattn_bo': _L1_xattn_in['bo'], 'L1_ffn_Wr': _L1_ffn_in['Wr'], 'L1_ffn_W1': _L1_ffn_in['W1'], 'L1_ffn_b1': _L1_ffn_in['b1'], 'L1_ffn_W2': _L1_ffn_in['W2'], 'L1_ffn_b2': _L1_ffn_in['b2']}

def reference(x, ctx_1024, g_xattn, g_ffn, L0_xattn_Wq, L0_xattn_Wk, L0_xattn_Wv, L0_xattn_Wo, L0_xattn_bo, L0_ffn_w1, L0_ffn_b1, L0_ffn_w2, L0_ffn_b2, L1_xattn_Wq, L1_xattn_bq, L1_xattn_Wk, L1_xattn_bk, L1_xattn_Wv, L1_xattn_bv, L1_xattn_Wo, L1_xattn_bo, L1_ffn_Wr, L1_ffn_W1, L1_ffn_b1, L1_ffn_W2, L1_ffn_b2):
    import jax
    import jax.numpy as jnp

    def _L0_xattn_ref(query, key, value, Wq, Wk, Wv, Wo, bo):
        import jax, jax.numpy as jnp
        import numpy as np
        B, NQ, NK = (2, 512, 512)
        DIM_Q = DIM_KV = DIM_E = DIM_O = 256
        H = 16
        HD = DIM_E // H
        SCALE = HD ** (-0.5)
        b, nq, _ = query.shape
        nk = key.shape[1]
        q = (query @ Wq).reshape(b, nq, H, HD).transpose(0, 2, 1, 3)
        k = (key @ Wk).reshape(b, nk, H, HD).transpose(0, 2, 1, 3)
        v = (value @ Wv).reshape(b, nk, H, HD).transpose(0, 2, 1, 3)
        attn = jnp.einsum('bhqd,bhkd->bhqk', q, k) * SCALE
        attn = jax.nn.softmax(attn, axis=-1)
        x = jnp.einsum('bhqk,bhkd->bhqd', attn, v)
        x = x.transpose(0, 2, 1, 3).reshape(b, nq, H * HD)
        return x @ Wo + bo

    def _L0_ffn_ref(x, w1, b1, w2, b2):
        import jax, jax.numpy as jnp
        import numpy as np
        EPS = 1e-05

        def rmsnorm(x):
            var = jnp.mean(jnp.square(x), axis=-1, keepdims=True)
            return x * jax.lax.rsqrt(var + 1e-06)

        def activation_quant(x):
            scale = 127.0 / jnp.clip(jnp.max(jnp.abs(x), axis=-1, keepdims=True), EPS, None)
            return jnp.clip(jnp.round(x * scale), -128, 127) / scale

        def weight_quant(w):
            scale = 1.0 / jnp.clip(jnp.mean(jnp.abs(w)), EPS, None)
            return jnp.clip(jnp.round(w * scale), -1, 1) / scale

        def bitlinear(x, w, b):
            xn = rmsnorm(x)
            xq = xn + jax.lax.stop_gradient(activation_quant(xn) - xn)
            wq = w + jax.lax.stop_gradient(weight_quant(w) - w)
            return jnp.einsum('bsi,oi->bso', xq, wq) + b
        h = bitlinear(x, w1, b1)
        h = jax.nn.gelu(h, approximate=False)
        return bitlinear(h, w2, b2)

    def _L1_xattn_ref(q, k, v, Wq, bq, Wk, bk, Wv, bv, Wo, bo):
        import jax, jax.numpy as jnp
        import numpy as np
        D_MODEL = 256
        NUM_HEADS = 16
        D_K = D_MODEL // NUM_HEADS

        def _split_heads(x):
            B, S, _ = x.shape
            return x.reshape(B, S, NUM_HEADS, D_K).transpose(0, 2, 1, 3)
        Q = _split_heads(q @ Wq.T + bq)
        K = _split_heads(k @ Wk.T + bk)
        V = _split_heads(v @ Wv.T + bv)
        scores = jnp.einsum('bhqd,bhkd->bhqk', Q, K) / jnp.sqrt(jnp.float32(D_K))
        attn = jax.nn.softmax(scores, axis=-1)
        ctx = jnp.einsum('bhqk,bhkd->bhqd', attn, V)
        B, H, S, dk = ctx.shape
        ctx = ctx.transpose(0, 2, 1, 3).reshape(B, S, D_MODEL)
        return ctx @ Wo.T + bo

    def _L1_ffn_ref(x, Wr, W1, b1, W2, b2):
        import jax, jax.numpy as jnp
        import numpy as np
        B, S, H, M, E, K = (4, 512, 256, 1024, 8, 2)
        logits = jnp.einsum('bsh,eh->bse', x, Wr)
        probs = jax.nn.softmax(logits, axis=-1)
        top_v, top_i = jax.lax.top_k(probs, K)
        top_v = top_v / jnp.sum(top_v, axis=-1, keepdims=True)
        out = jnp.zeros_like(x)
        for e in range(E):
            w_e = jnp.sum(jnp.where(top_i == e, top_v, 0.0), axis=-1)
            h = jnp.einsum('bsh,mh->bsm', x, W1[e]) + b1[e]
            h = jax.nn.gelu(h, approximate=False)
            y = jnp.einsum('bsm,hm->bsh', h, W2[e]) + b2[e]
            out = out + y * w_e[..., None]
        return out
    x = x + jnp.tanh(g_xattn[0]) * _L0_xattn_ref(_layernorm(x, axis=-1), ctx_1024, ctx_1024, L0_xattn_Wq, L0_xattn_Wk, L0_xattn_Wv, L0_xattn_Wo, L0_xattn_bo)
    x = x + jnp.tanh(g_ffn[0]) * _L0_ffn_ref(_layernorm(x, axis=-1), L0_ffn_w1, L0_ffn_b1, L0_ffn_w2, L0_ffn_b2)
    x = x + jnp.tanh(g_xattn[1]) * _L1_xattn_ref(_layernorm(x, axis=-1), ctx_1024, ctx_1024, L1_xattn_Wq, L1_xattn_bq, L1_xattn_Wk, L1_xattn_bk, L1_xattn_Wv, L1_xattn_bv, L1_xattn_Wo, L1_xattn_bo)
    x = x + jnp.tanh(g_ffn[1]) * _L1_ffn_ref(_layernorm(x, axis=-1), L1_ffn_Wr, L1_ffn_W1, L1_ffn_b1, L1_ffn_W2, L1_ffn_b2)
    return x

_drawn_inputs = setup_inputs


def setup_inputs(seed=0):
    import zlib

    import numpy as np

    out = dict(_drawn_inputs(seed))
    spreads = {'g_ffn': (-1.0, 0.6),
     'L0_ffn_b1': (0.0, 0.1),
     'L0_ffn_b2': (0.0, 0.1),
     'L1_xattn_bq': (0.0, 0.28),
     'L1_xattn_bk': (0.0, 0.8),
     'L1_xattn_bv': (0.0, 0.1),
     'L1_xattn_bo': (0.0, 0.1)}
    factors = {'L0_xattn_bo': 3.645, 'L1_ffn_b1': 8.0, 'L1_ffn_b2': 8.0}
    for name, (base, spread) in spreads.items():
        noise = np.random.default_rng([zlib.crc32(name.encode()), seed]).standard_normal(out[name].shape)
        drawn = base * np.exp(spread * noise) if base else spread * noise
        out[name] = jnp.asarray(drawn.astype(out[name].dtype))
    for name, factor in factors.items():
        out[name] = (out[name] * factor).astype(out[name].dtype)
    return out
```

```python
import numpy as np
import concourse.bass as bass
from concourse import mybir
from contextlib import ExitStack

F32, F16, BF16 = mybir.dt.float32, mybir.dt.float16, mybir.dt.bfloat16
I32, U32, U16 = mybir.dt.int32, mybir.dt.uint32, mybir.dt.uint16
ACT, ALU, AX = mybir.ActivationFunctionType, mybir.AluOpType, mybir.AxisListType

P = 128
B, S, D = 4, 1024, 256
NT = B * S // P
TB = S // P
GT = 4
GN = GT * P
NG = NT // GT
KC = D // P
H, HD, NK = 16, 16, 77
HG = P // HD
FK = HG * NK
NC5 = -(-FK // P)
ROWS = [min(P, FK - P * c) for c in range(NC5)]
HEAD0 = [min(P * c // NK, HG - 3) for c in range(NC5)]
VW = HD + 1
M = 1024
MC = M // P
E, TOPK = 8, 2
ST = 256
NST = (B * S * TOPK + E * (ST - 1)) // ST
NSP = NST + 3
NSC = NSP * ST // P
ROWW = 2 * D + 2 * E
WS = 32.0
MAGIC = 1.5 * 2.0 ** 23
HALF, MAGIC_H = 1536.0, MAGIC + 0x6600
LN_EPS, RMS_EPS, Q_EPS = 1e-5, 1e-6, 1e-5
NPB = 4
LATE = 3
CODE0 = 0x0400
NPC = 4
PC = TOPK * NT // NPC
FAR = 65536.0

C_MASKK, C_MASKV, C_ONE = 0, HG, HG + 6 * NC5
C_CODE, C_IOTA, C_END = HG + 12 * NC5, HG + 12 * NC5 + NT, HG + 12 * NC5 + NT + P
H_IDF, H_IDB, H_UP, H_ONES, H_END = 0, P, 2 * P, 3 * P, 4 * P


def build(nc, x, ctxT, g_att, g_ffn, attn_w, attn_bcol, attn_brow, fw1, fb1, fw2, fb2,
          wr, ew1, eb1, ew2, eb2, c32, c16, ind, selk, out):
    es = ExitStack()
    with es:
        def sb(name, shape, dt):
            return es.enter_context(nc.sbuf_tensor(name, shape, dt))

        sems = {}

        def sem(name):
            if name not in sems:
                sems[name] = es.enter_context(nc.semaphore(name))
            return sems[name]

        def after(engine, name, value):
            if not isinstance(value, int) or value > 0:
                engine.wait_ge(sem(name), value)

        def hold(engine, name, value):
            after(engine, name, value)
            if not isinstance(value, int):
                engine.sem_inc(sem("carrier"), 1)

        X = sb("X", [P, NT, D], F32)
        WE = sb("WE", [P, E, 8 * M], F16)
        k32 = sb("k32", [P, C_END], F32)
        k16 = sb("k16", [P, H_END], U16)
        indt = sb("indt", [16, KC * FK], U16)
        gsc = sb("gsc", [P, 8], F32)
        gsr = sb("gsr", [P, 4], F32)
        b1t = sb("b1t", [P, E * MC], F32)
        mhalf = sb("mhalf", [P, 8], F32)
        AREA = 10900
        late = WE[:, E - LATE:E, :].rearrange("p e n -> p (e n)").bitcast(F32)
        area = sb("area", [P, AREA], F32)

        class Arena:
            def __init__(self):
                self.a, self.l = 0, 0

            def take(self, shape, dt=F32, parts=P):
                n = int(np.prod(shape)) * (2 if dt in (F16, BF16, U16) else 4) // 4
                if self.l + n <= LATE * 4 * M:
                    ap, self.l = late[0:parts, self.l:self.l + n], self.l + n
                else:
                    assert self.a + n <= AREA, (self.a, n)
                    ap, self.a = area[0:parts, self.a:self.a + n], self.a + n
                if dt != F32:
                    ap = ap.bitcast(dt)
                if len(shape) == 1:
                    return ap
                names = "abcdef"[:len(shape)]
                pat = f"p ({' '.join(names)}) -> p {' '.join(names)}"
                return ap.rearrange(pat, **dict(zip(names[1:], shape[1:])))

        ps = es.enter_context(nc.psum_tensor("ps", [P, 8, 512], F32))
        idf = k16[:, H_IDF:H_IDF + P].bitcast(F16)
        idb = k16[:, H_IDB:H_IDB + P].bitcast(BF16)
        upper = k16[:, H_UP:H_UP + P].bitcast(BF16)
        onesb = k16[:, H_ONES:H_ONES + P].bitcast(BF16)
        indb = indt[:, :].bitcast(BF16).rearrange("h (g n) -> h g n", g=KC)
        maskk = k32[:, C_MASKK:C_MASKK + HG]
        maskv = k32[:, C_MASKV:C_MASKV + 6 * NC5]
        maskone = k32[:, C_ONE:C_ONE + 6 * NC5]
        code = k32[:, C_CODE:C_CODE + NT]
        iota = k32[:, C_IOTA:C_IOTA + P]
        GA = [0, 1]
        GF = [2, 3]
        GX = [4, 5]

        ar = Arena()
        KB = ar.take([B, 2, KC, FK], F16)
        V = ar.take([B, KC * NC5, 6 * VW], F16)
        WQ = ar.take([2, KC, D], F16)
        WO = ar.take([2, KC, D], F16)
        gbo = ar.take([D])
        bcol = ar.take([4])
        wst = ar.take([1024])
        xn = ar.take([GT, D])
        work0 = (ar.a, ar.l)
        stats = ar.take([TB, 6])
        mv = ar.take([TB, 2])
        rstd = ar.take([TB])
        xs = [ar.take([GT * D], F16) for _ in range(2)]
        xT = ar.take([2, KC, GN], F16)
        qT = ar.take([2, 2, KC, GN], F16)
        mx = ar.take([GT, H], BF16)
        mxT = ar.take([2, GN], BF16, 16)
        PT = ar.take([2, GN])
        PP = ar.take([NPB, 2, GN], F16)
        cx = ar.take([GT, D])
        cs = [ar.take([GT * D], F16) for _ in range(2)]
        cT = ar.take([2, KC, GN], F16)
        rec = ar.take([2, 2, HG])
        pr = Arena()
        pr.a, pr.l = work0
        wraw = pr.take([4, KC, D])
        sel = pr.take([FK], F16)
        vs = pr.take([B, 2, D], F16)
        cxt = pr.take([KC, B * NK])
        KT = pr.take([2, KC, B * NK], F16)
        bvr = pr.take([D], F32, 1)
        one1 = pr.take([P], F32, 1)
        bosr = pr.take([D])

        fr = Arena()
        w1q = fr.take([KC, M], F16)
        w2q = fr.take([MC, D], F16)
        fb1c = fr.take([M])
        fb2c = fr.take([D])
        fraw = fr.take([2, KC * M])
        y8 = fr.take([TB, D])
        xqT = fr.take([KC, TB * P], F16)
        hpre = fr.take([2, M])
        gl = fr.take([4, M])
        hqT = fr.take([2, MC, P], F16)
        fst = fr.take([TB, 6])
        fmv = fr.take([TB, 2])
        fsm = fr.take([8, TB])
        RS_, VE, R2, AM, INV, SC, DN, D1 = (fsm[:, k, :] for k in range(8))
        tsm = fr.take([8, 4])
        MS, RR, A2, IV2, S2, D2 = (tsm[:, k, :] for k in range(6))
        wsm = fr.take([8])
        onef = fr.take([P])
        fsq = fr.take([M], BF16)

        rr = Arena()
        rr.l = LATE * 4 * M
        wstg = rr.take([4, M])
        xr = rr.take([2, GT, 2 * D], F16)
        xrT = rr.take([2, KC, GN], F16)
        xsT0 = rr.a
        xsT = rr.take([2, 2, KC, ST], F16)
        rxn = area[:, xsT0:xsT0 + GT * D].rearrange("p (t d) -> p t d", t=GT)
        rst = area[:, xsT0 - NT * 6:xsT0].rearrange("p (t s) -> p t s", s=6)
        rmv, rrs = rr.take([NT, 2]), rr.take([NT])
        wrr = rr.take([KC, E])
        wrs = rr.take([2, KC, E], F16)
        lg = rr.take([NT, E])
        oh = rr.take([TOPK, NT, E])
        ta, tb = rr.take([NT, E]), rr.take([NT, E])
        gates = rr.take([NT, E])
        Mb = rr.take([NT, E], BF16)
        desc = rr.take([E])
        top, top_s = rr.take([TOPK, NT]), rr.take([NT])
        wts = rr.take([3, NT])
        pos, phi = rr.take([TOPK * NT]), rr.take([TOPK * NT])
        cnt, nb, ce, ce2, base_e = (rr.take([E]) for _ in range(5))
        idh = rr.take([NSC], F16)
        idn, idt = rr.take([NSC]), rr.take([NSC])
        gidx, sidx = rr.take([NSC]).bitcast(I32), rr.take([NSC]).bitcast(I32)
        exf, exi = rr.take([NSP]), rr.take([NSP]).bitcast(I32)
        gi2, si2 = rr.take([2, 2]).bitcast(I32), rr.take([2, 2]).bitcast(I32)
        gcur = rr.take([2, 2])
        xg_ = area[:, 4 * M:4 * M + 2 * 2 * (ROWW // 2)].bitcast(F16).rearrange("p (a s n) -> p a s n", a=2, s=2)
        xgf = area[:, 4 * M:4 * M + 2 * 2 * (ROWW // 2)].rearrange("p (a s n) -> p a s n", a=2, s=2)
        yb = area[:, 0:4 * D].rearrange("p (a s n) -> p a s n", a=2, s=2)
        xall = X[:].rearrange("p t d -> p (t d)")
        hid = xall[:, 0:4096].bitcast(F16).rearrange("p (a w n) -> p a w n", a=2, w=2)
        gel = xall[:, 4096:6144].rearrange("p (q n) -> p q n", q=4)
        b2t = xall[:, 6144:8192].rearrange("p (e n) -> p e n", e=E)
        ohL = [xall[:, b * 1024:(b + 1) * 1024].bitcast(F16).rearrange("p (i n) -> p i n", i=PC) for b in range(2)]
        ohH = [xall[:, 2048 + b * 1024:2048 + b * 1024 + PC * NSC // 2].bitcast(F16).rearrange("p (i n) -> p i n", i=PC) for b in range(2)]
        eflat = area
        cmpb = xall[:, 4096:4096 + NSP * E].rearrange("p (j e) -> p j e", e=E)
        rowsd = nc.dram_tensor("rows", (B * S, ROWW), U16, kind="Internal").ap()
        def low_halves(ap):
            return ap.bitcast(F16).rearrange("p (n two) -> p n two", two=2)[:, :, 0]
        block = es.enter_context(nc.Block())
        DL = {"dve": 0, "act": 0, "pool": 0}

        def gate(t, n):
            return ps[:, t:t + n, :]
        S0, PV0, WF, WT = 0, 2, 4, 6

        NSLOT = KC * NC5

        @block.sync
        def _(sp):
            sp.dma_start(k32[:], c32).then_inc(sem("c_in"), 16)
            sp.dma_start(k16[:], c16).then_inc(sem("c_in"), 16)
            sp.dma_start(indt[:], ind).then_inc(sem("c_in"), 16)
            sp.dma_start(gsr[:, 0:2], g_att.partition_broadcast(P)).then_inc(sem("c_in"), 16)
            sp.dma_start(gsr[:, 2:4], g_ffn.partition_broadcast(P)).then_inc(sem("c_in"), 16)
            sp.dma_start(b1t[:], eb1).then_inc(sem("c_in"), 16)

            def layer_loads(l):
                if l:
                    sp.wait_ge(sem("ffn_out"), NT)
                sp.dma_start(wraw, attn_w[l].rearrange("w (c p) n -> p w c n", p=P)).then_inc(sem("prep_in"), 16)
                sp.dma_start(cxt, ctxT.rearrange("(c p) n -> p c n", p=P)).then_inc(sem("prep_in"), 16)
                sp.dma_start(sel, selk.bitcast(F16)).then_inc(sem("prep_in"), 16)
                sp.dma_start(bcol, attn_bcol[l]).then_inc(sem("prep_in"), 16)
                sp.dma_start(bvr, attn_brow[l, 0:1, :]).then_inc(sem("prep_in"), 16)
                sp.dma_start(bosr, attn_brow[l, 1, :].partition_broadcast(P)).then_inc(sem("prep_in"), 16)
            for b in range(1):
                sp.dma_start(X[:, b * TB:(b + 1) * TB, :], x[b].rearrange("(t p) d -> p t d", p=P)).then_inc(sem("x_in"), 16)
            layer_loads(0)
            for b in range(1, B):
                sp.dma_start(X[:, b * TB:(b + 1) * TB, :], x[b].rearrange("(t p) d -> p t d", p=P)).then_inc(sem("x_in2"), 16)
            sp.wait_ge(sem("att_out"), 2 * NG)
            sp.dma_start(fraw[:, 0, :].rearrange("p (c n) -> p c n", c=KC), fw1.rearrange("(c p) n -> p c n", p=P)).then_inc(sem("fw_in"), 16)
            sp.dma_start(fraw[:, 1, :].rearrange("p (c n) -> p c n", c=MC), fw2.rearrange("(c p) n -> p c n", p=P)).then_inc(sem("fw_in"), 16)
            sp.dma_start(fb1c, fb1.partition_broadcast(P)).then_inc(sem("fw_in"), 16)
            sp.dma_start(fb2c, fb2.partition_broadcast(P)).then_inc(sem("fw_in"), 16)
            layer_loads(1)
            sp.wait_ge(sem("att_out"), 4 * NG)
            sp.dma_start(wrr, wr.rearrange("(c p) e -> p c e", p=P)).then_inc(sem("wr_in"), 16)
            xout = out.rearrange("(t p) d -> p t d", p=P)
            rout = rowsd.rearrange("(t p) n -> p t n", p=P)
            for g in range(NG):
                t = slice(g * GT, (g + 1) * GT)
                sp.wait_ge(sem("rlo_ready"), g + 1)
                sp.dma_start(rout[:, t, 0:2 * D], xr[:, g % 2].bitcast(U16)).then_inc(sem(("rows_even", "rows_odd")[g % 2]), 16)
                sp.dma_start(xout[:, t, :], X[:, t, :]).then_inc(sem("x_out"), 16)
            sp.wait_ge(sem("gates_ready"), 1)
            sp.dma_start(rout[:, :, 2 * D:], gates.rearrange("p t e -> p (t e)").bitcast(U16).rearrange("p (t e) -> p t e", t=NT)).then_inc(sem("gates_out"), 16)
            sp.wait_ge(sem("onehot_used"), NPC + 2)
            sp.wait_ge(sem("x_out"), 16 * NG)
            sp.dma_start(b2t, eb2.partition_broadcast(P)).then_inc(sem("b2_in"), 16)
            sp.wait_ge(sem("scattered"), 16 * 2 * NST)

        PREP_DMAS = 6

        @block.tensor
        def _(pe):
            T = nc.tensor

            def prep(l):
                pe.wait_ge(sem("prep_in"), 16 * PREP_DMAS * (l + 1))
                for m in range(KC):
                    for c in range(KC):
                        last = T.matmul(ps[:, m, 0:B * NK], wraw[:, 1, c, m * P:(m + 1) * P], cxt[:, c, :],
                                        start=c == 0, stop=c == KC - 1)
                    last.then_inc(sem("kt_ps"), 1)
                pe.wait_ge(sem("one_set"), l + 1)
                for b in range(B):
                    o = ps[0:NK, 4 + b, 0:D]
                    for k in range(KC):
                        T.matmul(o, cxt[:, k, b * NK:(b + 1) * NK], wraw[:, 2, k, :], start=k == 0, stop=False)
                    T.matmul(o, one1[:, 0:NK], bvr, start=False, stop=True).then_inc(sem("v_ps"), 1)
                for b in range(B):
                    pe.wait_ge(sem("vlo_ready"), B * l + b + 1)
                    pe.wait_ge(sem("klo_ready"), KC * (l + 1))
                    if b >= 2:
                        pe.wait_ge(sem("v_ready"), KC * (B * l + b - 1))
                    for g in range(KC):
                        for c in range(NC5):
                            col = g * P + HD * HEAD0[c]
                            last = T.matmul(ps[0:ROWS[c], 2 * (b % 2) + g, c * 96:(c + 1) * 96].rearrange("p (a n) -> p a n", a=2),
                                            sel[0:NK, c * P:c * P + ROWS[c]], vs[0:NK, b, :, col:col + 48],
                                            start=True, stop=True)
                        last.then_inc(sem("vsel_ps"), 1)

            def transposes(bank, src, rows=GT):
                dst = ps[:, bank, :].bitcast(F16).rearrange("p (c n) -> p c n", c=KC)
                sv = src.rearrange("p (t c n) -> p t c n", t=GT, c=KC)
                for c in range(KC):
                    for t in range(GT):
                        last = T.transpose(dst[:, c, t * P:(t + 1) * P], sv[:, t, c, :], idf)
                return last

            def query_jobs(l, i, b, par):
                gi = i + NG * l

                def x_hi():
                    pe.wait_ge(sem("xhi_ready"), gi + 1)
                    transposes(WF, xs[0]).then_inc(sem("xT_ps"), 1)

                def x_lo():
                    pe.wait_ge(sem("xlo_ready"), gi + 1)
                    transposes(WF + 1, xs[1]).then_inc(sem("xT_ps"), 1)

                def query(m):
                    pe.wait_ge(sem("xThi_ready"), gi + 1)
                    cols = slice(m * P, (m + 1) * P)
                    T.matmul(ps[:, WF + m, :], WQ[:, 0, 0, cols], xT[:, 0, 0, :], start=True, stop=False)
                    T.matmul(ps[:, WF + m, :], WQ[:, 0, 1, cols], xT[:, 0, 1, :], start=False, stop=False)
                    T.matmul(ps[:, WF + m, :], WQ[:, 1, 0, cols], xT[:, 0, 0, :], start=False, stop=False)
                    T.matmul(ps[:, WF + m, :], WQ[:, 1, 1, cols], xT[:, 0, 1, :], start=False, stop=False)
                    pe.wait_ge(sem("xTlo_ready"), gi + 1)
                    T.matmul(ps[:, WF + m, :], WQ[:, 0, 0, cols], xT[:, 1, 0, :], start=False, stop=False)
                    T.matmul(ps[:, WF + m, :], WQ[:, 0, 1, cols], xT[:, 1, 1, :], start=False, stop=True).then_inc(sem("q_ps"), 1)

                def q0():
                    query(0)

                def q1():
                    query(1)
                    
                def max_scores(n):
                    def run():
                        t, g = n // KC, n % KC
                        if n == 0:
                            pe.wait_ge(sem("qhi_ready"), KC * (gi + 1))
                            pe.wait_ge(sem("qlo_ready"), KC * (gi + 1))
                        else:
                            pe.wait_ge(sem("max_done"), GT * KC * gi + n)
                        for h in range(2):
                            last = T.matmul(ps[:, WF + h, 0:4 * NK], qT[:, par, 0, g, t * P:(t + 1) * P],
                                            KB[:, b, 0, g, h * 4 * NK:(h + 1) * 4 * NK], start=True, stop=True)
                        last.then_inc(sem("max_ps"), 1)
                    return run

                def max_t():
                    pe.wait_ge(sem("max_done"), GT * KC * (gi + 1))
                    dst = ps[0:H, WF, :].bitcast(BF16)
                    for t in range(GT):
                        last = T.transpose(dst[:, t * P:(t + 1) * P], mx[:, t, :], idb)
                    last.then_inc(sem("mxT_ps"), 1)
                return x_hi, x_lo, q0, q1, [max_scores(n) for n in range(GT * KC)], max_t

            def out_jobs(l, i):
                gi = i + NG * l

                def c_hi():
                    pe.wait_ge(sem("chi_ready"), gi + 1)
                    transposes(WT, cs[0]).then_inc(sem("cT_ps"), 1)

                def c_lo():
                    pe.wait_ge(sem("clo_ready"), gi + 1)
                    transposes(WT + 1, cs[1]).then_inc(sem("cT_ps"), 1)

                def project(u):
                    pe.wait_ge(sem("cThi_ready"), gi + 1)
                    pe.wait_ge(sem("cTlo_ready"), gi + 1)
                    for v in range(2):
                        t = 2 * u + v
                        o = ps[:, WT + u, v * D:(v + 1) * D]
                        n = 0
                        for a, w in ((0, 0), (0, 1), (1, 0)):
                            for c in range(KC):
                                last = T.matmul(o, cT[:, a, c, t * P:(t + 1) * P], WO[:, w, c, :],
                                                start=n == 0, stop=n == 5)
                                n += 1
                    last.then_inc(sem("o_ps"), 1)
                return c_hi, c_lo, lambda: project(0), lambda: project(1)

            PARTS = ((0, 0), (0, 1), (1, 0))

            def scores(l, i, b, par, n):
                N = NSLOT * (i + NG * l) + n
                g, c = n // NC5, n % NC5
                rows = ROWS[c]
                if n == 0:
                    pe.wait_ge(sem("mxT_ready"), i + NG * l + 1)
                pe.wait_ge(sem("p_ready"), N + 1)
                o = ps[0:rows, S0 + n % 2, :]
                cols = slice(c * P, c * P + rows)
                T.matmul(o, KB[:, b, 0, g, cols], qT[:, par, 0, g, :], start=True, stop=False)
                T.matmul(o, KB[:, b, 1, g, cols], qT[:, par, 0, g, :], start=False, stop=False)
                T.matmul(o, KB[:, b, 0, g, cols], qT[:, par, 1, g, :], start=False, stop=False)
                T.matmul(o, indb[:, g, cols], mxT[:, par, :], start=False, stop=True).then_inc(sem("s_ps"), 1)

            def values(l, i, b, par, n):
                gi = i + NG * l
                N = NSLOT * gi + n
                g, c = n // NC5, n % NC5
                if c == 0:
                    pe.wait_ge(sem("pv_free"), 4 * gi + 2 * g + 2)
                pe.wait_ge(sem(("plo_even", "plo_odd")[n % 2]), NSLOT // 2 * gi + n // 2 + 2)
                rows, h0 = ROWS[c], HEAD0[c]
                for t in range(GT):
                    o = ps[:, PV0 + t // 2, (t % 2) * HG * VW + h0 * VW:(t % 2) * HG * VW + (h0 + 3) * VW]
                    for m, (a, w) in enumerate(PARTS):
                        last = T.matmul(o, PP[0:rows, (NSLOT * par + n) % NPB, a, t * P:(t + 1) * P], V[0:rows, b, n, w * 3 * VW:(w + 1) * 3 * VW],
                                        start=c == 0 and t % 2 == 0 and m == 0, stop=c == NC5 - 1 and m == 2,
                                        skip_group_check=True)
                last.then_inc(sem("pv_ps"), 1)

            def half(l, i, b, par, before, after, nxt):
                for n in range(NSLOT):
                    if n + 2 < NSLOT:
                        scores(l, i, b, par, n + 2)
                    for job in before.get(n, ()):
                        job()
                    values(l, i, b, par, n)
                    for job in after.get(n, ()):
                        job()
                    if n + 2 >= NSLOT and nxt is not None:
                        scores(l, i + 1, nxt, 1 - par, n + 2 - NSLOT)

            def slots(front, back):
                before, after = {}, {}
                if front:
                    xh, xl, q0, q1, mxs, mt = front
                    before = {0: [xh, xl], 1: [q0, q1], 2: [mxs[0]], 3: [mxs[1]], 4: [mxs[3]], 5: [mxs[5]],
                              6: [mxs[6]], 7: [mxs[7]], 8: [mt]}
                    after = {3: [mxs[2]], 4: [mxs[4]]}
                if back:
                    for n, job in ((5, back[0]), (5, back[1]), (6, back[2]), (7, back[3])):
                        after.setdefault(n, []).append(job)
                return before, after

            def batch(l, b, first=False, last=False):
                half(l, 2 * b, b, 0, *slots(query_jobs(l, 2 * b + 1, b, 1), None if first else out_jobs(l, 2 * b - 1)), b)
                front = None if last else query_jobs(l, 2 * b + 2, b + 1, 0)
                half(l, 2 * b + 1, b, 1, *slots(front, out_jobs(l, 2 * b)), None if last else b + 1)

            def attention(l):
                prep(l)
                pe.wait_ge(sem("kb_ready"), 2 * (l + 1))
                pe.wait_ge(sem("wsplit"), 2 * (l + 1))
                xh, xl, q0, q1, mxs, mt = query_jobs(l, 0, 0, 0)
                for job in (xh, xl, q0, q1, *mxs, mt):
                    job()
                pe.wait_ge(sem("v_ready"), KC * B * (l + 1))
                scores(l, 0, 0, 0, 0)
                scores(l, 0, 0, 0, 1)
                batch(l, 0, first=True)
                with pe.Fori(1, B - 1) as b:
                    batch(l, pe.snap(b))
                batch(l, B - 1, last=True)
                for job in out_jobs(l, NG - 1):
                    job()
            HB, TQ, YB = (2, 4), 6, (7, 0)

            def ffn():
                pe.wait_ge(sem("w_sums"), 1)
                T.matmul(ps[:, 7, 0:2], onef, wsm[:, 0:2], start=True, stop=True).then_inc(sem("w_tot"), 1)
                pe.wait_ge(sem("wq_ready"), 1)

                def xq_t(b, v):
                    if v == 0:
                        pe.wait_ge(sem("z_ready"), b + 1)
                    else:
                        pe.wait_ge(sem("xqT_ready"), 2 * b + 1)
                    dst = ps[:, 1, :].bitcast(F16).rearrange("p (c n) -> p c n", c=KC)
                    for c in range(KC):
                        for t in range(GT):
                            last = T.transpose(dst[:, c, t * P:(t + 1) * P], low_halves(y8[:, GT * v + t, c * P:(c + 1) * P]), idf)
                    last.then_inc(sem("xqT_ps"), 1)

                def hidden(b, t):
                    if t % GT == 0:
                        pe.wait_ge(sem("xqT_ready"), 2 * b + t // GT + 1)
                    pe.wait_ge(sem("hpre_ready"), TB * b + t + 1)
                    for h in range(2):
                        for c in range(KC):
                            last = T.matmul(ps[:, HB[t % 2] + h, :], xqT[:, c, t * P:(t + 1) * P],
                                            w1q[:, c, h * 512:(h + 1) * 512], start=c == 0, stop=c == KC - 1)
                    last.then_inc(sem("h_ps"), 1)

                def hidden_t(k, t):
                    pe.wait_ge(sem("zz_ready"), k + 1)
                    pe.wait_ge(sem("hqT_ready"), k + 1)
                    dst = ps[:, TQ, :].bitcast(F16)
                    for c in range(MC):
                        last = T.transpose(dst[:, c * P:(c + 1) * P], low_halves(gl[:, t % 4, c * P:(c + 1) * P]), idf)
                    last.then_inc(sem("hqT_ps"), 1)

                def project(k, t):
                    pe.wait_ge(sem("hqT_ready"), k + 2)
                    after(pe, "ffn_out", k - 1)
                    for c in range(MC):
                        last = T.matmul(ps[:, YB[t % 2], 0:D], hqT[:, t % 2, c, :], w2q[:, c, :], start=c == 0, stop=c == MC - 1)
                    last.then_inc(sem("y_ps"), 1)

                def batch(b, first=False, last=False):
                    for t in range(TB):
                        k = TB * b + t
                        hidden(b, t)
                        if not last and t == TB - 1:
                            xq_t(b + 1, 0)
                            xq_t(b + 1, 1)
                        if not first or t >= 2:
                            hidden_t(k - 2, (t - 2) % TB)
                        if not first or t >= 3:
                            project(k - 3, (t - 3) % TB)
                xq_t(0, 0)
                xq_t(0, 1)
                batch(0, first=True)
                with pe.Fori(1, B - 1) as b:
                    batch(pe.snap(b))
                batch(B - 1, last=True)
                hidden_t(NT - 2, TB - 2)
                project(NT - 3, TB - 3)
                hidden_t(NT - 1, TB - 1)
                project(NT - 2, TB - 2)
                project(NT - 1, TB - 1)

            RT, LGB, RK = (6, 7), 5, 4

            def router():
                pe.wait_ge(sem("wr_split"), 1)

                def group(g, par):
                    pe.wait_ge(sem("rlo_ready"), g + 1)
                    for a in range(2):
                        dst = ps[:, RT[a], :].bitcast(F16).rearrange("p (c n) -> p c n", c=KC)
                        for c in range(KC):
                            for t in range(GT):
                                last = T.transpose(dst[:, c, t * P:(t + 1) * P], xr[:, par, t, a * D + c * P:a * D + (c + 1) * P], idf)
                        last.then_inc(sem("rT_ps"), 1)
                    pe.wait_ge(sem("rT_ready"), 2 * (g + 1))
                    pe.wait_ge(sem("lg_ready"), g + 1)
                    for t in range(GT):
                        n = 0
                        for a, w in ((0, 0), (0, 1), (1, 0)):
                            for c in range(KC):
                                last = T.matmul(ps[:, LGB, t * E:(t + 1) * E], xrT[:, a, c, t * P:(t + 1) * P], wrs[:, w, c, :],
                                                start=n == 0, stop=n == 5)
                                n += 1
                    last.then_inc(sem("lg_ps"), 1)
                with pe.Fori(0, NG // 2) as r:
                    r = pe.snap(r)
                    for u in range(2):
                        group(2 * r + u, u)

            def dispatch():
                pe.wait_ge(sem("m_ready"), 1)
                T.matmul(ps[:, RK, 0:NT * E], upper, Mb.rearrange("p t e -> p (t e)"), start=True, stop=False, skip_group_check=True)
                for t in range(NT):
                    last = T.matmul(ps[:, RK, (t + 1) * E:(NT + 1) * E].rearrange("p (t e) -> p t e", e=E), onesb,
                                    Mb[:, t, :].unsqueeze(1).to_broadcast([P, NT - t, E]), start=False, stop=t == NT - 1, skip_group_check=True)
                last.then_inc(sem("rank_ps"), 1)
                for n in range(NPC):
                    pe.wait_ge(sem("onehot_ready"), n + 1)
                    for i in range(PC):
                        last = T.matmul(ps[:, 6, 0:NSC], ohL[n % 2][:, i, :], ohH[n % 2][:, i, :],
                                        start=n == 0 and i == 0, stop=n == NPC - 1 and i == PC - 1)
                    last.then_inc(sem("onehot_used"), 1)

            XTB, H1, YB2 = 0, 1, (5, 6)

            def experts():
                pe.wait_ge(sem("ex_ready"), 1)
                pe.wait_ge(sem("wlo_done"), 4 * E + 4)

                def expert_of(j):
                    return pe.value_load(exi[0:1, j:j + 1] if isinstance(j, int) else exi[0:1, bass.ds(j, 1)], min_val=0, max_val=E - 1)

                def rows_t(j, par, jh):
                    pe.wait_ge(sem(("gathered_even", "gathered_odd")[par]), 32 * (jh + 1))
                    pe.wait_ge(sem("xsT_ready"), j + 1)
                    dst = ps[:, XTB, :].bitcast(F16).rearrange("p (w c n) -> p w c n", w=2, c=KC)
                    for w in range(2):
                        for c in range(KC):
                            for s_ in range(2):
                                last = T.transpose(dst[:, w, c, s_ * P:(s_ + 1) * P], xg_[:, par, s_, w * D + c * P:w * D + (c + 1) * P], idf)
                    last.then_inc(sem("xsT_ps"), 1)

                def hidden(j, par):
                    e = expert_of(j)
                    pe.wait_ge(sem("xsT_ready"), j + 2)
                    for q in range(4):
                        pe.wait_ge(sem("gelu_done"), 4 * j + q + 1)
                        for m in (2 * q, 2 * q + 1):
                            n = 0
                            for a, w in ((0, 0), (1, 0), (0, 1)):
                                for c in range(KC):
                                    lw = WE[:, bass.ds(e, 1), a * 2 * M + c * M + m * P:a * 2 * M + c * M + (m + 1) * P].rearrange("p a n -> p (a n)")
                                    last = T.matmul(ps[:, H1 + q, (m % 2) * ST:(m % 2 + 1) * ST], lw, xsT[:, par, w, c, :],
                                                    start=n == 0, stop=n == 5)
                                    n += 1
                        last.then_inc(sem("eh_ps"), 1)

                def project(j, par):
                    e = expert_of(j)
                    for s_ in range(2):
                        pe.wait_ge(sem("ey_done"), 2 * j + s_ + 1)
                        n = 0
                        for m in range(MC):
                            if s_ == 0 and m % 2 == 0:
                                pe.wait_ge(sem("hlo_ready"), 4 * j + m // 2 + 5)
                            for a, w in ((0, 0), (0, 1), (1, 0)):
                                rw = WE[:, bass.ds(e, 1), 4 * M + a * 2 * M + m * D:4 * M + a * 2 * M + (m + 1) * D].rearrange("p a n -> p (a n)")
                                last = T.matmul(ps[:, YB2[s_], 0:D], hid[:, par, w, m * ST + s_ * P:m * ST + (s_ + 1) * P], rw,
                                                start=n == 0, stop=n == 3 * MC - 1)
                                n += 1
                        last.then_inc(sem("ey_ps"), 1)
                rows_t(0, 0, 0)
                hidden(0, 0)
                rows_t(1, 1, 0)
                with pe.Fori(0, (NST - 1) // 2) as r:
                    r = pe.snap(r)
                    for u in range(2):
                        hidden(2 * r + u + 1, 1 - u)
                        rows_t(2 * r + u + 2, u, r + 1)
                        project(2 * r + u, u)
                project(NST - 1, (NST - 1) % 2)
            pe.wait_ge(sem("c_in"), 96)
            attention(0)
            ffn()
            attention(1)
            router()
            dispatch()
            experts()

        @block.scalar
        def _(act):
            A = nc.scalar

            def prep(l):
                act.wait_ge(sem("prep_in"), 16 * PREP_DMAS * (l + 1))
                for w, dst in ((0, WQ), (3, WO)):
                    A.mul(dst[:, 0, :, :], wraw[:, w, :, :], WS).then_inc(sem("whi_ready"), 1)
                for m in range(KC):
                    act.wait_ge(sem("kt_ps"), KC * l + m + 1)
                    A.activation(KT[:, 0, m, :], ps[:, m, 0:B * NK], ACT.Identity, bias=bcol[:, 2 + m:3 + m]).then_inc(sem("khi_ready"), 1)

                for b in range(B):
                    act.wait_ge(sem("v_ps"), B * l + b + 1)
                    A.copy(vs[0:NK, b, 0, :], ps[0:NK, 4 + b, 0:D]).then_inc(sem("vhi_ready"), 1)

            def half(l, i, par, front, back):
                gi = i + NG * l
                qp = 1 - par

                def exp(n):
                    N = NSLOT * gi + n
                    rows = ROWS[n % NC5]
                    act.wait_ge(sem("s_ps"), N + 1)
                    act.wait_ge(sem("pv_ps"), N + 1)
                    src = ps[0:rows, S0 + n % 2, :]
                    A.activation(PP[0:rows, (NSLOT * par + n) % NPB, 0, :], src, ACT.Exp, scale=HD ** -0.5 / WS)
                    act.wait_ge(sem(("plo_even", "plo_odd")[n % 2]), NSLOT // 2 * gi + n // 2 + 1)
                    A.activation(PT[0:rows, n % 2, :], src, ACT.Exp, scale=HD ** -0.5 / WS).then_inc(sem("p_ready"), 1)
                for n in range(NSLOT):
                    exp(n)
                    if front and n == 1:
                        x_hi(gi + 1)
                    if front and n == 2:
                        q_hi(gi + 1, qp, 0)
                        q_hi(gi + 1, qp, 1)
                    if back and n == 6:
                        c_hi(gi - 1)
                    if front and n == 8:
                        m_t(gi + 1, qp)

            def x_hi(gi):
                act.wait_ge(sem("xT_ps"), 2 * gi + 1)
                A.copy(xT[:, 0, :, :], ps[:, WF, :].bitcast(F16).rearrange("p (c n) -> p c n", c=KC)).then_inc(sem("xThi_ready"), 1)

            def q_hi(gi, par, m):
                act.wait_ge(sem("q_ps"), KC * gi + m + 1)
                A.activation(qT[:, par, 0, m, :], ps[:, WF + m, :], ACT.Identity, bias=bcol[:, m:m + 1]).then_inc(sem("qhi_ready"), 1)

            def m_t(gi, par):
                act.wait_ge(sem("mxT_ps"), gi + 1)
                A.copy(mxT[:, par, :], ps[0:H, WF, :].bitcast(BF16)[:, 0:GN]).then_inc(sem("mxT_ready"), 1)

            def c_hi(gi):
                act.wait_ge(sem("cT_ps"), 2 * gi + 1)
                A.copy(cT[:, 0, :, :], ps[:, WT, :].bitcast(F16).rearrange("p (c n) -> p c n", c=KC)).then_inc(sem("cThi_ready"), 1)

            def batch(l, b, first=False, last=False):
                half(l, 2 * b, 0, True, not first)
                half(l, 2 * b + 1, 1, not last, True)

            def attention(l):
                prep(l)
                act.wait_ge(sem("bq_ready"), l + 1)
                g0 = NG * l
                x_hi(g0)
                q_hi(g0, 0, 0)
                q_hi(g0, 0, 1)
                m_t(g0, 0)
                batch(l, 0, first=True)
                with act.Fori(1, B - 1) as b:
                    batch(l, act.snap(b))
                batch(l, B - 1, last=True)
                c_hi(NG * (l + 1) - 1)
            def ffn():
                def xq_copy(b, v):
                    act.wait_ge(sem("xqT_ps"), 2 * b + v + 1)
                    A.activation(xqT[:, :, v * GN:(v + 1) * GN], ps[:, 1, :].bitcast(F16).rearrange("p (c n) -> p c n", c=KC), ACT.Copy,
                                 bias=-HALF).then_inc(sem("xqT_ready"), 1)

                def gelu(k, t):
                    act.wait_ge(sem("hpre_ready"), k + 3)
                    after(act, "hqT_ps", k - 3)
                    A.activation(gl[:, t % 4, :], hpre[:, t % 2, :], ACT.Gelu).then_inc(sem("gl_ready"), 1)
                    act.wait_ge(sem("gl_ready"), k + 1)
                    A.activation(fsq, gl[:, t % 4, :], ACT.Square, scale=M ** -0.5,
                                 accum_out=MS[:, t % 4:t % 4 + 1]).then_inc(sem("ms_ready"), 1)

                def multiple(k, t):
                    act.wait_ge(sem("s2_ready"), k + 1)
                    g = gl[:, t % 4, :]
                    A.activation(g, g, ACT.Copy, bias=MAGIC_H, scale=S2[:, t % 4:t % 4 + 1]).then_inc(sem("zz_ready"), 1)

                def batch(b, first=False, last=False):
                    for t in range(TB):
                        k = TB * b + t
                        gelu(k, t)
                        if not last and t == TB - 1:
                            xq_copy(b + 1, 0)
                            xq_copy(b + 1, 1)
                        if not first or t >= 1:
                            multiple(k - 1, (t - 1) % TB)
                xq_copy(0, 0)
                xq_copy(0, 1)
                batch(0, first=True)
                with act.Fori(1, B - 1) as b:
                    batch(act.snap(b))
                batch(B - 1, last=True)
                multiple(NT - 1, TB - 1)

            def split_weights():
                def src(e, ch):
                    w = (ew1, ew2)[ch // 2][e, :, :] if isinstance(e, int) else (ew1, ew2)[ch // 2][bass.ds(e, 1), :, :].rearrange("a k n -> (a k) n")
                    return w[ch * P:(ch + 1) * P, :] if ch < 2 else w[(ch - 2) * 4 * P:(ch - 1) * 4 * P, :].rearrange("(c p) n -> p c n", p=P)

                def load(e, ch):
                    dst = wstg[:, ch, :] if ch < 2 else wstg[:, ch, :].rearrange("p (c n) -> p c n", c=4)
                    act.wait_ge(sem("wlo_done"), 4 * e + ch + 1)
                    act.dma_start(dst, src(e, ch)).then_inc(sem(f"w_in{ch}"), 16)

                def split(e, ch):
                    act.wait_ge(sem(f"w_in{ch}"), 16 * (e + 1))
                    A.mul(wstg[:, ch, :], wstg[:, ch, :], WS).then_inc(sem("w_scaled"), 1)
                    act.wait_ge(sem("w_scaled"), 4 * e + ch + 1)
                    c0 = (ch // 2) * 4 * M + (ch % 2) * M
                    A.copy(WE[:, e, c0:c0 + M] if isinstance(e, int) else WE[:, bass.ds(e, 1), c0:c0 + M].rearrange("p a n -> p (a n)"),
                           wstg[:, ch, :]).then_inc(sem("whi_done"), 1)
                act.wait_ge(sem("att_out"), 4 * NG)
                load(0, 0)
                load(0, 1)
                with act.Fori(0, E - 1) as e:
                    e = act.snap(e)
                    for ch in range(4):
                        load(e + (ch + 2) // 4, (ch + 2) % 4)
                        split(e, ch)
                for ch in range(4):
                    if ch < 2:
                        load(E - 1, ch + 2)
                    split(E - 1, ch)
                act.wait_ge(sem("tops_ready"), 1)
                A.activation(wts[:, 0, :], wts[:, 0, :], ACT.Exp).then_inc(sem("exp_ready"), 1)

            def experts():
                act.wait_ge(sem("ex_ready"), 1)

                def gelu(j):
                    e = act.value_load(exi[0:1, j:j + 1] if isinstance(j, int) else exi[0:1, bass.ds(j, 1)], min_val=0, max_val=E - 1)
                    for q in range(4):
                        act.wait_ge(sem("eh_ps"), 4 * j + q + 1)
                        act.wait_ge(sem("hlo_ready"), 4 * j + q + 1)
                        for v in range(2):
                            last = A.activation(gel[:, q, v * ST:(v + 1) * ST], ps[:, 1 + q, v * ST:(v + 1) * ST], ACT.Gelu,
                                                bias=b1t[:, bass.ds(e * MC + 2 * q + v, 1)], scale=1.0 / WS)
                        last.then_inc(sem("gelu_done"), 1)
                gelu(0)
                with act.Fori(0, (NST - 1) // 2) as r:
                    r = act.snap(r)
                    for u in range(2):
                        gelu(2 * r + u + 1)
            act.sem_inc(sem("gelu_done"), 4)
            act.sem_inc(sem("p_ready"), 2)
            act.wait_ge(sem("c_in"), 96)
            A.activation(gsc[:, 2:4], gsr[:, 2:4], ACT.Tanh).then_inc(sem("tanh"), 1)
            A.activation(gsc[:, 4:6], gsr[:, 0:2], ACT.Tanh).then_inc(sem("tanh"), 1)
            attention(0)
            ffn()
            attention(1)
            split_weights()
            experts()

        @block.vector
        def _(dve):
            V_ = nc.vector
            base = [0, 0]

            def link(ins, wait=after):
                base[1] += 1
                ins.then_inc(sem("dve_link"), 1)
                wait(dve, "dve_link", base[0] + base[1])

            def loop(lo, hi, links, body):
                start = base[0] + base[1]
                with dve.Fori(lo, hi) as r:
                    r = dve.snap(r)
                    base[0], base[1] = r * links + (start - lo * links), 0
                    body(r)
                    assert base[1] == links, base[1]
                base[0], base[1] = start + (hi - lo) * links, 0

            def prep(l):
                dve.wait_ge(sem("prep_in"), 16 * PREP_DMAS * (l + 1))
                V_.memset(one1, 1.0).then_inc(sem("one_set"), 1)
                link(V_.tensor_scalar(bcol[:, 0:KC], bcol[:, 0:KC], WS, None, ALU.mult))
                V_.tensor_scalar(gbo, bosr, gsc[:, GX[l]:GX[l] + 1], None, ALU.mult).then_inc(sem("bq_ready"), 1)
                for n, (w, dst) in enumerate(((0, WQ), (3, WO))):
                    dve.wait_ge(sem("whi_ready"), 2 * l + n + 1)
                    V_.scalar_tensor_tensor(dst[:, 1, :, :], wraw[:, w, :, :], WS, dst[:, 0, :, :],
                                            ALU.mult, ALU.subtract).then_inc(sem("wsplit"), 1)
                for m in range(KC):
                    dve.wait_ge(sem("khi_ready"), KC * l + m + 1)
                    ins = V_.scalar_tensor_tensor(KT[:, 1, m, :], ps[:, m, 0:B * NK], bcol[:, 2 + m:3 + m],
                                                  KT[:, 0, m, :], ALU.add, ALU.subtract)
                    ins.then_inc(sem("klo_ready"), 1)
                for b in range(B):
                    dve.wait_ge(sem("vhi_ready"), B * l + b + 1)
                    V_.tensor_tensor(vs[0:NK, b, 1, :], ps[0:NK, 4 + b, 0:D], vs[0:NK, b, 0, :], ALU.subtract).then_inc(sem("vlo_ready"), 1)
                for b in range(B):
                    for g in range(KC):
                        last = V_.tensor_tensor(KB[:, b, 0, g, :].rearrange("p (h k) -> p h k", k=NK),
                                                KT[:, 0, g, b * NK:(b + 1) * NK].unsqueeze(1).to_broadcast([P, HG, NK]),
                                                maskk.unsqueeze(2).to_broadcast([P, HG, NK]), ALU.mult)
                last.then_inc(sem("kb_ready"), 1)
                for b in range(B):
                    for g in range(KC):
                        dve.wait_ge(sem("vsel_ps"), KC * (B * l + b) + g + 1)
                        n4 = NC5 - 1
                        for r, c0, nc_ in ((P, 0, n4), (ROWS[n4], n4, 1)):
                            dst = V[0:r, b, g * NC5 + c0:g * NC5 + c0 + nc_, :].rearrange("p c (j v) -> p (c j) v", v=VW)
                            V_.tensor_tensor(dst[:, :, 0:HD],
                                             ps[0:r, 2 * (b % 2) + g, c0 * 96:(c0 + nc_) * 96].rearrange("p (j v) -> p j v", v=HD),
                                             maskv[0:r, 6 * c0:6 * (c0 + nc_)].unsqueeze(2).to_broadcast([r, 6 * nc_, HD]), ALU.mult)
                            last = V_.tensor_copy(dst[:, :, HD], maskone[0:r, 6 * c0:6 * (c0 + nc_)])
                        last.then_inc(sem("v_ready"), 1)

            def norm_stats(gi, i):
                for t in range(GT):
                    ins = V_.bn_stats(stats[:, t, :], X[:, t + GT * i, :] if isinstance(i, int) else X[:, bass.ds(i * GT + t, 1), :])
                link(ins, hold)
                for t in range(GT):
                    ins = V_.bn_aggr(mv[:, t, :], stats[:, t, :])
                ins.then_inc(sem("var_ready"), 1)

            def norm(gi, i):
                dve.wait_ge(sem("rstd_ready"), gi + 1)
                for t in range(GT):
                    xt = X[:, t + GT * i, :] if isinstance(i, int) else X[:, bass.ds(i * GT + t, 1), :]
                    ins = V_.tensor_scalar(xn[:, t, :], xt, mv[:, t, 0:1], rstd[:, t:t + 1], ALU.subtract, ALU.mult)
                link(ins)
                V_.tensor_copy(xs[0], xn.rearrange("p t d -> p (t d)")).then_inc(sem("xhi_ready"), 1)

            def x_lo(gi):
                dve.wait_ge(sem("xT_ps"), 2 * gi + 2)
                V_.tensor_copy(xT[:, 1, :, :], ps[:, WF + 1, :].bitcast(F16).rearrange("p (c n) -> p c n", c=KC)).then_inc(sem("xTlo_ready"), 1)

            def q_lo(gi, par, m):
                dve.wait_ge(sem("qhi_ready"), KC * gi + m + 1)
                V_.scalar_tensor_tensor(qT[:, par, 1, m, :], ps[:, WF + m, :], bcol[:, m:m + 1], qT[:, par, 0, m, :],
                                        ALU.add, ALU.subtract).then_inc(sem("qlo_ready"), 1)

            def maxima(gi, n):
                t, g = n // KC, n % KC
                dve.wait_ge(sem("max_ps"), GT * KC * gi + n + 1)
                V_.tensor_reduce(mx[:, t, g * HG:(g + 1) * HG],
                                 ps[:, WF:WF + 2, 0:4 * NK].rearrange("p a (h k) -> p a h k", k=NK),
                                 AX.X, ALU.max, negate=True).then_inc(sem("max_done"), 1)

            def attend(gi, g):
                dve.wait_ge(sem("pv_ps"), NPB + NSLOT * gi + NC5 * (g + 1))
                pv = [ps[:, PV0 + u, 0:2 * HG * VW].rearrange("p (t h v) -> p t h v", t=2, v=VW) for u in range(2)]
                dve.wait_ge(sem("pv_free"), 2 + 4 * gi + 2 * g)
                for u in range(2):
                    ins = V_.reciprocal(rec[:, u], pv[u][:, :, :, HD])
                link(ins)
                for u in range(2):
                    dst = cx[:, 2 * u:2 * u + 2, g * P:(g + 1) * P].rearrange("p t (h v) -> p t h v", v=HD)
                    for t in range(2):
                        ins = V_.tensor_tensor(dst[:, t], pv[u][:, t, :, 0:HD],
                                               rec[:, u, t, :].unsqueeze(2).to_broadcast([P, HG, HD]), ALU.mult)
                    ins.then_inc(sem("pv_free"), 1)

            def ctx_hi(gi):
                dve.wait_ge(sem("pv_free"), 4 * gi + 4 + 2)
                V_.tensor_copy(cs[0], cx.rearrange("p t d -> p (t d)")).then_inc(sem("chi_ready"), 1)

            def ctx_lo(gi):
                dve.wait_ge(sem("cT_ps"), 2 * gi + 2)
                V_.tensor_copy(cT[:, 1, :, :], ps[:, WT + 1, :].bitcast(F16).rearrange("p (c n) -> p c n", c=KC)).then_inc(sem("cTlo_ready"), 1)

            def add_out(l, gi, i, u):
                dve.wait_ge(sem("o_ps"), 2 * gi + u + 1)
                dve.wait_ge(sem("xb_ready"), gi + 1)
                xt = X[:, bass.ds(i * GT + 2 * u, 2), :]
                V_.scalar_tensor_tensor(xt, ps[:, WT + u, :].rearrange("p (t d) -> p t d", t=2), gsc[:, GA[l]:GA[l] + 1], xt,
                                        ALU.mult, ALU.add).then_inc(sem("att_out"), 1)

            def p_lo(gi, par, n):
                rows = ROWS[n % NC5]
                dve.wait_ge(sem("p_ready"), NSLOT * gi + n + 3)
                buf = (NSLOT * par + n) % NPB
                V_.tensor_tensor(PP[0:rows, buf, 1, :], PT[0:rows, n % 2, :], PP[0:rows, buf, 0, :],
                                 ALU.subtract).then_inc(sem("plo_even"), 1)

            def half(l, i, par, front, stats_next, back):
                gi = i + NG * l
                for n in range(NSLOT):
                    if n % 2 == 0:
                        p_lo(gi, par, n)
                    if front and n == 0:
                        x_lo(gi + 1)
                    if front and n == 1:
                        q_lo(gi + 1, 1 - par, 0)
                        q_lo(gi + 1, 1 - par, 1)
                    if front and 2 <= n <= 7:
                        for m in ((0,), (1, 2), (3, 4), (5,), (6,), (7,))[n - 2]:
                            maxima(gi + 1, m)
                    if stats_next and n == 2:
                        norm_stats(gi + 2, i + 2)
                    if n == 4:
                        if back:
                            dve.wait_ge(sem("clo_ready"), gi)
                        attend(gi, 0)
                    if back and n == 6:
                        ctx_lo(gi - 1)
                    if back and n == 8:
                        add_out(l, gi - 1, i - 1, 0)
                        add_out(l, gi - 1, i - 1, 1)
                    if stats_next and n == 5:
                        norm(gi + 2, i + 2)
                attend(gi, 1)
                ctx_hi(gi)

            def batch(l, b, first=False, last=False):
                half(l, 2 * b, 0, True, not last, not first)
                half(l, 2 * b + 1, 1, not last, not last, True)

            def attention(l):
                prep(l)
                norm_stats(NG * l, 0)
                norm(NG * l, 0)
                x_lo(NG * l)
                q_lo(NG * l, 0, 0)
                q_lo(NG * l, 0, 1)
                for n in range(KC * GT):
                    maxima(NG * l, n)
                norm_stats(NG * l + 1, 1)
                norm(NG * l + 1, 1)
                if l == 0:
                    dve.wait_ge(sem("x_in2"), 48)
                batch(l, 0, first=True)
                loop(1, B - 1, 8, lambda b: batch(l, b))
                batch(l, B - 1, last=True)
                gi = NG * (l + 1) - 1
                ctx_lo(gi)
                add_out(l, gi, NG - 1, 0)
                add_out(l, gi, NG - 1, 1)

            def ffn():
                dve.wait_ge(sem("att_out"), 2 * NG)
                V_.memset(onef, 1.0)
                dve.wait_ge(sem("fw_in"), 64)
                for w in range(2):
                    ins = V_.tensor_reduce(wsm[:, w:w + 1], fraw[:, w, :], AX.X, ALU.add, apply_absolute_value=True)
                ins.then_inc(sem("w_sums"), 1)
                dve.wait_ge(sem("w_tot"), 1)
                link(V_.tensor_scalar(wsm[:, 2:4], ps[:, 7, 0:2], 1.0 / (D * M), Q_EPS, ALU.mult, ALU.max))
                link(V_.reciprocal(wsm[:, 4:6], wsm[:, 2:4]))
                for w in range(2):
                    ins = V_.tensor_scalar(fraw[:, w, :], fraw[:, w, :], wsm[:, 4 + w:5 + w], MAGIC, ALU.mult, ALU.add)
                link(ins)
                for w in range(2):
                    ins = V_.tensor_scalar(fraw[:, w, :], fraw[:, w, :], MAGIC + 1, MAGIC - 1, ALU.min, ALU.max)
                link(ins)
                V_.tensor_scalar(w1q.rearrange("p c n -> p (c n)"), fraw[:, 0, :], MAGIC, None, ALU.subtract)
                V_.tensor_scalar(w2q.rearrange("p c n -> p (c n)"), fraw[:, 1, :], MAGIC, None, ALU.subtract).then_inc(sem("wq_ready"), 1)
                link(V_.tensor_scalar(wsm[:, 2:4], wsm[:, 2:4], 1.0 / 127, None, ALU.mult))
                link(V_.tensor_scalar(wsm[:, 3:4], wsm[:, 3:4], gsc[:, 2:3], None, ALU.mult))
                V_.tensor_scalar(fb2c, fb2c, gsc[:, 2:3], None, ALU.mult).then_inc(sem("fb2_ready"), 1)

                def rows(b, t):
                    return X[:, b * TB + t, :] if isinstance(b, int) else X[:, bass.ds(b * TB + t, 1), :]

                def front(b, part):
                    if part == 0:
                        for t in range(TB):
                            ins = V_.bn_stats(fst[:, t, :], rows(b, t))
                        link(ins, hold)
                        for t in range(TB):
                            ins = V_.bn_aggr(fmv[:, t, :], fst[:, t, :])
                        ins.then_inc(sem("fvar_ready"), 1)
                    elif part == 1:
                        dve.wait_ge(sem("frs_ready"), b + 1)
                        after(dve, "xqT_ps", 2 * b)
                        for t in range(TB):
                            ins = V_.tensor_scalar(y8[:, t, :], rows(b, t), fmv[:, t, 0:1], RS_[:, t:t + 1], ALU.subtract, ALU.mult)
                        link(ins)
                    elif part == 2:
                        link(V_.tensor_reduce(AM, y8, AX.X, ALU.max, apply_absolute_value=True))
                        link(V_.tensor_tensor(AM, AM, R2, ALU.mult))
                        link(V_.tensor_scalar(AM, AM, Q_EPS, None, ALU.max))
                        V_.tensor_scalar(DN, AM, wsm[:, 2:3], None, ALU.mult)
                        link(V_.reciprocal(INV, AM))
                        link(V_.scalar_tensor_tensor(SC, INV, 127.0, R2, ALU.mult, ALU.mult))
                    else:
                        for t in range(TB):
                            ins = V_.tensor_scalar(y8[:, t, :], y8[:, t, :], SC[:, t:t + 1], MAGIC_H, ALU.mult, ALU.add)
                        ins.then_inc(sem("z_ready"), 1)
                FRONT_LINKS = 7

                def pre(k, b, t):
                    dve.wait_ge(sem("h_ps"), k + 1)
                    after(dve, "gl_ready", k - 1)
                    h = HBD[t % 2]
                    V_.scalar_tensor_tensor(hpre[:, t % 2, :].rearrange("p (a n) -> p a n", a=2), ps[:, h:h + 2, :], D1[:, t:t + 1],
                                            fb1c.rearrange("p (a n) -> p a n", a=2), ALU.mult, ALU.add).then_inc(sem("hpre_ready"), 1)

                def small(k, t):
                    c = slice(t % 4, t % 4 + 1)
                    dve.wait_ge(sem("gl_ready"), k + 1)
                    link(V_.tensor_reduce(A2[:, c], gl[:, t % 4, :], AX.X, ALU.max, apply_absolute_value=True))
                    dve.wait_ge(sem("rr_ready"), k + 1)
                    link(V_.tensor_scalar(A2[:, c], A2[:, c], RR[:, c], Q_EPS, ALU.mult, ALU.max))
                    V_.tensor_scalar(D2[:, c], A2[:, c], wsm[:, 3:4], None, ALU.mult)
                    link(V_.reciprocal(IV2[:, c], A2[:, c]))
                    V_.tensor_scalar(S2[:, c], IV2[:, c], 127.0, RR[:, c], ALU.mult, ALU.mult).then_inc(sem("s2_ready"), 1)

                def hqt_copy(k, t):
                    dve.wait_ge(sem("hqT_ps"), k + 1)
                    V_.tensor_scalar(hqT[:, t % 2, :, :], ps[:, 6, :].bitcast(F16).rearrange("p (c n) -> p c n", c=MC), HALF, None,
                                     ALU.subtract).then_inc(sem("hqT_ready"), 1)

                def add(k, t, b):
                    dve.wait_ge(sem("xb2_ready"), b + 1)
                    dve.wait_ge(sem("y_ps"), k + 1)
                    xt = X[:, bass.ds(k, 1), :].rearrange("p a d -> p (a d)")
                    V_.scalar_tensor_tensor(xt, ps[:, (7, 0)[t % 2], 0:D], D2[:, t % 4:t % 4 + 1], xt, ALU.mult, ALU.add).then_inc(sem("ffn_out"), 1)
                HBD = (2, 4)

                def batch(b, first=False, last=False):
                    link(V_.tensor_copy(D1, DN))
                    for t in range(TB):
                        k = TB * b + t
                        pre(k, b, t)
                        if not first or t >= 1:
                            small(k - 1, (t - 1) % TB)
                        if not first or t >= 2:
                            hqt_copy(k - 2, (t - 2) % TB)
                        if not first or t >= 3:
                            add(k - 3, (t - 3) % TB, b if t >= 3 else b - 1)
                        if not last and t in (0, 2, 3, 4):
                            front(b + 1, (0, 2, 3, 4).index(t))
                dve.sem_inc(sem("hpre_ready"), 2)
                dve.sem_inc(sem("hqT_ready"), 1)
                for part in range(4):
                    front(0, part)
                batch(0, first=True)
                loop(1, B - 1, 1 + 3 * TB + FRONT_LINKS, lambda b: batch(b))
                batch(B - 1, last=True)
                small(NT - 1, TB - 1)
                hqt_copy(NT - 2, TB - 2)
                add(NT - 3, TB - 3, B - 1)
                hqt_copy(NT - 1, TB - 1)
                add(NT - 2, TB - 2, B - 1)
                add(NT - 1, TB - 1, B - 1)


            def router():
                dve.wait_ge(sem("att_out"), 4 * NG)
                dve.wait_ge(sem("wr_in"), 16)
                link(V_.tensor_scalar(wrr, wrr, WS, None, ALU.mult))
                link(V_.tensor_copy(wrs[:, 0], wrr))
                V_.tensor_tensor(wrs[:, 1], wrr, wrs[:, 0], ALU.subtract).then_inc(sem("wr_split"), 1)

                for t in range(NT):
                    ins = V_.bn_stats(rst[:, t, :], X[:, t, :])
                link(ins)
                for t in range(NT):
                    ins = V_.bn_aggr(rmv[:, t, :], rst[:, t, :])
                ins.then_inc(sem("rvar_ready"), 1)
                dve.wait_ge(sem("rrs_ready"), 1)

                def rows(g, par, r):
                    after(dve, "rlo_ready", g)
                    for t in range(GT):
                        ins = V_.tensor_scalar(rxn[:, t, :], X[:, bass.ds(g * GT + t, 1), :].rearrange("p a d -> p (a d)"),
                                               rmv[:, bass.ds(g * GT + t, 1), 0:1].rearrange("p a d -> p (a d)"), rrs[:, bass.ds(g * GT + t, 1)],
                                               ALU.subtract, ALU.mult)
                    ins.then_inc(sem("rxn_ready"), 1)
                    dve.wait_ge(sem("rxn_ready"), g + 1)
                    dve.wait_ge(sem(("rows_even", "rows_odd")[par]), 16 * (r + 1))
                    V_.tensor_copy(xr[:, par, :, 0:D], rxn).then_inc(sem("rhi_ready"), 1)
                    dve.wait_ge(sem("rhi_ready"), g + 1)
                    V_.tensor_tensor(xr[:, par, :, D:], rxn, xr[:, par, :, 0:D], ALU.subtract).then_inc(sem("rlo_ready"), 1)

                def logits(g):
                    for a in range(2):
                        dve.wait_ge(sem("rT_ps"), 2 * g + a + 1)
                        V_.tensor_copy(xrT[:, a], ps[:, 6 + a, :].bitcast(F16).rearrange("p (c n) -> p c n", c=KC)).then_inc(sem("rT_ready"), 1)
                    dve.wait_ge(sem("lg_ps"), g + 1)
                    V_.tensor_scalar(lg[:, bass.ds(g * GT, GT), :], ps[:, 5, 0:GT * E].rearrange("p (t e) -> p t e", e=E), 1.0 / WS, None,
                                     ALU.mult).then_inc(sem("lg_ready"), 1)
                rows(0, 0, 0)
                with dve.Fori(0, NG // 2 - 1) as r:
                    r = dve.snap(r)
                    rows(2 * r + 1, 1, r)
                    logits(2 * r)
                    rows(2 * r + 2, 0, r + 1)
                    logits(2 * r + 1)
                rows(NG - 1, 1, NG // 2 - 1)
                logits(NG - 2)
                logits(NG - 1)

            def tiles(ap):
                return ap.unsqueeze(1).to_broadcast([P, NT, E])

            def choices(ap):
                return ap.unsqueeze(2).to_broadcast([P, NT, E])

            def whole(ap):
                link(V_.tensor_scalar(ap, ap, MAGIC, None, ALU.add))
                link(V_.tensor_scalar(ap, ap, MAGIC, None, ALU.subtract))

            def dispatch():
                link(V_.tensor_scalar(desc, iota[:, 0:E], -1.0, float(E), ALU.mult, ALU.add))
                dve.wait_ge(sem("lg_ready"), NG + 1)
                for k in range(TOPK):
                    link(V_.tensor_reduce(top[:, k], lg, AX.X, ALU.max))
                    link(V_.tensor_tensor(ta, lg, choices(top[:, k]), ALU.is_equal))
                    link(V_.tensor_tensor(ta, ta, tiles(desc), ALU.mult))
                    link(V_.tensor_reduce(top_s, ta, AX.X, ALU.max))
                    link(V_.tensor_tensor(oh[:, k], ta, choices(top_s), ALU.is_equal))
                    if k == 0:
                        link(V_.scalar_tensor_tensor(lg, oh[:, 0], -1e37, lg, ALU.mult, ALU.add))
                V_.tensor_tensor(Mb, oh[:, 0], oh[:, 1], ALU.add).then_inc(sem("m_ready"), 1)
                V_.tensor_tensor(wts[:, 0], top[:, 1], top[:, 0], ALU.subtract).then_inc(sem("tops_ready"), 1)
                dve.wait_ge(sem("rank_ps"), 1)
                link(V_.tensor_copy(cnt, ps[:, 4, NT * E:(NT + 1) * E]))
                link(V_.tensor_scalar(nb, cnt, 1.0 / ST, 0.5 - 0.5 / ST, ALU.mult, ALU.add))
                whole(nb)
                link(V_.tensor_copy(ce, nb))
                src, dst = ce, ce2
                for step in (1, 2, 4):
                    link(V_.tensor_copy(dst[:, 0:step], src[:, 0:step]))
                    link(V_.tensor_tensor(dst[:, step:E], src[:, step:E], src[:, 0:E - step], ALU.add))
                    src, dst = dst, src
                ends = src
                link(V_.tensor_tensor(base_e, ends, nb, ALU.subtract))
                link(V_.tensor_scalar(base_e, base_e, float(ST), None, ALU.mult))
                link(V_.tensor_tensor(ta, ps[:, 4, 0:NT * E].rearrange("p (t e) -> p t e", e=E), tiles(base_e), ALU.add))
                for k in range(TOPK):
                    link(V_.tensor_tensor(tb, oh[:, k], ta, ALU.mult))
                    link(V_.tensor_reduce(pos[:, k * NT:(k + 1) * NT], tb, AX.X, ALU.add))
                link(V_.tensor_scalar(phi, pos, 1.0 / P, -(0.5 - 0.5 / P), ALU.mult, ALU.add))
                whole(phi)
                link(V_.scalar_tensor_tensor(pos, phi, -float(P), pos, ALU.mult, ALU.add))
                dve.wait_ge(sem("x_out"), 16 * NG)
                for n in range(NPC):
                    dve.wait_ge(sem("onehot_used"), n + 1)
                    V_.tensor_tensor(ohL[n % 2], iota.unsqueeze(1).to_broadcast([P, PC, P]),
                                     pos[:, n * PC:(n + 1) * PC].unsqueeze(2).to_broadcast([P, PC, P]), ALU.is_equal)
                    for i in range(PC):
                        m = n * PC + i
                        ins = V_.tensor_scalar(ohH[n % 2][:, i, :], iota[:, 0:NSC], phi[:, m:m + 1], code[:, m % NT:m % NT + 1],
                                               ALU.is_equal, ALU.mult)
                    ins.then_inc(sem("onehot_ready"), 1)
                link(V_.tensor_tensor(cmpb, ends.unsqueeze(1).to_broadcast([P, NSP, E]), iota[:, 0:NSP].unsqueeze(2).to_broadcast([P, NSP, E]), ALU.is_le))
                link(V_.tensor_reduce(exf, cmpb, AX.X, ALU.add))
                V_.tensor_scalar(exi, exf, float(E - 1), None, ALU.min).then_inc(sem("ex_ready"), 1)
                dve.wait_ge(sem("exp_ready"), 1)
                link(V_.tensor_scalar(wts[:, 1], wts[:, 0], 1.0, None, ALU.add))
                link(V_.reciprocal(wts[:, 1], wts[:, 1]))
                link(V_.tensor_scalar(wts[:, 1], wts[:, 1], gsc[:, 3:4], None, ALU.mult))
                link(V_.tensor_tensor(wts[:, 2], wts[:, 0], wts[:, 1], ALU.mult))
                link(V_.tensor_tensor(gates, oh[:, 0], choices(wts[:, 1]), ALU.mult))
                link(V_.tensor_tensor(ta, oh[:, 1], choices(wts[:, 2]), ALU.mult))
                V_.tensor_tensor(gates, gates, ta, ALU.add).then_inc(sem("gates_ready"), 1)
                dve.wait_ge(sem("onehot_used"), NPC + 2)
                link(V_.tensor_copy(idh, ps[:, 6, 0:NSC]))
                link(V_.tensor_copy(idn, idh.bitcast(U16)))
                link(V_.tensor_scalar(idn, idn, float(CODE0), None, ALU.subtract))
                V_.tensor_scalar(gidx, idn, 0.0, None, ALU.max)
                link(V_.tensor_scalar(idt, idn, 0.0, FAR, ALU.is_lt, ALU.mult))
                link(V_.tensor_tensor(sidx, idn, idt, ALU.add))

            def experts():
                dve.wait_ge(sem("b2_in"), 16)

                def cols(ap, j):
                    return ap[:, bass.ds(2 * j, 2)]

                def rows_t(j, par):
                    dve.wait_ge(sem("xsT_ps"), j + 1)
                    after(dve, "eh_ps", 4 * j - 4)
                    V_.tensor_copy(xsT[:, par], ps[:, 0, :].bitcast(F16).rearrange("p (w c n) -> p w c n", w=2, c=KC)).then_inc(sem("xsT_ready"), 1)

                def take_gates(j, par, e):
                    after(dve, "ey_out", 2 * j - 2)
                    V_.tensor_copy(gcur[:, par].unsqueeze(2), xgf[:, par, :, bass.ds(e + D, 1)]).then_inc(sem("gate_ready"), 1)

                def expert_of(j):
                    return dve.value_load(exi[0:1, j:j + 1] if isinstance(j, int) else exi[0:1, bass.ds(j, 1)], min_val=0, max_val=E - 1)

                def split(j, par):
                    def hi(q):
                        dve.wait_ge(sem("gelu_done"), 4 * j + q + 5)
                        if q == 0:
                            after(dve, "ey_ps", 2 * j)
                        V_.tensor_copy(hid[:, par, 0, q * 512:(q + 1) * 512], gel[:, q, :]).then_inc(sem("hhi_ready"), 1)

                    def lo(q):
                        dve.wait_ge(sem("hhi_ready"), 4 * j + q + 1)
                        V_.tensor_tensor(hid[:, par, 1, q * 512:(q + 1) * 512], gel[:, q, :], hid[:, par, 0, q * 512:(q + 1) * 512],
                                         ALU.subtract).then_inc(sem("hlo_ready"), 1)
                    for q in range(4):
                        hi(q)
                        lo(q)

                def output(j, par, e):
                    for s_ in range(2):
                        dve.wait_ge(sem("ey_ps"), 2 * j + s_ + 3)
                        after(dve, "scattered", 16 * (2 * j + s_ - 3))
                        V_.tensor_copy(si2[:, par, s_:s_ + 1], sidx[:, bass.ds(2 * j + s_, 1)])
                        y = yb[:, par, s_, :]
                        V_.scalar_tensor_tensor(y, ps[:, 5 + s_, 0:D], 1.0 / WS, b2t[:, bass.ds(e, 1), :].rearrange("p a n -> p (a n)"),
                                                ALU.mult, ALU.add).then_inc(sem("ey_done"), 1)
                        dve.wait_ge(sem("ey_done"), 2 * j + s_ + 3)
                        V_.tensor_scalar(y, y, gcur[:, par, s_:s_ + 1], None, ALU.mult).then_inc(sem("ey_out"), 1)
                for j in range(2):
                    V_.tensor_copy(gi2[:, j], cols(gidx, j)).then_inc(sem("gidx_ready"), 1)
                e0 = expert_of(0)
                rows_t(0, 0)
                take_gates(0, 0, e0)
                V_.tensor_copy(gi2[:, 0], cols(gidx, 2)).then_inc(sem("gidx_ready"), 1)
                split(0, 0)
                rows_t(1, 1)
                take_gates(1, 1, expert_of(1))
                V_.tensor_copy(gi2[:, 1], cols(gidx, 3)).then_inc(sem("gidx_ready"), 1)

                def pair(r):
                    for u in range(2):
                        j = 2 * r + u
                        split(j + 1, 1 - u)
                        rows_t(j + 2, u)
                        V_.tensor_copy(gi2[:, u], cols(gidx, j + 4)).then_inc(sem("gidx_ready"), 1)
                        output(j, u, expert_of(j))
                        take_gates(j + 2, u, expert_of(j + 2))
                pair(0)
                with dve.Fori(1, (NST - 1) // 2) as r:
                    pair(dve.snap(r))
                output(NST - 1, (NST - 1) % 2, expert_of(NST - 1))

            dve.sem_inc(sem("rows_even"), 16)
            dve.sem_inc(sem("rows_odd"), 16)
            dve.sem_inc(sem("lg_ready"), 1)
            dve.sem_inc(sem("onehot_used"), 2)
            dve.sem_inc(sem("xsT_ready"), 1)
            dve.sem_inc(sem("ey_done"), 2)
            dve.sem_inc(sem("ey_ps"), 2)
            dve.sem_inc(sem("hlo_ready"), 4)
            dve.sem_inc(sem("pv_free"), 2)
            dve.sem_inc(sem("plo_even"), 1)
            dve.sem_inc(sem("plo_odd"), 1)
            dve.sem_inc(sem("pv_ps"), NPB)
            V_.memset(mhalf[:], -0.5).then_inc(sem("half_set"), 1)
            dve.wait_ge(sem("tanh"), 2)
            link(V_.tensor_scalar(gsc[:, 0:2], gsc[:, 4:6], 1.0 / WS, None, ALU.mult))
            dve.wait_ge(sem("x_in"), 16)
            attention(0)
            ffn()
            attention(1)
            router()
            dispatch()
            experts()

        @block.gpsimd
        def _(pool):
            G = nc.gpsimd
            base = [0, 0]

            def link(ins):
                base[1] += 1
                ins.then_inc(sem("pool_link"), 1)
                hold(pool, "pool_link", base[0] + base[1])

            def loop(lo, hi, links, body):
                start = base[0] + base[1]
                with pool.Fori(lo, hi) as r:
                    r = pool.snap(r)
                    base[0], base[1] = r * links + (start - lo * links), 0
                    body(r)
                    assert base[1] == links, base[1]
                base[0], base[1] = start + (hi - lo) * links, 0

            def prep(l):
                for b in range(B):
                    pool.wait_ge(sem("klo_ready"), KC * (l + 1))
                    for g in range(KC):
                        last = G.tensor_tensor(KB[:, b, 1, g, :].rearrange("p (h k) -> p h k", k=NK),
                                               KT[:, 1, g, b * NK:(b + 1) * NK].unsqueeze(1).to_broadcast([P, HG, NK]),
                                               maskk.unsqueeze(2).to_broadcast([P, HG, NK]), ALU.mult)
                last.then_inc(sem("kb_ready"), 1)

            def rsqrt(gi):
                hold(pool, "var_ready", gi + 1)
                link(G.tensor_scalar(rstd[:, 0:GT], mv[:, 0:GT, 1], LN_EPS, None, ALU.add))
                G.tensor_tensor(rstd[:, 0:GT], rstd[:, 0:GT], mhalf[:, 0:GT], ALU.pow).then_inc(sem("rstd_ready"), 1)

            def x_lo(gi):
                hold(pool, "xhi_ready", gi + 1)
                G.tensor_tensor(xs[1], xn.rearrange("p t d -> p (t d)"), xs[0], ALU.subtract).then_inc(sem("xlo_ready"), 1)

            def c_lo(gi):
                hold(pool, "chi_ready", gi + 1)
                G.tensor_tensor(cs[1], cx.rearrange("p t d -> p (t d)"), cs[0], ALU.subtract).then_inc(sem("clo_ready"), 1)

            def add_bias(gi, i):
                xt = X[:, bass.ds(i * GT, GT), :]
                G.tensor_tensor(xt, xt, gbo.unsqueeze(1).to_broadcast([P, GT, D]), ALU.add).then_inc(sem("xb_ready"), 1)

            def half(l, i, par, stats_next, back):
                gi = i + NG * l
                for n in range(NSLOT):
                    if n % 2:
                        rows = ROWS[n % NC5]
                        hold(pool, "p_ready", NSLOT * gi + n + 3)
                        buf = (NSLOT * par + n) % NPB
                        G.tensor_tensor(PP[0:rows, buf, 1, :], PT[0:rows, n % 2, :], PP[0:rows, buf, 0, :],
                                        ALU.subtract).then_inc(sem("plo_odd"), 1)
                    if back and n == 1:
                        c_lo(gi - 1)
                    if stats_next and n == 3:
                        rsqrt(gi + 2)
                    if back and n == 4:
                        add_bias(gi - 1, i - 1)
                    if stats_next and n == 6:
                        x_lo(gi + 2)

            def batch(l, b, first=False, last=False):
                half(l, 2 * b, 0, not last, not first)
                half(l, 2 * b + 1, 1, not last, True)

            def attention(l):
                pool.wait_ge(sem("half_set"), 1)
                rsqrt(NG * l)
                prep(l)
                pool.wait_ge(sem("kb_ready"), 2 * (l + 1))
                x_lo(NG * l)
                hold(pool, "bq_ready", l + 1)
                rsqrt(NG * l + 1)
                x_lo(NG * l + 1)
                batch(l, 0, first=True)
                loop(1, B - 1, 2, lambda b: batch(l, b))
                batch(l, B - 1, last=True)
                c_lo(NG * (l + 1) - 1)
                add_bias(NG * (l + 1) - 1, NG - 1)
            def ffn():
                pool.wait_ge(sem("fb2_ready"), 1)
                def scales(b):
                    hold(pool, "fvar_ready", b + 1)
                    var = fmv[:, :, 1]
                    link(G.tensor_scalar(VE, var, LN_EPS, None, ALU.add))
                    link(G.tensor_tensor(RS_, VE, mhalf[:], ALU.pow))
                    link(G.tensor_tensor(R2, RS_, RS_, ALU.mult))
                    link(G.tensor_tensor(R2, R2, var, ALU.mult))
                    link(G.tensor_scalar(R2, R2, RMS_EPS, None, ALU.add))
                    G.tensor_tensor(R2, R2, mhalf[:], ALU.pow).then_inc(sem("frs_ready"), 1)

                def bias(b):
                    pool.wait_ge(sem("z_ready"), b + 1)
                    xb = X[:, b * TB:(b + 1) * TB, :] if isinstance(b, int) else X[:, bass.ds(b * TB, TB), :]
                    G.tensor_tensor(xb, xb, fb2c.unsqueeze(1).to_broadcast([P, TB, D]), ALU.add).then_inc(sem("xb2_ready"), 1)

                def hidden_rsqrt(k, t):
                    c = slice(t % 4, t % 4 + 1)
                    hold(pool, "ms_ready", k + 1)
                    link(G.tensor_scalar(RR[:, c], MS[:, c], RMS_EPS, None, ALU.add))
                    G.tensor_tensor(RR[:, c], RR[:, c], mhalf[:, 0:1], ALU.pow).then_inc(sem("rr_ready"), 1)

                def batch(b, first=False, last=False):
                    for t in range(TB):
                        hidden_rsqrt(TB * b + t, t)
                        if not last and t == 1:
                            scales(b + 1)
                        if not last and t == 5:
                            bias(b + 1)
                scales(0)
                bias(0)
                batch(0, first=True)
                loop(1, B - 1, TB + 5, lambda b: batch(b))
                batch(B - 1, last=True)

            def split_weights():
                pool.wait_ge(sem("rvar_ready"), 1)
                link(G.tensor_scalar(rrs, rmv[:, :, 1], LN_EPS, None, ALU.add))
                G.tensor_tensor(rrs, rrs, mhalf[:, 0:1].to_broadcast([P, NT]), ALU.pow).then_inc(sem("rrs_ready"), 1)
                with pool.Fori(0, E) as e:
                    e = pool.snap(e)
                    for ch in range(4):
                        hold(pool, "whi_done", 4 * e + ch + 1)
                        c0 = (ch // 2) * 4 * M + (ch % 2) * M
                        hi, lo = (WE[:, bass.ds(e, 1), c:c + M].rearrange("p a n -> p (a n)") for c in (c0, c0 + 2 * M))
                        G.tensor_tensor(lo, wstg[:, ch, :], hi, ALU.subtract).then_inc(sem("wlo_done"), 1)

            def experts():
                def gather(j, par):
                    hold(pool, "gidx_ready", j + 1)
                    hold(pool, "xsT_ps", j - 1)
                    hold(pool, "gate_ready", j - 1)
                    for s_ in range(2):
                        G.indirect_dma_start(xg_[:, par, s_, :].bitcast(U16), None, rowsd, bass.IndirectOffsetOnAxis(ap=gi2[:, par, s_:s_ + 1], axis=0)
                                             ).then_inc(sem(("gathered_even", "gathered_odd")[par]), 16)

                def scatter(j, par):
                    for s_ in range(2):
                        n = 2 * j + s_
                        hold(pool, "ey_out", n + 1)
                        hold(pool, "scattered", 16 * n)
                        G.indirect_dma_start(out, bass.IndirectOffsetOnAxis(ap=si2[:, par, s_:s_ + 1], axis=0), yb[:, par, s_, :], None,
                                             bounds_check=B * S - 1, oob_is_err=False, compute_op=ALU.add).then_inc(sem("scattered"), 16)
                pool.wait_ge(sem("rows_even"), 16 * (NG // 2 + 1))
                pool.wait_ge(sem("rows_odd"), 16 * (NG // 2 + 1))
                pool.wait_ge(sem("gates_out"), 16)
                pool.wait_ge(sem("x_out"), 16 * NG)
                gather(0, 0)
                gather(1, 1)

                def pair(r):
                    for u in range(2):
                        gather(2 * r + u + 2, u)
                        scatter(2 * r + u, u)
                pair(0)
                with pool.Fori(1, (NST - 1) // 2) as r:
                    pair(pool.snap(r))
                scatter(NST - 1, (NST - 1) % 2)
            pool.sem_inc(sem("wlo_done"), 4)
            pool.wait_ge(sem("c_in"), 96)
            attention(0)
            ffn()
            attention(1)
            split_weights()
            experts()


def constants():
    p = np.arange(P)
    c32 = np.zeros((P, C_END), np.float32)
    c32[:, C_MASKK:C_MASKK + HG] = p[:, None] // HD == np.arange(HG)
    for c in range(NC5):
        for j in range(3):
            own = (P * c + p) // NK == HEAD0[c] + j
            c32[:, C_MASKV + 6 * c + j] = c32[:, C_MASKV + 6 * c + 3 + j] = own
            c32[:, C_ONE + 6 * c + j] = own
    ids = CODE0 + np.arange(NT) * P + p[:, None]
    c32[:, C_CODE:C_CODE + NT] = ids.astype(np.uint16).view(np.float16)
    c32[:, C_IOTA:] = np.arange(P)
    one_f, one_b = 0x3C00, 0x3F80
    c16 = np.zeros((P, H_END), np.uint16)
    c16[:, H_IDF:H_IDF + P] = np.eye(P) * one_f
    c16[:, H_IDB:H_IDB + P] = np.eye(P) * one_b
    c16[:, H_UP:H_UP + P] = (p[:, None] < p) * one_b
    c16[:, H_ONES:] = one_b
    ind = (np.arange(H)[:, None] == np.arange(KC * FK) // NK) * one_b
    selk = (p[:, None] == np.arange(FK) % NK) * one_f
    return c32, c16, ind.astype(np.uint16), selk.astype(np.uint16)


def kernel(**inputs):
    import concourse.bacc as _bacc
    from concourse.bass_utils import run_bass_kernel_spmd as _run
    a = {k: np.asarray(v) for k, v in inputs.items()}
    c = np.ascontiguousarray
    zero = np.zeros(D, np.float32)
    L1 = {k: a[f"L1_xattn_{k}"] for k in ("Wq", "Wk", "Wv", "Wo", "bq", "bk", "bv", "bo")}
    bcol = [np.stack([q.reshape(KC, P), k.reshape(KC, P)]).reshape(2 * KC, P).T
            for q, k in ((zero, zero), (L1["bq"], L1["bk"]))]
    c32, c16, ind, selk = constants()
    arrays = {
        "x": c(a["x"]),
        "ctxT": c(a["ctx_1024"].reshape(B * NK, D).T),
        "g_att": c(a["g_xattn"]), "g_ffn": c(a["g_ffn"]),
        "attn_w": np.stack([np.stack([a[f"L0_xattn_{w}"] for w in ("Wq", "Wk", "Wv", "Wo")]),
                            np.stack([L1[w].T for w in ("Wq", "Wk", "Wv", "Wo")])]),
        "attn_bcol": c(np.stack(bcol)),
        "attn_brow": np.stack([np.stack([zero, a["L0_xattn_bo"]]), np.stack([L1["bv"], L1["bo"]])]),
        "fw1": c(a["L0_ffn_w1"].T), "fb1": c(a["L0_ffn_b1"]),
        "fw2": c(a["L0_ffn_w2"].T), "fb2": c(a["L0_ffn_b2"]),
        "wr": c(a["L1_ffn_Wr"].T),
        "ew1": c(a["L1_ffn_W1"].transpose(0, 2, 1)),
        "eb1": c(a["L1_ffn_b1"].reshape(E, MC, P).transpose(2, 0, 1).reshape(P, E * MC)),
        "ew2": c(a["L1_ffn_W2"].transpose(0, 2, 1)),
        "eb2": c(a["L1_ffn_b2"]),
        "c32": c32, "c16": c16, "ind": ind, "selk": selk,
    }
    nc = _bacc.Bacc("TRN2", target_bir_lowering=False, num_devices=1)
    args = {k: nc.dram_tensor(k, v.shape, mybir.dt.from_np(v.dtype), kind="ExternalInput").ap() for k, v in arrays.items()}
    args["out"] = nc.dram_tensor("out", (B * S, D), F32, kind="ExternalOutput").ap()
    build(nc, **args)
    r = _run(nc, [arrays], core_ids=[0])
    return r.results[0]["out"].reshape(B, S, D)
```

```python
import numpy as np
import concourse.bass as bass
from concourse import mybir
from contextlib import ExitStack

F32, F16, BF16 = mybir.dt.float32, mybir.dt.float16, mybir.dt.bfloat16
I32, U32, U16 = mybir.dt.int32, mybir.dt.uint32, mybir.dt.uint16
ACT, ALU, AX = mybir.ActivationFunctionType, mybir.AluOpType, mybir.AxisListType

P = 128
B, S, D = 4, 1024, 256
NT = B * S // P
TB = S // P
GT = 4
GN = GT * P
NG = NT // GT
KC = D // P
H, HD, NK = 16, 16, 77
HG = P // HD
FK = HG * NK
NC5 = -(-FK // P)
ROWS = [min(P, FK - P * c) for c in range(NC5)]
HEAD0 = [min(P * c // NK, HG - 3) for c in range(NC5)]
VW = HD + 1
M = 1024
MC = M // P
E, TOPK = 8, 2
ST = 256
NST = (B * S * TOPK + E * (ST - 1)) // ST
NSP = NST + 3
NSC = NSP * ST // P
ROWW = 2 * D + 2 * E
WS = 32.0
MAGIC = 1.5 * 2.0 ** 23
HALF, MAGIC_H = 1536.0, MAGIC + 0x6600
LN_EPS, RMS_EPS, Q_EPS = 1e-5, 1e-6, 1e-5
NPB = 4
LATE = 4
CODE0 = 0x0400
NPC = 4
PC = TOPK * NT // NPC
FAR = 65536.0

C_MASKK, C_MASKV, C_ONE = 0, HG, HG + 6 * NC5
C_CODE, C_IOTA, C_END = HG + 12 * NC5, HG + 12 * NC5 + NT, HG + 12 * NC5 + NT + P
H_IDF, H_IDB, H_UP, H_ONES, H_IOTA, H_END = 0, P, 2 * P, 3 * P, 4 * P, 5 * P


SLOTS = {
    "pe": {"xh": 0, "xl": 0, "q0": 2, "q1": 2, "max": (4, 6, 7, 8, 9, 10, 12, 14), "mt": 16, "ch": 10, "cl": 11, "p0": 14, "p1": 16},
    "act": {"x": 1, "q0": 2, "q1": 2, "c": 6, "mt": 9},
    "dve": {"x": 1, "q0": 1, "q1": 2, "max": (3, 3, 3, 4, 4, 5, 6, 7), "stats": 2, "attend": 4, "c": 6, "out": 8, "norm": 4},
    "pool": {"c": 2, "rsqrt": 3, "bias": 4, "x": 5},
}


def build(nc, x, ctxT, g_att, g_ffn, attn_w, attn_bcol, attn_brow, fw1, fb1, fw2, fb2,
          wr, ew1, eb1, ew2, eb2, c32, c16, ind, selk, out):
    es = ExitStack()
    with es:
        def sb(name, shape, dt):
            return es.enter_context(nc.sbuf_tensor(name, shape, dt))

        sems = {}

        def sem(name):
            if name not in sems:
                sems[name] = es.enter_context(nc.semaphore(name))
            return sems[name]

        def after(engine, name, value):
            if not isinstance(value, int) or value > 0:
                engine.wait_ge(sem(name), value)

        def hold(engine, name, value):
            after(engine, name, value)
            if not isinstance(value, int):
                engine.sem_inc(sem("carrier"), 1)

        X = sb("X", [P, NT, D], F32)
        WE = sb("WE", [P, E, 8 * M], F16)
        k32 = sb("k32", [P, C_END], F32)
        k16 = sb("k16", [P, H_END], U16)
        indt = sb("indt", [16, KC * FK], U16)
        gsc = sb("gsc", [P, 8], F32)
        gsr = sb("gsr", [P, 4], F32)
        b1t = sb("b1t", [P, E * MC], F32)
        mhalf = sb("mhalf", [P, 8], F32)
        AREA = 10900
        late = WE[:, E - LATE:E, :].rearrange("p e n -> p (e n)").bitcast(F32)
        area = sb("area", [P, AREA], F32)

        class Arena:
            def __init__(self):
                self.a, self.l = 0, 0

            def take(self, shape, dt=F32, parts=P):
                n = int(np.prod(shape)) * (2 if dt in (F16, BF16, U16) else 4) // 4
                if self.l + n <= LATE * 4 * M:
                    ap, self.l = late[0:parts, self.l:self.l + n], self.l + n
                else:
                    assert self.a + n <= AREA, (self.a, n)
                    ap, self.a = area[0:parts, self.a:self.a + n], self.a + n
                if dt != F32:
                    ap = ap.bitcast(dt)
                if len(shape) == 1:
                    return ap
                names = "abcdef"[:len(shape)]
                pat = f"p ({' '.join(names)}) -> p {' '.join(names)}"
                return ap.rearrange(pat, **dict(zip(names[1:], shape[1:])))

        ps = es.enter_context(nc.psum_tensor("ps", [P, 8, 512], F32))
        idf = k16[:, H_IDF:H_IDF + P].bitcast(F16)
        idb = k16[:, H_IDB:H_IDB + P].bitcast(BF16)
        upper = k16[:, H_UP:H_UP + P].bitcast(BF16)
        onesb = k16[:, H_ONES:H_ONES + P].bitcast(BF16)
        indb = indt[:, :].bitcast(BF16).rearrange("h (g n) -> h g n", g=KC)
        maskk = k32[:, C_MASKK:C_MASKK + HG]
        maskv = k32[:, C_MASKV:C_MASKV + 6 * NC5]
        maskone = k32[:, C_ONE:C_ONE + 6 * NC5]
        code = k32[:, C_CODE:C_CODE + NT]
        iota16 = k16[:, H_IOTA:H_IOTA + P].bitcast(F16)
        iota = k32[:, C_IOTA:C_IOTA + P]
        GA = [0, 1]
        GF = [2, 3]
        GX = [4, 5]

        ar = Arena()
        KB = ar.take([B, 2, KC, FK], F16)
        V = ar.take([B, KC * NC5, 6 * VW], F16)
        WQ = ar.take([2, KC, D], F16)
        WO = ar.take([2, KC, D], F16)
        gbo = ar.take([D])
        bcol = ar.take([4])
        xn = ar.take([GT, D])
        stats = ar.take([TB, 6])
        mv = ar.take([TB, 2])
        rstd = ar.take([TB])
        xs = [ar.take([GT * D], F16) for _ in range(2)]
        xT = ar.take([2, KC, GN], F16)
        work0 = (ar.a, ar.l)
        qT = ar.take([2, 2, KC, GN], F16)
        mx = ar.take([GT, H], BF16)
        mxT = ar.take([2, GN], BF16, 16)
        PT = ar.take([2, GN])
        PP = ar.take([NPB, 2, GN], F16)
        cx = ar.take([GT, D])
        cs = [ar.take([GT * D], F16) for _ in range(2)]
        cT = ar.take([2, KC, GN], F16)
        rec = ar.take([2, 2, HG])
        pr = Arena()
        pr.a, pr.l = work0
        wraw = pr.take([4, KC, D])
        sel = pr.take([FK], F16)
        vs = pr.take([B, 2, D], F16)
        cxt = pr.take([KC, B * NK])
        KT = pr.take([2, KC, B * NK], F16)
        bvr = pr.take([D], F32, 1)
        one1 = pr.take([P], F32, 1)
        bosr = pr.take([D])

        fr = Arena()
        wstg = area[:, 0:4 * M].rearrange("p (c n) -> p c n", c=4)
        fr.a = 4 * M
        fw = Arena()
        fw.l, fw.a = LATE * 4 * M, 4 * M
        fraw = fw.take([2, KC * M])
        w1q = fw.take([KC, M], F16)
        w2q = fw.take([MC, D], F16)
        wsm = fw.take([8])
        onef = fw.take([P])
        assert ar.a <= 4 * M
        fb1c = fr.take([M])
        fb2c = fr.take([D])
        y8 = fr.take([TB, D])
        xqT = fr.take([KC, TB * P], F16)
        hpre = fr.take([2, M])
        gl = fr.take([4, M])
        hqT = fr.take([2, MC, P], F16)
        fst = fr.take([TB, 6])
        fmv = fr.take([TB, 2])
        fsm = fr.take([8, TB])
        RS_, VE, R2, AM, INV, SC, DN, D1 = (fsm[:, k, :] for k in range(8))
        tsm = fr.take([8, 4])
        MS, RR, A2, IV2, S2, D2 = (tsm[:, k, :] for k in range(6))
        assert fr.a <= 8 * M
        fsq = fr.take([M], BF16)

        rr = Arena()
        rr.l = LATE * 4 * M
        rr.a = 4 * M
        xr = rr.take([2, GT, 2 * D], F16)
        xrT = rr.take([2, KC, GN], F16)
        xsT0 = rr.a
        xsT = rr.take([2, 2, KC, ST], F16)
        rxn = area[:, xsT0:xsT0 + GT * D].rearrange("p (t d) -> p t d", t=GT)
        rst = area[:, xsT0 - NT * 6:xsT0].rearrange("p (t s) -> p t s", s=6)
        rmv, rrs = rr.take([NT, 2]), rr.take([NT])
        wrr = rr.take([KC, E])
        wrs = rr.take([2, KC, E], F16)
        lg = rr.take([NT, E])
        oh = rr.take([TOPK, NT, E])
        ta, tb = rr.take([NT, E]), rr.take([NT, E])
        gates = rr.take([NT, E])
        Mb = rr.take([NT, E], BF16)
        desc = rr.take([E])
        top, top_s = rr.take([TOPK, NT]), rr.take([NT])
        wts = rr.take([3, NT])
        pos, phi = rr.take([TOPK * NT]), rr.take([TOPK * NT])
        cnt, nb, ce, ce2, base_e = (rr.take([E]) for _ in range(5))
        idh = rr.take([NSC], F16)
        idn, idt = rr.take([NSC]), rr.take([NSC])
        gidx, sidx = rr.take([NSC]).bitcast(I32), rr.take([NSC]).bitcast(I32)
        exf, exi = rr.take([NSP]), rr.take([NSP]).bitcast(I32)
        gi2, si2 = rr.take([2, 2]).bitcast(I32), rr.take([2, 2]).bitcast(I32)
        gcur = rr.take([2, 2])
        xg_ = area[:, 4 * M:4 * M + 2 * 2 * (ROWW // 2)].bitcast(F16).rearrange("p (a s n) -> p a s n", a=2, s=2)
        xgf = area[:, 4 * M:4 * M + 2 * 2 * (ROWW // 2)].rearrange("p (a s n) -> p a s n", a=2, s=2)
        yb = area[:, 0:4 * D].rearrange("p (a s n) -> p a s n", a=2, s=2)
        xall = X[:].rearrange("p t d -> p (t d)")
        hid = xall[:, 0:4096].bitcast(F16).rearrange("p (a w n) -> p a w n", a=2, w=2)
        gel = xall[:, 4096:6144].rearrange("p (q n) -> p q n", q=4)
        b2t = xall[:, 6144:8192].rearrange("p (e n) -> p e n", e=E)
        ohL = [xall[:, b * 1024:(b + 1) * 1024].bitcast(F16).rearrange("p (i n) -> p i n", i=PC) for b in range(2)]
        ohH = [xall[:, 2048 + b * 1024:2048 + b * 1024 + PC * NSC // 2].bitcast(F16).rearrange("p (i n) -> p i n", i=PC) for b in range(2)]
        eflat = area
        cmpb = xall[:, 4096:4096 + NSP * E].rearrange("p (j e) -> p j e", e=E)
        rowsd = nc.dram_tensor("rows", (B * S, ROWW), U16, kind="Internal").ap()
        def low_halves(ap):
            return ap.bitcast(F16).rearrange("p (n two) -> p n two", two=2)[:, :, 0]
        block = es.enter_context(nc.Block())
        DL = {"dve": 0, "act": 0, "pool": 0}

        def gate(t, n):
            return ps[:, t:t + n, :]
        S0, PV0, WF, WT = 0, 2, 4, 6

        NSLOT = KC * NC5
        assert LATE == B and E == 2 * LATE and NG == 2 * LATE

        def load_weights(engine, e, ch):
            w = (ew1, ew2)[ch // 2]
            w = w[e, :, :] if isinstance(e, int) else w[bass.ds(e, 1), :, :].rearrange("a k n -> (a k) n")
            dst = wstg[:, ch, :] if ch < 2 else wstg[:, ch, :].rearrange("p (c n) -> p c n", c=4)
            src = w[ch * P:(ch + 1) * P, :] if ch < 2 else w[(ch - 2) * 4 * P:(ch - 1) * 4 * P, :].rearrange("(c p) n -> p c n", p=P)
            engine.wait_ge(sem("wlo_done"), 4 * e + ch + 1)
            engine.dma_start(dst, src).then_inc(sem(f"w_in{ch}"), 16)

        @block.sync
        def _(sp):
            sp.dma_start(k32[:], c32).then_inc(sem("c_in"), 16)
            sp.dma_start(k16[:], c16).then_inc(sem("c_in"), 16)
            sp.dma_start(indt[:], ind).then_inc(sem("c_in"), 16)
            sp.dma_start(gsr[:, 0:2], g_att.partition_broadcast(P)).then_inc(sem("c_in"), 16)
            sp.dma_start(gsr[:, 2:4], g_ffn.partition_broadcast(P)).then_inc(sem("c_in"), 16)
            sp.dma_start(b1t[:], eb1).then_inc(sem("c_in"), 16)

            def layer_loads(l):
                if l:
                    sp.wait_ge(sem("ffn_out"), NT)
                sp.dma_start(wraw, attn_w[l].rearrange("w (c p) n -> p w c n", p=P)).then_inc(sem("prep_in"), 16)
                sp.dma_start(cxt, ctxT.rearrange("(c p) n -> p c n", p=P)).then_inc(sem("prep_in"), 16)
                sp.dma_start(sel, selk.bitcast(F16)).then_inc(sem("prep_in"), 16)
                sp.dma_start(bcol, attn_bcol[l]).then_inc(sem("prep_in"), 16)
                sp.dma_start(bvr, attn_brow[l, 0:1, :]).then_inc(sem("prep_in"), 16)
                sp.dma_start(bosr, attn_brow[l, 1, :].partition_broadcast(P)).then_inc(sem("prep_in"), 16)
            for b in range(1):
                sp.dma_start(X[:, b * TB:(b + 1) * TB, :], x[b].rearrange("(t p) d -> p t d", p=P)).then_inc(sem("x_in"), 16)
            layer_loads(0)
            for b in range(1, B):
                sp.dma_start(X[:, b * TB:(b + 1) * TB, :], x[b].rearrange("(t p) d -> p t d", p=P)).then_inc(sem("x_in2"), 16)
            sp.dma_start(fraw[:, 0, :].rearrange("p (c n) -> p c n", c=KC), fw1.rearrange("(c p) n -> p c n", p=P)).then_inc(sem("fw_in"), 16)
            sp.dma_start(fraw[:, 1, :].rearrange("p (c n) -> p c n", c=MC), fw2.rearrange("(c p) n -> p c n", p=P)).then_inc(sem("fw_in"), 16)
            sp.wait_ge(sem("att_out"), 2 * NG)
            sp.dma_start(fb1c, fb1.partition_broadcast(P)).then_inc(sem("fb_in"), 16)
            sp.dma_start(fb2c, fb2.partition_broadcast(P)).then_inc(sem("fb_in"), 16)
            with sp.Fori(0, E - LATE) as e:
                e = sp.snap(e)
                for ch in range(4):
                    load_weights(sp, e, ch)
            layer_loads(1)
            sp.wait_ge(sem("att_out"), 4 * NG)
            sp.dma_start(wrr, wr.rearrange("(c p) e -> p c e", p=P)).then_inc(sem("wr_in"), 16)
            xout = out.rearrange("(t p) d -> p t d", p=P)
            rout = rowsd.rearrange("(t p) n -> p t n", p=P)
            for g in range(NG):
                t = slice(g * GT, (g + 1) * GT)
                sp.wait_ge(sem("rlo_ready"), g + 1)
                sp.dma_start(rout[:, t, 0:2 * D], xr[:, g % 2].bitcast(U16)).then_inc(sem(("rows_even", "rows_odd")[g % 2]), 16)
                sp.dma_start(xout[:, t, :], X[:, t, :]).then_inc(sem("x_out"), 16)
            sp.wait_ge(sem("gates_ready"), 1)
            sp.dma_start(rout[:, :, 2 * D:], gates.rearrange("p t e -> p (t e)").bitcast(U16).rearrange("p (t e) -> p t e", t=NT)).then_inc(sem("gates_out"), 16)
            sp.wait_ge(sem("onehot_used"), NPC + 2)
            sp.wait_ge(sem("x_out"), 16 * NG)
            sp.dma_start(b2t, eb2.partition_broadcast(P)).then_inc(sem("b2_in"), 16)
            sp.wait_ge(sem("scattered"), 16 * 2 * NST)

        PREP_DMAS = 6

        @block.tensor
        def _(pe):
            T = nc.tensor

            def prep(l):
                pe.wait_ge(sem("prep_in"), 16 * PREP_DMAS * (l + 1))
                for m in range(KC):
                    for c in range(KC):
                        last = T.matmul(ps[:, m, 0:B * NK], wraw[:, 1, c, m * P:(m + 1) * P], cxt[:, c, :],
                                        start=c == 0, stop=c == KC - 1)
                    last.then_inc(sem("kt_ps"), 1)
                pe.wait_ge(sem("one_set"), l + 1)
                for b in range(B):
                    o = ps[0:NK, 4 + b, 0:D]
                    for k in range(KC):
                        T.matmul(o, cxt[:, k, b * NK:(b + 1) * NK], wraw[:, 2, k, :], start=k == 0, stop=False)
                    T.matmul(o, one1[:, 0:NK], bvr, start=False, stop=True).then_inc(sem("v_ps"), 1)
                for b in range(B):
                    pe.wait_ge(sem("vlo_ready"), B * l + b + 1)
                    pe.wait_ge(sem("klo_ready"), KC * (l + 1))
                    if b >= 2:
                        pe.wait_ge(sem("v_ready"), KC * (B * l + b - 1))
                    for g in range(KC):
                        for c in range(NC5):
                            col = g * P + HD * HEAD0[c]
                            last = T.matmul(ps[0:ROWS[c], 2 * (b % 2) + g, c * 96:(c + 1) * 96].rearrange("p (a n) -> p a n", a=2),
                                            sel[0:NK, c * P:c * P + ROWS[c]], vs[0:NK, b, :, col:col + 48],
                                            start=True, stop=True)
                        last.then_inc(sem("vsel_ps"), 1)

            def transposes(bank, src, rows=GT):
                dst = ps[:, bank, :].bitcast(F16).rearrange("p (c n) -> p c n", c=KC)
                sv = src.rearrange("p (t c n) -> p t c n", t=GT, c=KC)
                for c in range(KC):
                    for t in range(GT):
                        last = T.transpose(dst[:, c, t * P:(t + 1) * P], sv[:, t, c, :], idf)
                return last

            def query_jobs(l, i, b, par, first=False):
                gi = i + NG * l

                def x_hi():
                    pe.wait_ge(sem("xhi_ready"), gi + 1)
                    transposes(WF, xs[0]).then_inc(sem("xT_ps"), 1)

                def x_lo():
                    pe.wait_ge(sem("xlo_ready"), gi + 1)
                    transposes(WF + 1, xs[1]).then_inc(sem("xT_ps"), 1)

                def query(m):
                    pe.wait_ge(sem("xThi_ready"), gi + 1)
                    cols = slice(m * P, (m + 1) * P)
                    T.matmul(ps[:, WF + m, :], WQ[:, 0, 0, cols], xT[:, 0, 0, :], start=True, stop=False)
                    T.matmul(ps[:, WF + m, :], WQ[:, 0, 1, cols], xT[:, 0, 1, :], start=False, stop=False)
                    T.matmul(ps[:, WF + m, :], WQ[:, 1, 0, cols], xT[:, 0, 0, :], start=False, stop=False)
                    T.matmul(ps[:, WF + m, :], WQ[:, 1, 1, cols], xT[:, 0, 1, :], start=False, stop=False)
                    pe.wait_ge(sem("xTlo_ready"), gi + 1)
                    T.matmul(ps[:, WF + m, :], WQ[:, 0, 0, cols], xT[:, 1, 0, :], start=False, stop=False)
                    T.matmul(ps[:, WF + m, :], WQ[:, 0, 1, cols], xT[:, 1, 1, :], start=False, stop=True).then_inc(sem("q_ps"), 1)

                def q0():
                    query(0)

                def q1():
                    query(1)
                    
                def max_scores(n, other=False):
                    base_ = WT if other and n % 2 else WF

                    def run():
                        t, g = n // KC, n % KC
                        if n == 0:
                            pe.wait_ge(sem("qhi_ready"), KC * (gi + 1))
                            pe.wait_ge(sem("qlo_ready"), KC * (gi + 1))
                        else:
                            after(pe, "max_done", GT * KC * gi + n - (1 if other else 0))
                        for h in range(2):
                            last = T.matmul(ps[:, base_ + h, 0:4 * NK], qT[:, par, 0, g, t * P:(t + 1) * P],
                                            KB[:, b, 0, g, h * 4 * NK:(h + 1) * 4 * NK], start=True, stop=True)
                        last.then_inc(sem("max_ps"), 1)
                    return run

                def max_t():
                    pe.wait_ge(sem("max_done"), GT * KC * (gi + 1))
                    dst = ps[0:H, WF, :].bitcast(BF16)
                    for t in range(GT):
                        last = T.transpose(dst[:, t * P:(t + 1) * P], mx[:, t, :], idb)
                    last.then_inc(sem("mxT_ps"), 1)
                return x_hi, x_lo, q0, q1, [max_scores(n, first) for n in range(GT * KC)], max_t

            def out_jobs(l, i):
                gi = i + NG * l

                def c_hi():
                    pe.wait_ge(sem("chi_ready"), gi + 1)
                    transposes(WT, cs[0]).then_inc(sem("cT_ps"), 1)

                def c_lo():
                    pe.wait_ge(sem("clo_ready"), gi + 1)
                    transposes(WT + 1, cs[1]).then_inc(sem("cT_ps"), 1)

                def project(u):
                    pe.wait_ge(sem("cThi_ready"), gi + 1)
                    pe.wait_ge(sem("cTlo_ready"), gi + 1)
                    for v in range(2):
                        t = 2 * u + v
                        o = ps[:, WT + u, v * D:(v + 1) * D]
                        n = 0
                        for a, w in ((0, 0), (0, 1), (1, 0)):
                            for c in range(KC):
                                last = T.matmul(o, cT[:, a, c, t * P:(t + 1) * P], WO[:, w, c, :],
                                                start=n == 0, stop=n == 5)
                                n += 1
                    last.then_inc(sem("o_ps"), 1)
                return c_hi, c_lo, lambda: project(0), lambda: project(1)

            PARTS = ((0, 0), (0, 1), (1, 0))

            def scores(l, i, b, par, n):
                N = NSLOT * (i + NG * l) + n
                g, c = n // NC5, n % NC5
                rows = ROWS[c]
                if n == 0:
                    pe.wait_ge(sem("mxT_ready"), i + NG * l + 1)
                pe.wait_ge(sem("p_ready"), N + 1)
                o = ps[0:rows, S0 + n % 2, :]
                cols = slice(c * P, c * P + rows)
                T.matmul(o, KB[:, b, 0, g, cols], qT[:, par, 0, g, :], start=True, stop=False)
                T.matmul(o, KB[:, b, 1, g, cols], qT[:, par, 0, g, :], start=False, stop=False)
                T.matmul(o, KB[:, b, 0, g, cols], qT[:, par, 1, g, :], start=False, stop=False)
                T.matmul(o, indb[:, g, cols], mxT[:, par, :], start=False, stop=True).then_inc(sem("s_ps"), 1)

            def values(l, i, b, par, n):
                gi = i + NG * l
                N = NSLOT * gi + n
                g, c = n // NC5, n % NC5
                if c == 0:
                    pe.wait_ge(sem("pv_free"), 4 * gi + 2 * g + 2)
                pe.wait_ge(sem(("plo_even", "plo_odd")[n % 2]), NSLOT // 2 * gi + n // 2 + 2)
                rows, h0 = ROWS[c], HEAD0[c]
                for t in range(GT):
                    o = ps[:, PV0 + t // 2, (t % 2) * HG * VW + h0 * VW:(t % 2) * HG * VW + (h0 + 3) * VW]
                    for m, (a, w) in enumerate(PARTS):
                        last = T.matmul(o, PP[0:rows, (NSLOT * par + n) % NPB, a, t * P:(t + 1) * P], V[0:rows, b, n, w * 3 * VW:(w + 1) * 3 * VW],
                                        start=c == 0 and t % 2 == 0 and m == 0, stop=c == NC5 - 1 and m == 2,
                                        skip_group_check=True)
                last.then_inc(sem("pv_ps"), 1)

            def weight_sums():
                pe.wait_ge(sem("w_sums"), 1)
                T.matmul(ps[:, 7, 0:2], onef, wsm[:, 0:2], start=True, stop=True).then_inc(sem("w_tot"), 1)

            def half(l, i, b, par, before, behind, nxt):
                for n in range(NSLOT):
                    if n + 2 < NSLOT:
                        scores(l, i, b, par, n + 2)
                    for job in before.get(n, ()):
                        job()
                    values(l, i, b, par, n)
                    for job in behind.get(n, ()):
                        job()
                    if n + 2 >= NSLOT and nxt is not None:
                        scores(l, i + 1, nxt, 1 - par, n + 2 - NSLOT)

            def slots(front, back):
                before, behind = {}, {}

                def put(place, job):
                    (behind if place % 2 else before).setdefault(place // 2, []).append(job)
                at = SLOTS["pe"]
                if front:
                    xh, xl, q0, q1, mxs, mt = front
                    put(at["xh"], xh)
                    put(at["xl"], xl)
                    put(at["q0"], q0)
                    put(at["q1"], q1)
                    for n, job in enumerate(mxs):
                        put(at["max"][n], job)
                    put(at["mt"], mt)
                if back:
                    for name, job in zip(("ch", "cl", "p0", "p1"), back):
                        put(at[name], job)
                return before, behind

            def batch(l, b, first=False, last=False):
                before, behind = slots(query_jobs(l, 2 * b + 1, b, 1), None if first else out_jobs(l, 2 * b - 1))
                if first and l == 0:
                    behind.setdefault(5, []).append(weight_sums)
                half(l, 2 * b, b, 0, before, behind, b)
                front = None if last else query_jobs(l, 2 * b + 2, b + 1, 0)
                half(l, 2 * b + 1, b, 1, *slots(front, out_jobs(l, 2 * b)), None if last else b + 1)

            def attention(l):
                prep(l)
                pe.wait_ge(sem("kb_ready"), 2 * (l + 1))
                pe.wait_ge(sem("wsplit"), 2 * (l + 1))
                xh, xl, q0, q1, mxs, mt = query_jobs(l, 0, 0, 0, first=True)
                for job in (xh, xl, q0, q1, *mxs, mt):
                    job()
                pe.wait_ge(sem("v_ready"), KC * B * (l + 1))
                scores(l, 0, 0, 0, 0)
                scores(l, 0, 0, 0, 1)
                batch(l, 0, first=True)
                with pe.Fori(1, B - 1) as b:
                    batch(l, pe.snap(b))
                batch(l, B - 1, last=True)
                for job in out_jobs(l, NG - 1):
                    job()
            HB, TQ, YB = (2, 4), 6, (7, 0)

            def ffn():
                pe.wait_ge(sem("wq_ready"), 2)

                def xq_t(b, v):
                    if v == 0:
                        pe.wait_ge(sem("z_ready"), b + 1)
                    else:
                        pe.wait_ge(sem("xqT_ready"), 2 * b + 1)
                    dst = ps[:, 1, :].bitcast(F16).rearrange("p (c n) -> p c n", c=KC)
                    for c in range(KC):
                        for t in range(GT):
                            last = T.transpose(dst[:, c, t * P:(t + 1) * P], low_halves(y8[:, GT * v + t, c * P:(c + 1) * P]), idf)
                    last.then_inc(sem("xqT_ps"), 1)

                def hidden(b, t):
                    if t % GT == 0:
                        pe.wait_ge(sem("xqT_ready"), 2 * b + t // GT + 1)
                    pe.wait_ge(sem("hpre_ready"), TB * b + t + 1)
                    for h in range(2):
                        for c in range(KC):
                            last = T.matmul(ps[:, HB[t % 2] + h, :], xqT[:, c, t * P:(t + 1) * P],
                                            w1q[:, c, h * 512:(h + 1) * 512], start=c == 0, stop=c == KC - 1)
                    last.then_inc(sem("h_ps"), 1)

                def hidden_t(k, t):
                    pe.wait_ge(sem("zz_ready"), k + 1)
                    pe.wait_ge(sem("hqT_ready"), k + 1)
                    dst = ps[:, TQ, :].bitcast(F16)
                    for c in range(MC):
                        last = T.transpose(dst[:, c * P:(c + 1) * P], low_halves(gl[:, t % 4, c * P:(c + 1) * P]), idf)
                    last.then_inc(sem("hqT_ps"), 1)

                def project(k, t):
                    pe.wait_ge(sem("hqT_ready"), k + 2)
                    after(pe, "ffn_out", k - 1)
                    for c in range(MC):
                        last = T.matmul(ps[:, YB[t % 2], 0:D], hqT[:, t % 2, c, :], w2q[:, c, :], start=c == 0, stop=c == MC - 1)
                    last.then_inc(sem("y_ps"), 1)

                def batch(b, first=False, last=False):
                    for t in range(TB):
                        k = TB * b + t
                        hidden(b, t)
                        if not last and t == TB - 1:
                            xq_t(b + 1, 0)
                            xq_t(b + 1, 1)
                        if not first or t >= 2:
                            hidden_t(k - 2, (t - 2) % TB)
                        if not first or t >= 3:
                            project(k - 3, (t - 3) % TB)
                xq_t(0, 0)
                xq_t(0, 1)
                batch(0, first=True)
                with pe.Fori(1, B - 1) as b:
                    batch(pe.snap(b))
                batch(B - 1, last=True)
                hidden_t(NT - 2, TB - 2)
                project(NT - 3, TB - 3)
                hidden_t(NT - 1, TB - 1)
                project(NT - 2, TB - 2)
                project(NT - 1, TB - 1)

            RT, LGB, RK = (6, 7), 5, 4

            def router():
                pe.wait_ge(sem("wr_split"), 1)

                def group(g, par):
                    pe.wait_ge(sem("rlo_ready"), g + 1)
                    for a in range(2):
                        dst = ps[:, RT[a], :].bitcast(F16).rearrange("p (c n) -> p c n", c=KC)
                        for c in range(KC):
                            for t in range(GT):
                                last = T.transpose(dst[:, c, t * P:(t + 1) * P], xr[:, par, t, a * D + c * P:a * D + (c + 1) * P], idf)
                        last.then_inc(sem("rT_ps"), 1)
                    pe.wait_ge(sem("rThi_ready"), g + 1)
                    pe.wait_ge(sem("rTlo_ready"), g + 1)
                    pe.wait_ge(sem("lg_ready"), g + 1)
                    for t in range(GT):
                        n = 0
                        for a, w in ((0, 0), (0, 1), (1, 0)):
                            for c in range(KC):
                                last = T.matmul(ps[:, LGB, t * E:(t + 1) * E], xrT[:, a, c, t * P:(t + 1) * P], wrs[:, w, c, :],
                                                start=n == 0, stop=n == 5)
                                n += 1
                    last.then_inc(sem("lg_ps"), 1)
                with pe.Fori(0, NG // 2) as r:
                    r = pe.snap(r)
                    for u in range(2):
                        group(2 * r + u, u)

            def dispatch():
                pe.wait_ge(sem("m_ready"), 1)
                T.matmul(ps[:, RK, 0:NT * E], upper, Mb.rearrange("p t e -> p (t e)"), start=True, stop=False, skip_group_check=True)
                for t in range(NT):
                    last = T.matmul(ps[:, RK, (t + 1) * E:(NT + 1) * E].rearrange("p (t e) -> p t e", e=E), onesb,
                                    Mb[:, t, :].unsqueeze(1).to_broadcast([P, NT - t, E]), start=False, stop=t == NT - 1, skip_group_check=True)
                last.then_inc(sem("rank_ps"), 1)
                for n in range(NPC):
                    pe.wait_ge(sem("onehot_ready"), n + 1)
                    for i in range(PC):
                        last = T.matmul(ps[:, 6, 0:NSC], ohL[n % 2][:, i, :], ohH[n % 2][:, i, :],
                                        start=n == 0 and i == 0, stop=n == NPC - 1 and i == PC - 1)
                    last.then_inc(sem("onehot_used"), 1)

            XTB, H1, YB2 = 0, 1, (5, 6)

            def experts():
                pe.wait_ge(sem("ex_ready"), 1)
                pe.wait_ge(sem("wlo_done"), 4 * E + 4)

                def expert_of(j):
                    return pe.value_load(exi[0:1, j:j + 1] if isinstance(j, int) else exi[0:1, bass.ds(j, 1)], min_val=0, max_val=E - 1)

                def rows_t(j, par, jh):
                    pe.wait_ge(sem(("gathered_even", "gathered_odd")[par]), 32 * (jh + 1))
                    pe.wait_ge(sem("xsT_ready"), j + 1)
                    dst = ps[:, XTB, :].bitcast(F16).rearrange("p (w c n) -> p w c n", w=2, c=KC)
                    for w in range(2):
                        for c in range(KC):
                            for s_ in range(2):
                                last = T.transpose(dst[:, w, c, s_ * P:(s_ + 1) * P], xg_[:, par, s_, w * D + c * P:w * D + (c + 1) * P], idf)
                    last.then_inc(sem("xsT_ps"), 1)

                def hidden(j, par, e):
                    pe.wait_ge(sem("xsT_ready"), j + 2)
                    for q in range(4):
                        pe.wait_ge(sem("gelu_done"), 4 * j + q + 1)
                        for m in (2 * q, 2 * q + 1):
                            n = 0
                            for a, w in ((0, 0), (1, 0), (0, 1)):
                                for c in range(KC):
                                    lw = WE[:, bass.ds(e, 1), a * 2 * M + c * M + m * P:a * 2 * M + c * M + (m + 1) * P].rearrange("p a n -> p (a n)")
                                    last = T.matmul(ps[:, H1 + q, (m % 2) * ST:(m % 2 + 1) * ST], lw, xsT[:, par, w, c, :],
                                                    start=n == 0, stop=n == 5)
                                    n += 1
                        last.then_inc(sem("eh_ps"), 1)

                def project(j, par, e):
                    for s_ in range(2):
                        pe.wait_ge(sem("ey_done"), 2 * j + s_ + 1)
                        n = 0
                        for m in range(MC):
                            if s_ == 0 and m % 2 == 0:
                                pe.wait_ge(sem("hlo_ready"), 4 * j + m // 2 + 5)
                            for a, w in ((0, 0), (0, 1), (1, 0)):
                                rw = WE[:, bass.ds(e, 1), 4 * M + a * 2 * M + m * D:4 * M + a * 2 * M + (m + 1) * D].rearrange("p a n -> p (a n)")
                                last = T.matmul(ps[:, YB2[s_], 0:D], hid[:, par, w, m * ST + s_ * P:m * ST + (s_ + 1) * P], rw,
                                                start=n == 0, stop=n == 3 * MC - 1)
                                n += 1
                        last.then_inc(sem("ey_ps"), 1)
                rows_t(0, 0, 0)
                hidden(0, 0, expert_of(0))
                rows_t(1, 1, 0)
                with pe.Fori(0, (NST - 1) // 2) as r:
                    r = pe.snap(r)
                    for u in range(2):
                        this, ahead = expert_of(2 * r + u), expert_of(2 * r + u + 1)
                        hidden(2 * r + u + 1, 1 - u, ahead)
                        rows_t(2 * r + u + 2, u, r + 1)
                        project(2 * r + u, u, this)
                project(NST - 1, (NST - 1) % 2, expert_of(NST - 1))
            pe.wait_ge(sem("c_in"), 96)
            attention(0)
            ffn()
            attention(1)
            router()
            dispatch()
            experts()

        @block.scalar
        def _(act):
            A = nc.scalar

            def prep(l):
                act.wait_ge(sem("prep_in"), 16 * PREP_DMAS * (l + 1))
                for w, dst in ((0, WQ), (3, WO)):
                    A.mul(dst[:, 0, :, :], wraw[:, w, :, :], WS).then_inc(sem("whi_ready"), 1)
                for m in range(KC):
                    act.wait_ge(sem("kt_ps"), KC * l + m + 1)
                    A.activation(KT[:, 0, m, :], ps[:, m, 0:B * NK], ACT.Identity, bias=bcol[:, 2 + m:3 + m]).then_inc(sem("khi_ready"), 1)

                for b in range(B):
                    act.wait_ge(sem("v_ps"), B * l + b + 1)
                    A.copy(vs[0:NK, b, 0, :], ps[0:NK, 4 + b, 0:D]).then_inc(sem("vhi_ready"), 1)

            def half(l, i, par, front, back):
                gi = i + NG * l
                qp = 1 - par

                def exp(n):
                    N = NSLOT * gi + n
                    rows = ROWS[n % NC5]
                    act.wait_ge(sem("s_ps"), N + 1)
                    act.wait_ge(sem("pv_ps"), N + 1)
                    src = ps[0:rows, S0 + n % 2, :]
                    A.activation(PP[0:rows, (NSLOT * par + n) % NPB, 0, :], src, ACT.Exp, scale=HD ** -0.5 / WS)
                    act.wait_ge(sem(("plo_even", "plo_odd")[n % 2]), NSLOT // 2 * gi + n // 2 + 1)
                    A.activation(PT[0:rows, n % 2, :], src, ACT.Exp, scale=HD ** -0.5 / WS).then_inc(sem("p_ready"), 1)
                at = SLOTS["act"]
                for n in range(NSLOT):
                    exp(n)
                    if front and n == at["x"]:
                        x_hi(gi + 1)
                    for m in range(KC):
                        if front and n == at[f"q{m}"]:
                            q_hi(gi + 1, qp, m)
                    if back and n == at["c"]:
                        c_hi(gi - 1)
                    if front and n == at["mt"]:
                        m_t(gi + 1, qp)

            def x_hi(gi):
                act.wait_ge(sem("xT_ps"), 2 * gi + 1)
                A.copy(xT[:, 0, :, :], ps[:, WF, :].bitcast(F16).rearrange("p (c n) -> p c n", c=KC)).then_inc(sem("xThi_ready"), 1)

            def q_hi(gi, par, m):
                act.wait_ge(sem("q_ps"), KC * gi + m + 1)
                A.activation(qT[:, par, 0, m, :], ps[:, WF + m, :], ACT.Identity, bias=bcol[:, m:m + 1]).then_inc(sem("qhi_ready"), 1)

            def m_t(gi, par):
                act.wait_ge(sem("mxT_ps"), gi + 1)
                A.copy(mxT[:, par, :], ps[0:H, WF, :].bitcast(BF16)[:, 0:GN]).then_inc(sem("mxT_ready"), 1)

            def c_hi(gi):
                act.wait_ge(sem("cT_ps"), 2 * gi + 1)
                A.copy(cT[:, 0, :, :], ps[:, WT, :].bitcast(F16).rearrange("p (c n) -> p c n", c=KC)).then_inc(sem("cThi_ready"), 1)

            def batch(l, b, first=False, last=False):
                half(l, 2 * b, 0, True, not first)
                half(l, 2 * b + 1, 1, not last, True)

            def attention(l):
                prep(l)
                act.wait_ge(sem("bq_ready"), l + 1)
                g0 = NG * l
                x_hi(g0)
                q_hi(g0, 0, 0)
                q_hi(g0, 0, 1)
                m_t(g0, 0)
                batch(l, 0, first=True)
                with act.Fori(1, B - 1) as b:
                    batch(l, act.snap(b))
                batch(l, B - 1, last=True)
                c_hi(NG * (l + 1) - 1)
            def ffn():
                def xq_copy(b, v):
                    act.wait_ge(sem("xqT_ps"), 2 * b + v + 1)
                    A.activation(xqT[:, :, v * GN:(v + 1) * GN], ps[:, 1, :].bitcast(F16).rearrange("p (c n) -> p c n", c=KC), ACT.Copy,
                                 bias=-HALF).then_inc(sem("xqT_ready"), 1)

                def gelu(k, t):
                    act.wait_ge(sem("hpre_ready"), k + 3)
                    after(act, "hqT_ps", k - 3)
                    A.activation(gl[:, t % 4, :], hpre[:, t % 2, :], ACT.Gelu).then_inc(sem("gl_ready"), 1)
                    act.wait_ge(sem("gl_ready"), k + 1)
                    A.activation(fsq, gl[:, t % 4, :], ACT.Square, scale=M ** -0.5,
                                 accum_out=MS[:, t % 4:t % 4 + 1]).then_inc(sem("ms_ready"), 1)

                def multiple(k, t):
                    act.wait_ge(sem("s2_ready"), k + 1)
                    g = gl[:, t % 4, :]
                    A.activation(g, g, ACT.Copy, bias=MAGIC_H, scale=S2[:, t % 4:t % 4 + 1]).then_inc(sem("zz_ready"), 1)

                def batch(b, first=False, last=False):
                    for t in range(TB):
                        k = TB * b + t
                        gelu(k, t)
                        if not last and t == TB - 1:
                            xq_copy(b + 1, 0)
                            xq_copy(b + 1, 1)
                        if not first or t >= 1:
                            multiple(k - 1, (t - 1) % TB)
                        if t % 2:
                            split(b, t // 2)
                xq_copy(0, 0)
                xq_copy(0, 1)
                batch(0, first=True)
                with act.Fori(1, B - 1) as b:
                    batch(act.snap(b))
                batch(B - 1, last=True)
                multiple(NT - 1, TB - 1)

            def split(e, ch):
                act.wait_ge(sem(f"w_in{ch}"), 16 * (e + 1))
                A.mul(wstg[:, ch, :], wstg[:, ch, :], WS).then_inc(sem("w_scaled"), 1)
                act.wait_ge(sem("w_scaled"), 4 * e + ch + 1)
                c0 = (ch // 2) * 4 * M + (ch % 2) * M
                A.copy(WE[:, e, c0:c0 + M] if isinstance(e, int) else WE[:, bass.ds(e, 1), c0:c0 + M].rearrange("p a n -> p (a n)"),
                       wstg[:, ch, :]).then_inc(sem("whi_done"), 1)

            def router():
                act.wait_ge(sem("att_out"), 4 * NG)
                e0 = E - LATE
                load_weights(act, e0, 0)
                load_weights(act, e0, 1)

                def expert(e, g, last=False):
                    for ch in range(4):
                        if ch % 2 == 0:
                            act.wait_ge(sem("rT_ps"), 2 * (g + ch // 2) + 1)
                            A.copy(xrT[:, 0], ps[:, 6, :].bitcast(F16).rearrange("p (c n) -> p c n", c=KC)).then_inc(sem("rThi_ready"), 1)
                        if not last or ch < 2:
                            load_weights(act, e + (ch + 2) // 4, (ch + 2) % 4)
                        split(e, ch)
                with act.Fori(0, LATE - 1) as r:
                    r = act.snap(r)
                    expert(e0 + r, 2 * r)
                expert(E - 1, NG - 2, last=True)
                act.wait_ge(sem("tops_ready"), 1)
                A.activation(wts[:, 0, :], wts[:, 0, :], ACT.Exp).then_inc(sem("exp_ready"), 1)

            def experts():
                act.wait_ge(sem("ex_ready"), 1)

                def gelu(j):
                    e = act.value_load(exi[0:1, j:j + 1] if isinstance(j, int) else exi[0:1, bass.ds(j, 1)], min_val=0, max_val=E - 1)
                    for q in range(4):
                        act.wait_ge(sem("eh_ps"), 4 * j + q + 1)
                        act.wait_ge(sem("hlo_ready"), 4 * j + q + 1)
                        for v in range(2):
                            last = A.activation(gel[:, q, v * ST:(v + 1) * ST], ps[:, 1 + q, v * ST:(v + 1) * ST], ACT.Gelu,
                                                bias=b1t[:, bass.ds(e * MC + 2 * q + v, 1)], scale=1.0 / WS)
                        last.then_inc(sem("gelu_done"), 1)
                gelu(0)
                with act.Fori(0, (NST - 1) // 2) as r:
                    r = act.snap(r)
                    for u in range(2):
                        gelu(2 * r + u + 1)
            act.sem_inc(sem("gelu_done"), 4)
            act.sem_inc(sem("p_ready"), 2)
            act.wait_ge(sem("c_in"), 96)
            A.activation(gsc[:, 2:4], gsr[:, 2:4], ACT.Tanh).then_inc(sem("tanh"), 1)
            A.activation(gsc[:, 4:6], gsr[:, 0:2], ACT.Tanh).then_inc(sem("tanh"), 1)
            attention(0)
            ffn()
            attention(1)
            router()
            experts()

        @block.vector
        def _(dve):
            V_ = nc.vector
            base = [0, 0]

            def link(ins, wait=after):
                base[1] += 1
                ins.then_inc(sem("dve_link"), 1)
                wait(dve, "dve_link", base[0] + base[1])

            def loop(lo, hi, links, body):
                start = base[0] + base[1]
                with dve.Fori(lo, hi) as r:
                    r = dve.snap(r)
                    base[0], base[1] = r * links + (start - lo * links), 0
                    body(r)
                    assert base[1] == links, base[1]
                base[0], base[1] = start + (hi - lo) * links, 0

            def prep(l):
                dve.wait_ge(sem("prep_in"), 16 * PREP_DMAS * (l + 1))
                V_.memset(one1, 1.0).then_inc(sem("one_set"), 1)
                link(V_.tensor_scalar(bcol[:, 0:KC], bcol[:, 0:KC], WS, None, ALU.mult))
                V_.tensor_scalar(gbo, bosr, gsc[:, GX[l]:GX[l] + 1], None, ALU.mult).then_inc(sem("bq_ready"), 1)
                for n, (w, dst) in enumerate(((0, WQ), (3, WO))):
                    dve.wait_ge(sem("whi_ready"), 2 * l + n + 1)
                    V_.scalar_tensor_tensor(dst[:, 1, :, :], wraw[:, w, :, :], WS, dst[:, 0, :, :],
                                            ALU.mult, ALU.subtract).then_inc(sem("wsplit"), 1)
                for m in range(KC):
                    dve.wait_ge(sem("khi_ready"), KC * l + m + 1)
                    ins = V_.scalar_tensor_tensor(KT[:, 1, m, :], ps[:, m, 0:B * NK], bcol[:, 2 + m:3 + m],
                                                  KT[:, 0, m, :], ALU.add, ALU.subtract)
                    ins.then_inc(sem("klo_ready"), 1)
                for b in range(B):
                    dve.wait_ge(sem("vhi_ready"), B * l + b + 1)
                    V_.tensor_tensor(vs[0:NK, b, 1, :], ps[0:NK, 4 + b, 0:D], vs[0:NK, b, 0, :], ALU.subtract).then_inc(sem("vlo_ready"), 1)
                for b in range(B):
                    for g in range(KC):
                        last = V_.tensor_tensor(KB[:, b, 0, g, :].rearrange("p (h k) -> p h k", k=NK),
                                                KT[:, 0, g, b * NK:(b + 1) * NK].unsqueeze(1).to_broadcast([P, HG, NK]),
                                                maskk.unsqueeze(2).to_broadcast([P, HG, NK]), ALU.mult)
                last.then_inc(sem("kb_ready"), 1)
                for b in range(B):
                    for g in range(KC):
                        dve.wait_ge(sem("vsel_ps"), KC * (B * l + b) + g + 1)
                        n4 = NC5 - 1
                        for r, c0, nc_ in ((P, 0, n4), (ROWS[n4], n4, 1)):
                            dst = V[0:r, b, g * NC5 + c0:g * NC5 + c0 + nc_, :].rearrange("p c (j v) -> p (c j) v", v=VW)
                            V_.tensor_tensor(dst[:, :, 0:HD],
                                             ps[0:r, 2 * (b % 2) + g, c0 * 96:(c0 + nc_) * 96].rearrange("p (j v) -> p j v", v=HD),
                                             maskv[0:r, 6 * c0:6 * (c0 + nc_)].unsqueeze(2).to_broadcast([r, 6 * nc_, HD]), ALU.mult)
                            last = V_.tensor_copy(dst[:, :, HD], maskone[0:r, 6 * c0:6 * (c0 + nc_)])
                        last.then_inc(sem("v_ready"), 1)

            def norm_stats(gi, i):
                for t in range(GT):
                    ins = V_.bn_stats(stats[:, t, :], X[:, t + GT * i, :] if isinstance(i, int) else X[:, bass.ds(i * GT + t, 1), :])
                link(ins, hold)
                for t in range(GT):
                    ins = V_.bn_aggr(mv[:, t, :], stats[:, t, :])
                ins.then_inc(sem("var_ready"), 1)

            def norm(gi, i):
                dve.wait_ge(sem("rstd_ready"), gi + 1)
                for t in range(GT):
                    xt = X[:, t + GT * i, :] if isinstance(i, int) else X[:, bass.ds(i * GT + t, 1), :]
                    ins = V_.tensor_scalar(xn[:, t, :], xt, mv[:, t, 0:1], rstd[:, t:t + 1], ALU.subtract, ALU.mult)
                link(ins)
                V_.tensor_copy(xs[0], xn.rearrange("p t d -> p (t d)")).then_inc(sem("xhi_ready"), 1)

            def x_lo(gi):
                dve.wait_ge(sem("xT_ps"), 2 * gi + 2)
                V_.tensor_copy(xT[:, 1, :, :], ps[:, WF + 1, :].bitcast(F16).rearrange("p (c n) -> p c n", c=KC)).then_inc(sem("xTlo_ready"), 1)

            def q_lo(gi, par, m):
                dve.wait_ge(sem("qhi_ready"), KC * gi + m + 1)
                V_.scalar_tensor_tensor(qT[:, par, 1, m, :], ps[:, WF + m, :], bcol[:, m:m + 1], qT[:, par, 0, m, :],
                                        ALU.add, ALU.subtract).then_inc(sem("qlo_ready"), 1)

            def maxima(gi, n, other=False):
                t, g = n // KC, n % KC
                bank = WT if other and n % 2 else WF
                dve.wait_ge(sem("max_ps"), GT * KC * gi + n + 1)
                V_.tensor_reduce(mx[:, t, g * HG:(g + 1) * HG],
                                 ps[:, bank:bank + 2, 0:4 * NK].rearrange("p a (h k) -> p a h k", k=NK),
                                 AX.X, ALU.max, negate=True).then_inc(sem("max_done"), 1)

            def attend(gi, g):
                dve.wait_ge(sem("pv_ps"), NPB + NSLOT * gi + NC5 * (g + 1))
                pv = [ps[:, PV0 + u, 0:2 * HG * VW].rearrange("p (t h v) -> p t h v", t=2, v=VW) for u in range(2)]
                dve.wait_ge(sem("pv_free"), 2 + 4 * gi + 2 * g)
                for u in range(2):
                    ins = V_.reciprocal(rec[:, u], pv[u][:, :, :, HD])
                link(ins)
                for u in range(2):
                    dst = cx[:, 2 * u:2 * u + 2, g * P:(g + 1) * P].rearrange("p t (h v) -> p t h v", v=HD)
                    for t in range(2):
                        ins = V_.tensor_tensor(dst[:, t], pv[u][:, t, :, 0:HD],
                                               rec[:, u, t, :].unsqueeze(2).to_broadcast([P, HG, HD]), ALU.mult)
                    ins.then_inc(sem("pv_free"), 1)

            def ctx_hi(gi):
                dve.wait_ge(sem("pv_free"), 4 * gi + 4 + 2)
                V_.tensor_copy(cs[0], cx.rearrange("p t d -> p (t d)")).then_inc(sem("chi_ready"), 1)

            def ctx_lo(gi):
                dve.wait_ge(sem("cT_ps"), 2 * gi + 2)
                V_.tensor_copy(cT[:, 1, :, :], ps[:, WT + 1, :].bitcast(F16).rearrange("p (c n) -> p c n", c=KC)).then_inc(sem("cTlo_ready"), 1)

            def add_out(l, gi, i, u):
                dve.wait_ge(sem("o_ps"), 2 * gi + u + 1)
                dve.wait_ge(sem("xb_ready"), gi + 1)
                xt = X[:, bass.ds(i * GT + 2 * u, 2), :]
                V_.scalar_tensor_tensor(xt, ps[:, WT + u, :].rearrange("p (t d) -> p t d", t=2), gsc[:, GA[l]:GA[l] + 1], xt,
                                        ALU.mult, ALU.add).then_inc(sem("att_out"), 1)

            def router_stats(gi, i):
                dve.wait_ge(sem("att_out"), 2 * gi + 2)
                for t in range(GT):
                    ins = V_.bn_stats(rst[:, t + GT * i, :] if isinstance(i, int) else rst[:, bass.ds(i * GT + t, 1), :],
                                      X[:, t + GT * i, :] if isinstance(i, int) else X[:, bass.ds(i * GT + t, 1), :])
                ins.then_inc(sem("rst_ready"), 1)

            def p_lo(gi, par, n):
                rows = ROWS[n % NC5]
                dve.wait_ge(sem("p_ready"), NSLOT * gi + n + 3)
                buf = (NSLOT * par + n) % NPB
                V_.tensor_tensor(PP[0:rows, buf, 1, :], PT[0:rows, n % 2, :], PP[0:rows, buf, 0, :],
                                 ALU.subtract).then_inc(sem("plo_even"), 1)

            def ternary():
                def mean(w):
                    V_.tensor_reduce(wsm[:, w:w + 1], fraw[:, w, :], AX.X, ALU.add, apply_absolute_value=True)

                def sums():
                    dve.wait_ge(sem("fw_in"), 32)
                    mean(0)
                    V_.memset(onef, 1.0)

                def sums_end():
                    V_.tensor_reduce(wsm[:, 1:2], fraw[:, 1, :], AX.X, ALU.add, apply_absolute_value=True).then_inc(sem("w_sums"), 1)

                def means():
                    dve.wait_ge(sem("w_tot"), 1)
                    link(V_.tensor_scalar(wsm[:, 2:4], ps[:, 7, 0:2], 1.0 / (D * M), Q_EPS, ALU.mult, ALU.max))
                    link(V_.reciprocal(wsm[:, 4:6], wsm[:, 2:4]))

                def rounded(w):
                    link(V_.tensor_scalar(fraw[:, w, :], fraw[:, w, :], wsm[:, 4 + w:5 + w], MAGIC, ALU.mult, ALU.add))

                def clipped(w):
                    link(V_.tensor_scalar(fraw[:, w, :], fraw[:, w, :], MAGIC + 1, MAGIC - 1, ALU.min, ALU.max))

                def stored(w):
                    dst = (w1q, w2q)[w].rearrange("p c n -> p (c n)")
                    V_.tensor_scalar(dst, fraw[:, w, :], MAGIC, None, ALU.subtract).then_inc(sem("wq_ready"), 1)
                return {(0, 2): [sums], (0, 3): [sums_end], (0, 6): [means], (0, 7): [lambda: rounded(0)], (0, 8): [lambda: rounded(1)],
                        (1, 0): [lambda: clipped(0)], (1, 1): [lambda: clipped(1)], (1, 2): [lambda: stored(0)], (1, 4): [lambda: stored(1)]}

            def half(l, i, par, front, stats_next, back, extra={}):
                gi = i + NG * l
                at = SLOTS["dve"]
                for n in range(NSLOT):
                    if n % 2 == 0:
                        p_lo(gi, par, n)
                    if front and n == at["x"]:
                        x_lo(gi + 1)
                    for m in range(KC):
                        if front and n == at[f"q{m}"]:
                            q_lo(gi + 1, 1 - par, m)
                    for m in range(GT * KC):
                        if front and n == at["max"][m]:
                            maxima(gi + 1, m)
                    if stats_next and n == at["stats"]:
                        norm_stats(gi + 2, i + 2)
                    if n == at["attend"]:
                        if back:
                            dve.wait_ge(sem("clo_ready"), gi)
                        attend(gi, 0)
                    if back and n == at["c"]:
                        ctx_lo(gi - 1)
                    if back and n == at["out"]:
                        add_out(l, gi - 1, i - 1, 0)
                        add_out(l, gi - 1, i - 1, 1)
                        if l:
                            router_stats(gi - 1, i - 1)
                    if stats_next and n == at["norm"]:
                        norm(gi + 2, i + 2)
                    for job in extra.get((par, n), ()):
                        job()
                attend(gi, 1)
                ctx_hi(gi)

            def batch(l, b, first=False, last=False):
                extra = ternary() if first and l == 0 else {}
                half(l, 2 * b, 0, True, not last, not first, extra)
                half(l, 2 * b + 1, 1, not last, not last, True, extra)

            def attention(l):
                norm_stats(NG * l, 0)
                norm(NG * l, 0)
                prep(l)
                x_lo(NG * l)
                q_lo(NG * l, 0, 0)
                q_lo(NG * l, 0, 1)
                for n in range(KC * GT):
                    maxima(NG * l, n, other=True)
                norm_stats(NG * l + 1, 1)
                norm(NG * l + 1, 1)
                if l == 0:
                    dve.wait_ge(sem("x_in2"), 48)
                batch(l, 0, first=True)
                loop(1, B - 1, 8, lambda b: batch(l, b))
                batch(l, B - 1, last=True)
                gi = NG * (l + 1) - 1
                ctx_lo(gi)
                add_out(l, gi, NG - 1, 0)
                add_out(l, gi, NG - 1, 1)
                if l:
                    router_stats(gi, NG - 1)

            def ffn():
                dve.wait_ge(sem("att_out"), 2 * NG)
                dve.wait_ge(sem("fb_in"), 32)
                link(V_.tensor_scalar(wsm[:, 2:4], wsm[:, 2:4], 1.0 / 127, None, ALU.mult))
                link(V_.tensor_scalar(wsm[:, 3:4], wsm[:, 3:4], gsc[:, 2:3], None, ALU.mult))
                V_.tensor_scalar(fb2c, fb2c, gsc[:, 2:3], None, ALU.mult).then_inc(sem("fb2_ready"), 1)

                def rows(b, t):
                    return X[:, b * TB + t, :] if isinstance(b, int) else X[:, bass.ds(b * TB + t, 1), :]

                def front(b, part):
                    if part == 0:
                        for t in range(TB):
                            ins = V_.bn_stats(fst[:, t, :], rows(b, t))
                        link(ins, hold)
                        for t in range(TB):
                            ins = V_.bn_aggr(fmv[:, t, :], fst[:, t, :])
                        ins.then_inc(sem("fvar_ready"), 1)
                    elif part == 1:
                        dve.wait_ge(sem("frs_ready"), b + 1)
                        after(dve, "xqT_ps", 2 * b)
                        for t in range(TB):
                            ins = V_.tensor_scalar(y8[:, t, :], rows(b, t), fmv[:, t, 0:1], RS_[:, t:t + 1], ALU.subtract, ALU.mult)
                        link(ins)
                    elif part == 2:
                        link(V_.tensor_reduce(AM, y8, AX.X, ALU.max, apply_absolute_value=True))
                        link(V_.tensor_tensor(AM, AM, R2, ALU.mult))
                        link(V_.tensor_scalar(AM, AM, Q_EPS, None, ALU.max))
                        V_.tensor_scalar(DN, AM, wsm[:, 2:3], None, ALU.mult)
                        link(V_.reciprocal(INV, AM))
                        link(V_.scalar_tensor_tensor(SC, INV, 127.0, R2, ALU.mult, ALU.mult))
                    else:
                        for t in range(TB):
                            ins = V_.tensor_scalar(y8[:, t, :], y8[:, t, :], SC[:, t:t + 1], MAGIC_H, ALU.mult, ALU.add)
                        ins.then_inc(sem("z_ready"), 1)
                FRONT_LINKS = 7

                def pre(k, b, t):
                    dve.wait_ge(sem("h_ps"), k + 1)
                    after(dve, "gl_ready", k - 1)
                    h = HBD[t % 2]
                    V_.scalar_tensor_tensor(hpre[:, t % 2, :].rearrange("p (a n) -> p a n", a=2), ps[:, h:h + 2, :], D1[:, t:t + 1],
                                            fb1c.rearrange("p (a n) -> p a n", a=2), ALU.mult, ALU.add).then_inc(sem("hpre_ready"), 1)

                def small(k, t):
                    c = slice(t % 4, t % 4 + 1)
                    dve.wait_ge(sem("gl_ready"), k + 1)
                    link(V_.tensor_reduce(A2[:, c], gl[:, t % 4, :], AX.X, ALU.max, apply_absolute_value=True))
                    dve.wait_ge(sem("rr_ready"), k + 1)
                    link(V_.tensor_scalar(A2[:, c], A2[:, c], RR[:, c], Q_EPS, ALU.mult, ALU.max))
                    V_.tensor_scalar(D2[:, c], A2[:, c], wsm[:, 3:4], None, ALU.mult)
                    link(V_.reciprocal(IV2[:, c], A2[:, c]))
                    V_.tensor_scalar(S2[:, c], IV2[:, c], 127.0, RR[:, c], ALU.mult, ALU.mult).then_inc(sem("s2_ready"), 1)

                def hqt_copy(k, t):
                    dve.wait_ge(sem("hqT_ps"), k + 1)
                    V_.tensor_scalar(hqT[:, t % 2, :, :], ps[:, 6, :].bitcast(F16).rearrange("p (c n) -> p c n", c=MC), HALF, None,
                                     ALU.subtract).then_inc(sem("hqT_ready"), 1)

                def add(k, t, b):
                    dve.wait_ge(sem("xb2_ready"), b + 1)
                    dve.wait_ge(sem("y_ps"), k + 1)
                    xt = X[:, bass.ds(k, 1), :].rearrange("p a d -> p (a d)")
                    V_.scalar_tensor_tensor(xt, ps[:, (7, 0)[t % 2], 0:D], D2[:, t % 4:t % 4 + 1], xt, ALU.mult, ALU.add).then_inc(sem("ffn_out"), 1)
                HBD = (2, 4)

                def batch(b, first=False, last=False):
                    link(V_.tensor_copy(D1, DN))
                    for t in range(TB):
                        k = TB * b + t
                        pre(k, b, t)
                        if not first or t >= 1:
                            small(k - 1, (t - 1) % TB)
                        if not first or t >= 2:
                            hqt_copy(k - 2, (t - 2) % TB)
                        if not first or t >= 3:
                            add(k - 3, (t - 3) % TB, b if t >= 3 else b - 1)
                        if not last and t in (0, 2, 3, 4):
                            front(b + 1, (0, 2, 3, 4).index(t))
                dve.sem_inc(sem("hpre_ready"), 2)
                dve.sem_inc(sem("hqT_ready"), 1)
                for part in range(4):
                    front(0, part)
                batch(0, first=True)
                loop(1, B - 1, 1 + 3 * TB + FRONT_LINKS, lambda b: batch(b))
                batch(B - 1, last=True)
                small(NT - 1, TB - 1)
                hqt_copy(NT - 2, TB - 2)
                add(NT - 3, TB - 3, B - 1)
                hqt_copy(NT - 1, TB - 1)
                add(NT - 2, TB - 2, B - 1)
                add(NT - 1, TB - 1, B - 1)


            def router():
                dve.wait_ge(sem("att_out"), 4 * NG)
                dve.wait_ge(sem("wr_in"), 16)
                link(V_.tensor_scalar(wrr, wrr, WS, None, ALU.mult))
                link(V_.tensor_copy(wrs[:, 0], wrr))
                V_.tensor_tensor(wrs[:, 1], wrr, wrs[:, 0], ALU.subtract).then_inc(sem("wr_split"), 1)

                dve.wait_ge(sem("rst_ready"), NG)
                for t in range(NT):
                    ins = V_.bn_aggr(rmv[:, t, :], rst[:, t, :])
                ins.then_inc(sem("rvar_ready"), 1)
                dve.wait_ge(sem("rrs_ready"), 1)

                def rows(g, par, r, between=lambda: None):
                    after(dve, "rlo_ready", g)
                    for t in range(GT):
                        ins = V_.tensor_scalar(rxn[:, t, :], X[:, bass.ds(g * GT + t, 1), :].rearrange("p a d -> p (a d)"),
                                               rmv[:, bass.ds(g * GT + t, 1), 0:1].rearrange("p a d -> p (a d)"), rrs[:, bass.ds(g * GT + t, 1)],
                                               ALU.subtract, ALU.mult)
                    ins.then_inc(sem("rxn_ready"), 1)
                    between()
                    dve.wait_ge(sem("rxn_ready"), g + 1)
                    dve.wait_ge(sem(("rows_even", "rows_odd")[par]), 16 * (r + 1))
                    V_.tensor_copy(xr[:, par, :, 0:D], rxn).then_inc(sem("rhi_ready"), 1)
                    dve.wait_ge(sem("rhi_ready"), g + 1)
                    V_.tensor_tensor(xr[:, par, :, D:], rxn, xr[:, par, :, 0:D], ALU.subtract).then_inc(sem("rlo_ready"), 1)

                def row_lo_t(g):
                    dve.wait_ge(sem("rT_ps"), 2 * g + 2)
                    V_.tensor_copy(xrT[:, 1], ps[:, 7, :].bitcast(F16).rearrange("p (c n) -> p c n", c=KC)).then_inc(sem("rTlo_ready"), 1)

                def logits(g):
                    dve.wait_ge(sem("lg_ps"), g + 1)
                    V_.tensor_scalar(lg[:, bass.ds(g * GT, GT), :], ps[:, 5, 0:GT * E].rearrange("p (t e) -> p t e", e=E), 1.0 / WS, None,
                                     ALU.mult).then_inc(sem("lg_ready"), 1)
                rows(0, 0, 0)
                with dve.Fori(0, NG // 2 - 1) as r:
                    r = dve.snap(r)
                    rows(2 * r + 1, 1, r, lambda: row_lo_t(2 * r))
                    logits(2 * r)
                    rows(2 * r + 2, 0, r + 1, lambda: row_lo_t(2 * r + 1))
                    logits(2 * r + 1)
                rows(NG - 1, 1, NG // 2 - 1, lambda: row_lo_t(NG - 2))
                logits(NG - 2)
                row_lo_t(NG - 1)
                logits(NG - 1)

            def tiles(ap):
                return ap.unsqueeze(1).to_broadcast([P, NT, E])

            def choices(ap):
                return ap.unsqueeze(2).to_broadcast([P, NT, E])

            def whole(ap):
                link(V_.tensor_scalar(ap, ap, MAGIC, None, ALU.add))
                link(V_.tensor_scalar(ap, ap, MAGIC, None, ALU.subtract))

            def dispatch():
                link(V_.tensor_scalar(desc, iota[:, 0:E], -1.0, float(E), ALU.mult, ALU.add))
                dve.wait_ge(sem("lg_ready"), NG + 1)
                for k in range(TOPK):
                    link(V_.tensor_reduce(top[:, k], lg, AX.X, ALU.max))
                    link(V_.tensor_tensor(ta, lg, choices(top[:, k]), ALU.is_equal))
                    link(V_.tensor_tensor(ta, ta, tiles(desc), ALU.mult))
                    link(V_.tensor_reduce(top_s, ta, AX.X, ALU.max))
                    link(V_.tensor_tensor(oh[:, k], ta, choices(top_s), ALU.is_equal))
                    if k == 0:
                        link(V_.scalar_tensor_tensor(lg, oh[:, 0], -1e37, lg, ALU.mult, ALU.add))
                V_.tensor_tensor(Mb, oh[:, 0], oh[:, 1], ALU.add).then_inc(sem("m_ready"), 1)
                V_.tensor_tensor(wts[:, 0], top[:, 1], top[:, 0], ALU.subtract).then_inc(sem("tops_ready"), 1)
                dve.wait_ge(sem("exp_ready"), 1)
                link(V_.tensor_scalar(wts[:, 1], wts[:, 0], 1.0, None, ALU.add))
                link(V_.reciprocal(wts[:, 1], wts[:, 1]))
                link(V_.tensor_scalar(wts[:, 1], wts[:, 1], gsc[:, 3:4], None, ALU.mult))
                link(V_.tensor_tensor(wts[:, 2], wts[:, 0], wts[:, 1], ALU.mult))
                link(V_.tensor_tensor(gates, oh[:, 0], choices(wts[:, 1]), ALU.mult))
                link(V_.tensor_tensor(ta, oh[:, 1], choices(wts[:, 2]), ALU.mult))
                V_.tensor_tensor(gates, gates, ta, ALU.add).then_inc(sem("gates_ready"), 1)
                dve.wait_ge(sem("rank_ps"), 1)
                link(V_.tensor_copy(cnt, ps[:, 4, NT * E:(NT + 1) * E]))
                link(V_.tensor_scalar(nb, cnt, 1.0 / ST, 0.5 - 0.5 / ST, ALU.mult, ALU.add))
                whole(nb)
                link(V_.tensor_copy(ce, nb))
                src, dst = ce, ce2
                for step in (1, 2, 4):
                    link(V_.tensor_copy(dst[:, 0:step], src[:, 0:step]))
                    link(V_.tensor_tensor(dst[:, step:E], src[:, step:E], src[:, 0:E - step], ALU.add))
                    src, dst = dst, src
                ends = src
                link(V_.tensor_tensor(base_e, ends, nb, ALU.subtract))
                link(V_.tensor_scalar(base_e, base_e, float(ST), None, ALU.mult))
                link(V_.tensor_tensor(ta, ps[:, 4, 0:NT * E].rearrange("p (t e) -> p t e", e=E), tiles(base_e), ALU.add))
                for k in range(TOPK):
                    link(V_.tensor_tensor(tb, oh[:, k], ta, ALU.mult))
                    link(V_.tensor_reduce(pos[:, k * NT:(k + 1) * NT], tb, AX.X, ALU.add))
                link(V_.tensor_scalar(phi, pos, 1.0 / P, -(0.5 - 0.5 / P), ALU.mult, ALU.add))
                whole(phi)
                ins = V_.scalar_tensor_tensor(pos, phi, -float(P), pos, ALU.mult, ALU.add)
                ins.then_inc(sem("pos_ready"), 1)
                dve.wait_ge(sem("pos_ready"), 1)
                dve.wait_ge(sem("x_out"), 16 * NG)
                for n in range(NPC):
                    dve.wait_ge(sem("onehot_used"), n + 1)
                    V_.tensor_tensor(ohL[n % 2], iota.unsqueeze(1).to_broadcast([P, PC, P]),
                                     pos[:, n * PC:(n + 1) * PC].unsqueeze(2).to_broadcast([P, PC, P]), ALU.is_equal)
                    for i in range(PC):
                        m = n * PC + i
                        ins = V_.tensor_scalar(ohH[n % 2][:, i, :], iota16[:, 0:NSC], phi[:, m:m + 1], code[:, m % NT:m % NT + 1],
                                               ALU.is_equal, ALU.mult)
                    ins.then_inc(sem("onehot_ready"), 1)
                link(V_.tensor_tensor(cmpb, ends.unsqueeze(1).to_broadcast([P, NSP, E]), iota[:, 0:NSP].unsqueeze(2).to_broadcast([P, NSP, E]), ALU.is_le))
                link(V_.tensor_reduce(exf, cmpb, AX.X, ALU.add))
                V_.tensor_scalar(exi, exf, float(E - 1), None, ALU.min).then_inc(sem("ex_ready"), 1)
                dve.wait_ge(sem("onehot_used"), NPC + 2)
                link(V_.tensor_copy(idh, ps[:, 6, 0:NSC]))
                link(V_.tensor_copy(idn, idh.bitcast(U16)))
                link(V_.tensor_scalar(idn, idn, float(CODE0), None, ALU.subtract))
                V_.tensor_scalar(gidx, idn, 0.0, None, ALU.max)
                link(V_.tensor_scalar(idt, idn, 0.0, FAR, ALU.is_lt, ALU.mult))
                link(V_.tensor_tensor(sidx, idn, idt, ALU.add))

            def experts():
                dve.wait_ge(sem("b2_in"), 16)

                def cols(ap, j):
                    return ap[:, bass.ds(2 * j, 2)]

                def rows_t(j, par):
                    dve.wait_ge(sem("xsT_ps"), j + 1)
                    after(dve, "eh_ps", 4 * j - 4)
                    V_.tensor_copy(xsT[:, par], ps[:, 0, :].bitcast(F16).rearrange("p (w c n) -> p w c n", w=2, c=KC)).then_inc(sem("xsT_ready"), 1)

                def take_gates(j, par, e):
                    after(dve, "ey_out", 2 * j - 2)
                    V_.tensor_copy(gcur[:, par].unsqueeze(2), xgf[:, par, :, bass.ds(e + D, 1)]).then_inc(sem("gate_ready"), 1)

                def expert_of(j):
                    return dve.value_load(exi[0:1, j:j + 1] if isinstance(j, int) else exi[0:1, bass.ds(j, 1)], min_val=0, max_val=E - 1)

                def split(j, par):
                    def hi(q):
                        dve.wait_ge(sem("gelu_done"), 4 * j + q + 5)
                        if q == 0:
                            after(dve, "ey_ps", 2 * j)
                        V_.tensor_copy(hid[:, par, 0, q * 512:(q + 1) * 512], gel[:, q, :]).then_inc(sem("hhi_ready"), 1)

                    def lo(q):
                        dve.wait_ge(sem("hhi_ready"), 4 * j + q + 1)
                        V_.tensor_tensor(hid[:, par, 1, q * 512:(q + 1) * 512], gel[:, q, :], hid[:, par, 0, q * 512:(q + 1) * 512],
                                         ALU.subtract).then_inc(sem("hlo_ready"), 1)
                    for q in range(4):
                        hi(q)
                        lo(q)

                def output(j, par, e):
                    for s_ in range(2):
                        dve.wait_ge(sem("ey_ps"), 2 * j + s_ + 3)
                        after(dve, "scattered", 16 * (2 * j + s_ - 3))
                        V_.tensor_copy(si2[:, par, s_:s_ + 1], sidx[:, bass.ds(2 * j + s_, 1)])
                        y = yb[:, par, s_, :]
                        V_.scalar_tensor_tensor(y, ps[:, 5 + s_, 0:D], 1.0 / WS, b2t[:, bass.ds(e, 1), :].rearrange("p a n -> p (a n)"),
                                                ALU.mult, ALU.add).then_inc(sem("ey_done"), 1)
                        dve.wait_ge(sem("ey_done"), 2 * j + s_ + 3)
                        V_.tensor_scalar(y, y, gcur[:, par, s_:s_ + 1], None, ALU.mult).then_inc(sem("ey_out"), 1)
                for j in range(2):
                    V_.tensor_copy(gi2[:, j], cols(gidx, j)).then_inc(sem("gidx_ready"), 1)
                e0 = expert_of(0)
                rows_t(0, 0)
                take_gates(0, 0, e0)
                V_.tensor_copy(gi2[:, 0], cols(gidx, 2)).then_inc(sem("gidx_ready"), 1)
                split(0, 0)
                rows_t(1, 1)
                take_gates(1, 1, expert_of(1))
                V_.tensor_copy(gi2[:, 1], cols(gidx, 3)).then_inc(sem("gidx_ready"), 1)

                def pair(r):
                    for u in range(2):
                        j = 2 * r + u
                        split(j + 1, 1 - u)
                        rows_t(j + 2, u)
                        V_.tensor_copy(gi2[:, u], cols(gidx, j + 4)).then_inc(sem("gidx_ready"), 1)
                        output(j, u, expert_of(j))
                        take_gates(j + 2, u, expert_of(j + 2))
                pair(0)
                with dve.Fori(1, (NST - 1) // 2) as r:
                    pair(dve.snap(r))
                output(NST - 1, (NST - 1) % 2, expert_of(NST - 1))

            dve.sem_inc(sem("rows_even"), 16)
            dve.sem_inc(sem("rows_odd"), 16)
            dve.sem_inc(sem("lg_ready"), 1)
            dve.sem_inc(sem("onehot_used"), 2)
            dve.sem_inc(sem("xsT_ready"), 1)
            dve.sem_inc(sem("ey_done"), 2)
            dve.sem_inc(sem("ey_ps"), 2)
            dve.sem_inc(sem("hlo_ready"), 4)
            dve.sem_inc(sem("pv_free"), 2)
            dve.sem_inc(sem("plo_even"), 1)
            dve.sem_inc(sem("plo_odd"), 1)
            dve.sem_inc(sem("pv_ps"), NPB)
            V_.memset(mhalf[:], -0.5).then_inc(sem("half_set"), 1)
            dve.wait_ge(sem("tanh"), 2)
            link(V_.tensor_scalar(gsc[:, 0:2], gsc[:, 4:6], 1.0 / WS, None, ALU.mult))
            dve.wait_ge(sem("x_in"), 16)
            attention(0)
            ffn()
            attention(1)
            router()
            dispatch()
            experts()

        @block.gpsimd
        def _(pool):
            G = nc.gpsimd
            base = [0, 0]

            def link(ins):
                base[1] += 1
                ins.then_inc(sem("pool_link"), 1)
                hold(pool, "pool_link", base[0] + base[1])

            def loop(lo, hi, links, body):
                start = base[0] + base[1]
                with pool.Fori(lo, hi) as r:
                    r = pool.snap(r)
                    base[0], base[1] = r * links + (start - lo * links), 0
                    body(r)
                    assert base[1] == links, base[1]
                base[0], base[1] = start + (hi - lo) * links, 0

            def prep(l):
                for b in range(B):
                    pool.wait_ge(sem("klo_ready"), KC * (l + 1))
                    for g in range(KC):
                        last = G.tensor_tensor(KB[:, b, 1, g, :].rearrange("p (h k) -> p h k", k=NK),
                                               KT[:, 1, g, b * NK:(b + 1) * NK].unsqueeze(1).to_broadcast([P, HG, NK]),
                                               maskk.unsqueeze(2).to_broadcast([P, HG, NK]), ALU.mult)
                last.then_inc(sem("kb_ready"), 1)

            def rsqrt(gi):
                hold(pool, "var_ready", gi + 1)
                link(G.tensor_scalar(rstd[:, 0:GT], mv[:, 0:GT, 1], LN_EPS, None, ALU.add))
                G.tensor_tensor(rstd[:, 0:GT], rstd[:, 0:GT], mhalf[:, 0:GT], ALU.pow).then_inc(sem("rstd_ready"), 1)

            def x_lo(gi):
                hold(pool, "xhi_ready", gi + 1)
                G.tensor_tensor(xs[1], xn.rearrange("p t d -> p (t d)"), xs[0], ALU.subtract).then_inc(sem("xlo_ready"), 1)

            def c_lo(gi):
                hold(pool, "chi_ready", gi + 1)
                G.tensor_tensor(cs[1], cx.rearrange("p t d -> p (t d)"), cs[0], ALU.subtract).then_inc(sem("clo_ready"), 1)

            def add_bias(gi, i):
                xt = X[:, bass.ds(i * GT, GT), :]
                G.tensor_tensor(xt, xt, gbo.unsqueeze(1).to_broadcast([P, GT, D]), ALU.add).then_inc(sem("xb_ready"), 1)

            def half(l, i, par, stats_next, back):
                gi = i + NG * l
                at = SLOTS["pool"]
                for n in range(NSLOT):
                    if n % 2:
                        rows = ROWS[n % NC5]
                        hold(pool, "p_ready", NSLOT * gi + n + 3)
                        buf = (NSLOT * par + n) % NPB
                        G.tensor_tensor(PP[0:rows, buf, 1, :], PT[0:rows, n % 2, :], PP[0:rows, buf, 0, :],
                                        ALU.subtract).then_inc(sem("plo_odd"), 1)
                    if back and n == at["c"]:
                        c_lo(gi - 1)
                    if stats_next and n == at["rsqrt"]:
                        rsqrt(gi + 2)
                    if back and n == at["bias"]:
                        add_bias(gi - 1, i - 1)
                    if stats_next and n == at["x"]:
                        x_lo(gi + 2)

            def batch(l, b, first=False, last=False):
                half(l, 2 * b, 0, not last, not first)
                half(l, 2 * b + 1, 1, not last, True)

            def attention(l):
                pool.wait_ge(sem("half_set"), 1)
                rsqrt(NG * l)
                x_lo(NG * l)
                prep(l)
                rsqrt(NG * l + 1)
                x_lo(NG * l + 1)
                batch(l, 0, first=True)
                loop(1, B - 1, 2, lambda b: batch(l, b))
                batch(l, B - 1, last=True)
                c_lo(NG * (l + 1) - 1)
                add_bias(NG * (l + 1) - 1, NG - 1)

            def weights_lo(e, ch):
                hold(pool, "whi_done", 4 * e + ch + 1)
                c0 = (ch // 2) * 4 * M + (ch % 2) * M
                hi, lo = (WE[:, e, c:c + M] if isinstance(e, int) else WE[:, bass.ds(e, 1), c:c + M].rearrange("p a n -> p (a n)")
                          for c in (c0, c0 + 2 * M))
                G.tensor_tensor(lo, wstg[:, ch, :], hi, ALU.subtract).then_inc(sem("wlo_done"), 1)

            def ffn():
                pool.wait_ge(sem("fb2_ready"), 1)

                def scales(b):
                    hold(pool, "fvar_ready", b + 1)
                    var = fmv[:, :, 1]
                    link(G.tensor_scalar(VE, var, LN_EPS, None, ALU.add))
                    link(G.tensor_tensor(RS_, VE, mhalf[:], ALU.pow))
                    link(G.tensor_tensor(R2, RS_, RS_, ALU.mult))
                    link(G.tensor_tensor(R2, R2, var, ALU.mult))
                    link(G.tensor_scalar(R2, R2, RMS_EPS, None, ALU.add))
                    G.tensor_tensor(R2, R2, mhalf[:], ALU.pow).then_inc(sem("frs_ready"), 1)

                def bias(b):
                    pool.wait_ge(sem("z_ready"), b + 1)
                    xb = X[:, b * TB:(b + 1) * TB, :] if isinstance(b, int) else X[:, bass.ds(b * TB, TB), :]
                    G.tensor_tensor(xb, xb, fb2c.unsqueeze(1).to_broadcast([P, TB, D]), ALU.add).then_inc(sem("xb2_ready"), 1)

                def hidden_rsqrt(k, t):
                    c = slice(t % 4, t % 4 + 1)
                    hold(pool, "ms_ready", k + 1)
                    link(G.tensor_scalar(RR[:, c], MS[:, c], RMS_EPS, None, ALU.add))
                    G.tensor_tensor(RR[:, c], RR[:, c], mhalf[:, 0:1], ALU.pow).then_inc(sem("rr_ready"), 1)

                def batch(b, first=False, last=False):
                    for t in range(TB):
                        hidden_rsqrt(TB * b + t, t)
                        if not last and t == 1:
                            scales(b + 1)
                        if not last and t == 5:
                            bias(b + 1)
                        if t % 2:
                            weights_lo(b, t // 2)
                scales(0)
                bias(0)
                batch(0, first=True)
                loop(1, B - 1, TB + 5, lambda b: batch(b))
                batch(B - 1, last=True)

            def router():
                pool.wait_ge(sem("rvar_ready"), 1)
                link(G.tensor_scalar(rrs, rmv[:, :, 1], LN_EPS, None, ALU.add))
                G.tensor_tensor(rrs, rrs, mhalf[:, 0:1].to_broadcast([P, NT]), ALU.pow).then_inc(sem("rrs_ready"), 1)
                with pool.Fori(E - LATE, E) as e:
                    e = pool.snap(e)
                    for ch in range(4):
                        weights_lo(e, ch)

            def experts():
                def gather(j, par):
                    hold(pool, "gidx_ready", j + 1)
                    hold(pool, "xsT_ps", j - 1)
                    hold(pool, "gate_ready", j - 1)
                    for s_ in range(2):
                        G.indirect_dma_start(xg_[:, par, s_, :].bitcast(U16), None, rowsd, bass.IndirectOffsetOnAxis(ap=gi2[:, par, s_:s_ + 1], axis=0)
                                             ).then_inc(sem(("gathered_even", "gathered_odd")[par]), 16)

                def scatter(j, par):
                    for s_ in range(2):
                        n = 2 * j + s_
                        hold(pool, "ey_out", n + 1)
                        hold(pool, "scattered", 16 * n)
                        G.indirect_dma_start(out, bass.IndirectOffsetOnAxis(ap=si2[:, par, s_:s_ + 1], axis=0), yb[:, par, s_, :], None,
                                             bounds_check=B * S - 1, oob_is_err=False, compute_op=ALU.add).then_inc(sem("scattered"), 16)
                pool.wait_ge(sem("rows_even"), 16 * (NG // 2 + 1))
                pool.wait_ge(sem("rows_odd"), 16 * (NG // 2 + 1))
                pool.wait_ge(sem("gates_out"), 16)
                pool.wait_ge(sem("x_out"), 16 * NG)
                gather(0, 0)
                gather(1, 1)
                gather(2, 0)

                def pair(r):
                    for u in range(2):
                        gather(2 * r + u + 3, 1 - u)
                        scatter(2 * r + u, u)
                pair(0)
                with pool.Fori(1, (NST - 1) // 2) as r:
                    pair(pool.snap(r))
                scatter(NST - 1, (NST - 1) % 2)
            pool.sem_inc(sem("wlo_done"), 4)
            pool.wait_ge(sem("c_in"), 96)
            attention(0)
            ffn()
            attention(1)
            router()
            experts()


def constants():
    p = np.arange(P)
    c32 = np.zeros((P, C_END), np.float32)
    c32[:, C_MASKK:C_MASKK + HG] = p[:, None] // HD == np.arange(HG)
    for c in range(NC5):
        for j in range(3):
            own = (P * c + p) // NK == HEAD0[c] + j
            c32[:, C_MASKV + 6 * c + j] = c32[:, C_MASKV + 6 * c + 3 + j] = own
            c32[:, C_ONE + 6 * c + j] = own
    ids = CODE0 + np.arange(NT) * P + p[:, None]
    c32[:, C_CODE:C_CODE + NT] = ids.astype(np.uint16).view(np.float16)
    c32[:, C_IOTA:] = np.arange(P)
    one_f, one_b = 0x3C00, 0x3F80
    c16 = np.zeros((P, H_END), np.uint16)
    c16[:, H_IDF:H_IDF + P] = np.eye(P) * one_f
    c16[:, H_IDB:H_IDB + P] = np.eye(P) * one_b
    c16[:, H_UP:H_UP + P] = (p[:, None] < p) * one_b
    c16[:, H_ONES:H_IOTA] = one_b
    c16[:, H_IOTA:] = np.arange(P).astype(np.float16).view(np.uint16)
    ind = (np.arange(H)[:, None] == np.arange(KC * FK) // NK) * one_b
    selk = (p[:, None] == np.arange(FK) % NK) * one_f
    return c32, c16, ind.astype(np.uint16), selk.astype(np.uint16)


def kernel(**inputs):
    import concourse.bacc as _bacc
    from concourse.bass_utils import run_bass_kernel_spmd as _run
    a = {k: np.asarray(v) for k, v in inputs.items()}
    c = np.ascontiguousarray
    zero = np.zeros(D, np.float32)
    L1 = {k: a[f"L1_xattn_{k}"] for k in ("Wq", "Wk", "Wv", "Wo", "bq", "bk", "bv", "bo")}
    bcol = [np.stack([q.reshape(KC, P), k.reshape(KC, P)]).reshape(2 * KC, P).T
            for q, k in ((zero, zero), (L1["bq"], L1["bk"]))]
    c32, c16, ind, selk = constants()
    arrays = {
        "x": c(a["x"]),
        "ctxT": c(a["ctx_1024"].reshape(B * NK, D).T),
        "g_att": c(a["g_xattn"]), "g_ffn": c(a["g_ffn"]),
        "attn_w": np.stack([np.stack([a[f"L0_xattn_{w}"] for w in ("Wq", "Wk", "Wv", "Wo")]),
                            np.stack([L1[w].T for w in ("Wq", "Wk", "Wv", "Wo")])]),
        "attn_bcol": c(np.stack(bcol)),
        "attn_brow": np.stack([np.stack([zero, a["L0_xattn_bo"]]), np.stack([L1["bv"], L1["bo"]])]),
        "fw1": c(a["L0_ffn_w1"].T), "fb1": c(a["L0_ffn_b1"]),
        "fw2": c(a["L0_ffn_w2"].T), "fb2": c(a["L0_ffn_b2"]),
        "wr": c(a["L1_ffn_Wr"].T),
        "ew1": c(a["L1_ffn_W1"].transpose(0, 2, 1)),
        "eb1": c(a["L1_ffn_b1"].reshape(E, MC, P).transpose(2, 0, 1).reshape(P, E * MC)),
        "ew2": c(a["L1_ffn_W2"].transpose(0, 2, 1)),
        "eb2": c(a["L1_ffn_b2"]),
        "c32": c32, "c16": c16, "ind": ind, "selk": selk,
    }
    nc = _bacc.Bacc("TRN2", target_bir_lowering=False, num_devices=1)
    args = {k: nc.dram_tensor(k, v.shape, mybir.dt.from_np(v.dtype), kind="ExternalInput").ap() for k, v in arrays.items()}
    args["out"] = nc.dram_tensor("out", (B * S, D), F32, kind="ExternalOutput").ap()
    build(nc, **args)
    r = _run(nc, [arrays], core_ids=[0])
    return r.results[0]["out"].reshape(B, S, D)
```

```python
import numpy as np
import concourse.bass as bass
from concourse import mybir
from contextlib import ExitStack

F32, F16, BF16 = mybir.dt.float32, mybir.dt.float16, mybir.dt.bfloat16
I32, U16 = mybir.dt.int32, mybir.dt.uint16
ACT, ALU, AX = mybir.ActivationFunctionType, mybir.AluOpType, mybir.AxisListType

P = 128
B, S, D = 4, 1024, 256
NT = B * S // P
TB = S // P
GT = 4
GN = GT * P
NG = NT // GT
KC = D // P
H, HD, NK = 16, 16, 77
HG = P // HD
FK = HG * NK
NC5 = -(-FK // P)
ROWS = [min(P, FK - P * c) for c in range(NC5)]
HEAD0 = [min(P * c // NK, HG - 3) for c in range(NC5)]
VW = HD + 1
M = 1024
MC = M // P
E, TOPK = 8, 2
ST = 256
NST = (B * S * TOPK + E * (ST - 1)) // ST
NSP = NST + 3
NSC = NSP * ST // P
ROWW = 2 * D + 2 * E
WS = 32.0
MAGIC = 1.5 * 2.0 ** 23
HALF, MAGIC_H = 1536.0, MAGIC + 0x6600
LN_EPS, RMS_EPS, Q_EPS = 1e-5, 1e-6, 1e-5
NPB = 4
LATE = 4
CODE0 = 0x0400
NPC = 4
PC = TOPK * NT // NPC
FAR = 65536.0

C_MASKK, C_MASKV, C_ONE = 0, HG, HG + 6 * NC5
C_CODE, C_IOTA, C_END = HG + 12 * NC5, HG + 12 * NC5 + NT, HG + 12 * NC5 + NT + P
H_IDF, H_IDB, H_UP, H_ONES, H_END = 0, P, 2 * P, 3 * P, 4 * P


LAGS = {"small": 1, "multiple": 1, "transpose": 3, "evacuate": 3, "project": 4, "add": 4}
SLOTS = {
    "pe": {"xh": 0, "xl": 0, "q0": 1, "q1": 1, "max": (5, 6, 7, 8, 9, 10, 11, 12), "mt": 16, "ch": 10, "cl": 11, "p0": 14, "p1": 16},
    "act": {"x": 0, "q0": 2, "q1": 2, "c": 7, "mt": 9},
    "dve": {"x": 1, "q0": 3, "q1": 3, "max": (3, 3, 3, 4, 4, 5, 6, 7), "stats": 1, "attend": 4, "c": 6, "out": 9, "norm": 6},
    "pool": {"c": 4, "rsqrt": 4, "bias": 5, "x": 7, "lo": (0, 1, 2, 3, 5, 7, 9)},
}


def build(nc, x, ctxT, g_att, g_ffn, attn_w, attn_bcol, attn_brow, fw1, fb1, fw2, fb2,
          wr, ew1, eb1, ew2, eb2, c32, c16, ind, selk, out):
    es = ExitStack()
    with es:
        def sb(name, shape, dt):
            return es.enter_context(nc.sbuf_tensor(name, shape, dt))

        sems = {}

        def sem(name):
            if name not in sems:
                sems[name] = es.enter_context(nc.semaphore(name))
            return sems[name]

        def after(engine, name, value):
            if not isinstance(value, int) or value > 0:
                engine.wait_ge(sem(name), value)

        def hold(engine, name, value):
            after(engine, name, value)
            if not isinstance(value, int):
                engine.sem_inc(sem("carrier"), 1)

        X = sb("X", [P, NT, D], F32)
        WE = sb("WE", [P, E, 8 * M], F16)
        k32 = sb("k32", [P, C_END], F32)
        k16 = sb("k16", [P, H_END], U16)
        indt = sb("indt", [16, KC * FK], U16)
        gsc = sb("gsc", [P, 8], F32)
        gsr = sb("gsr", [P, 4], F32)
        b1t = sb("b1t", [P, E * MC], F32)
        mhalf = sb("mhalf", [P, 8], F32)
        warm = sb("warm", [P, 1], F32)
        bcol = sb("bcol", [P, 4], F32)[:, :]
        AREA = 10900
        late = WE[:, E - LATE:E, :].rearrange("p e n -> p (e n)").bitcast(F32)
        area = sb("area", [P, AREA], F32)

        class Arena:
            def __init__(self):
                self.a, self.l = 0, 0

            def take(self, shape, dt=F32, parts=P):
                n = int(np.prod(shape)) * (2 if dt in (F16, BF16, U16) else 4) // 4
                if self.l + n <= LATE * 4 * M:
                    ap, self.l = late[0:parts, self.l:self.l + n], self.l + n
                else:
                    assert self.a + n <= AREA, (self.a, n)
                    ap, self.a = area[0:parts, self.a:self.a + n], self.a + n
                if dt != F32:
                    ap = ap.bitcast(dt)
                if len(shape) == 1:
                    return ap
                names = "abcdef"[:len(shape)]
                pat = f"p ({' '.join(names)}) -> p {' '.join(names)}"
                return ap.rearrange(pat, **dict(zip(names[1:], shape[1:])))

        ps = es.enter_context(nc.psum_tensor("ps", [P, 8, 512], F32))
        idf = k16[:, H_IDF:H_IDF + P].bitcast(F16)
        idb = k16[:, H_IDB:H_IDB + P].bitcast(BF16)
        upper = k16[:, H_UP:H_UP + P].bitcast(BF16)
        onesb = k16[:, H_ONES:H_ONES + P].bitcast(BF16)
        indb = indt[:, :].bitcast(BF16).rearrange("h (g n) -> h g n", g=KC)
        maskk = k32[:, C_MASKK:C_MASKK + HG]
        maskv = k32[:, C_MASKV:C_MASKV + 6 * NC5]
        maskone = k32[:, C_ONE:C_ONE + 6 * NC5]
        code = k32[:, C_CODE:C_CODE + NT]
        iota = k32[:, C_IOTA:C_IOTA + P]
        GA = [0, 1]
        GF = [2, 3]
        GX = [4, 5]

        ar = Arena()
        KB = ar.take([B, 2, KC, FK], F16)
        V = ar.take([B, KC * NC5, 6 * VW], F16)
        WQ = ar.take([2, KC, D], F16)
        WO = ar.take([2, KC, D], F16)
        gbo = ar.take([D])
        xn = ar.take([GT, D])
        stats = ar.take([TB, 6])
        mv = ar.take([TB, 2])
        rstd = ar.take([TB])
        xs = [ar.take([GT * D], F16) for _ in range(2)]
        xT = ar.take([2, KC, GN], F16)
        work0 = (ar.a, ar.l)
        qT = ar.take([2, 2, KC, GN], F16)
        mx = ar.take([GT, H], BF16)
        mxT = ar.take([2, GN], BF16, 16)
        PT = ar.take([2, GN])
        PP = ar.take([NPB, 2, GN], F16)
        cx = ar.take([GT, D])
        cs = [ar.take([GT * D], F16) for _ in range(2)]
        cT = ar.take([2, KC, GN], F16)
        rec = ar.take([2, 2, HG])
        pr = Arena()
        pr0 = pr.l = work0[1]
        pr.a = 10 * M + 8 + P
        wraw = pr.take([4, KC, D])
        sel = pr.take([FK], F16)
        vs = pr.take([B, 2, D], F16)
        cxt = pr.take([KC, B * NK])
        KT = pr.take([2, KC, B * NK], F16)
        bvr = pr.take([D], F32, 1)
        one1 = pr.take([P], F32, 1)
        bosr = pr.take([D])

        fr = Arena()
        wstg = area[:, 0:4 * M].rearrange("p (c n) -> p c n", c=4)
        fw = Arena()
        fw.l, fw.a = LATE * 4 * M, 4 * M
        fraw = fw.take([2, KC * M])
        w1q = fw.take([KC, M], F16)
        w2q = fw.take([MC, D], F16)
        wsm = fw.take([8])
        onef = fw.take([P])
        assert ar.a <= 4 * M and fw.a == 10 * M + 8 + P
        fx = Arena()
        fx.l, fx.a = fw.l, 4 * M
        y8 = fx.take([TB, D])
        fst = fx.take([TB, 6])
        fmv = fx.take([TB, 2])
        fsm = fx.take([8, TB])
        fb1c = fr.take([M])
        fb2c = fr.take([D])
        xqT = fr.take([KC, TB * P], F16)
        hpre = fr.take([2, M])
        gl = fr.take([4, M])
        hqT = fr.take([2, MC, P], F16)
        RS_, VE, R2, AM, INV, SC, DN, D1 = (fsm[:, k, :] for k in range(8))
        tsm = fr.take([8, 4])
        MS, RR, A2, IV2, S2, D2 = (tsm[:, k, :] for k in range(6))
        assert fx.a <= 8 * M and fr.a == 0 and fr.l <= pr0
        fsq = fr.take([M], BF16)

        ra = Arena()
        ra.l = LATE * 4 * M
        ra.a = 4 * M
        xr = ra.take([2, GT, 2 * D], F16)
        xrT = ra.take([2, KC, GN], F16)
        xsT0 = ra.a
        xsT = ra.take([2, 2, KC, ST], F16)
        rxn = area[:, xsT0:xsT0 + GT * D].rearrange("p (t d) -> p t d", t=GT)
        rst = area[:, xsT0 - NT * 6:xsT0].rearrange("p (t s) -> p t s", s=6)
        rmv, rrs = ra.take([NT, 2]), ra.take([NT])
        wrr = ra.take([KC, E])
        wrs = ra.take([2, KC, E], F16)
        lg = ra.take([NT, E])
        oh = ra.take([TOPK, NT, E])
        ta, tb = ra.take([NT, E]), ra.take([NT, E])
        gates = ra.take([NT, E])
        Mb = ra.take([NT, E], BF16)
        desc = ra.take([E])
        top, top_s = ra.take([TOPK, NT]), ra.take([NT])
        wts = ra.take([3, NT])
        pos, phi = ra.take([TOPK * NT]), ra.take([TOPK * NT])
        cnt, nb, base_e = (ra.take([E]) for _ in range(3))
        ce, ce2 = ra.take([E]), ra.take([E])
        idh = ra.take([NSC], F16)
        idn, idt = ra.take([NSC]), ra.take([NSC])
        gidx, sidx = ra.take([NSC]).bitcast(I32), ra.take([NSC]).bitcast(I32)
        exf, exi = ra.take([NSP]), ra.take([NSP]).bitcast(I32)
        gather_now, scatter_now = ra.take([2, 2]).bitcast(I32), ra.take([2, 2]).bitcast(I32)
        gcur = ra.take([2, 2])
        xgat = area[:, 4 * M:4 * M + 2 * 2 * (ROWW // 2)].bitcast(F16).rearrange("p (a s n) -> p a s n", a=2, s=2)
        xgf = area[:, 4 * M:4 * M + 2 * 2 * (ROWW // 2)].rearrange("p (a s n) -> p a s n", a=2, s=2)
        yb = area[:, 0:4 * D].rearrange("p (a s n) -> p a s n", a=2, s=2)
        xall = X[:].rearrange("p t d -> p (t d)")
        hid = xall[:, 0:4096].bitcast(F16).rearrange("p (a w n) -> p a w n", a=2, w=2)
        gel = xall[:, 4096:6144].rearrange("p (q n) -> p q n", q=4)
        b2t = xall[:, 6144:8192].rearrange("p (e n) -> p e n", e=E)
        ohL = [xall[:, b * 1024:(b + 1) * 1024].bitcast(F16).rearrange("p (i n) -> p i n", i=PC) for b in range(2)]
        ohH = [xall[:, 2048 + b * 1024:2048 + b * 1024 + PC * NSC // 2].bitcast(F16).rearrange("p (i n) -> p i n", i=PC) for b in range(2)]
        cmpb = xall[:, 4096:4096 + NSP * E].rearrange("p (j e) -> p j e", e=E)
        rowsd = nc.dram_tensor("rows", (B * S, ROWW), U16, kind="Internal").ap()

        def low_halves(ap):
            return ap.bitcast(F16).rearrange("p (n two) -> p n two", two=2)[:, :, 0]

        block = es.enter_context(nc.Block())
        S0, PV0, WF, WT = 0, 2, 4, 6

        def due(t, lag, first):
            return (t >= lag or not first) and t - TB < lag

        NSLOT = KC * NC5
        assert LATE == B and E == 2 * LATE and NG == 2 * LATE

        def lo_split(n):
            on_pool = SLOTS["pool"]["lo"]
            mine = [m for m in range(NSLOT) if (m in on_pool) == (n in on_pool)]
            return "plo_pool" if n in on_pool else "plo_dve", len(mine), mine.index(n) + 1

        def load_weights(engine, e, ch):
            w = (ew1, ew2)[ch // 2]
            w = w[e, :, :] if isinstance(e, int) else w[bass.ds(e, 1), :, :].rearrange("a k n -> (a k) n")
            dst = wstg[:, ch, :] if ch < 2 else wstg[:, ch, :].rearrange("p (c n) -> p c n", c=4)
            src = w[ch * P:(ch + 1) * P, :] if ch < 2 else w[(ch - 2) * 4 * P:(ch - 1) * 4 * P, :].rearrange("(c p) n -> p c n", p=P)
            engine.wait_ge(sem("wlo_done"), 4 * e + ch + 1)
            engine.dma_start(dst, src).then_inc(sem(f"w_in{ch}"), 16)

        @block.sync
        def _(sp):
            def layer_loads(l):
                w = attn_w[l].rearrange("w (c p) n -> p w c n", p=P)
                sp.dma_start(cxt, ctxT.rearrange("(c p) n -> p c n", p=P)).then_inc(sem("kv_in"), 16)
                sp.dma_start(wraw[:, 1:3], w[:, 1:3]).then_inc(sem("kv_in"), 16)
                sp.dma_start(bvr, attn_brow[l, 0:1, :]).then_inc(sem("kv_in"), 16)
                sp.dma_start(bcol, attn_bcol[l]).then_inc(sem("kv_in"), 16)
                if l == 0:
                    sp.dma_start(X[:, 0:GT, :], x[0, 0:GN].rearrange("(t p) d -> p t d", p=P)).then_inc(sem("x_in"), 16)
                    sp.dma_start(k32[:], c32).then_inc(sem("c_in"), 16)
                    sp.dma_start(k16[:], c16).then_inc(sem("c_in"), 16)
                    sp.dma_start(indt[:], ind).then_inc(sem("c_in"), 16)
                    sp.dma_start(gsr[:, 0:2], g_att.partition_broadcast(P)).then_inc(sem("c_in"), 16)
                    sp.dma_start(gsr[:, 2:4], g_ffn.partition_broadcast(P)).then_inc(sem("c_in"), 16)
                    sp.dma_start(b1t[:], eb1).then_inc(sem("c_in"), 16)
                sp.dma_start(wraw[:, 0], w[:, 0]).then_inc(sem("prep_in"), 16)
                sp.dma_start(wraw[:, 3], w[:, 3]).then_inc(sem("prep_in"), 16)
                sp.dma_start(sel, selk.bitcast(F16)).then_inc(sem("prep_in"), 16)
                sp.dma_start(bosr, attn_brow[l, 1, :].partition_broadcast(P)).then_inc(sem("prep_in"), 16)
            layer_loads(0)
            sp.dma_start(X[:, GT:TB, :], x[0, GN:].rearrange("(t p) d -> p t d", p=P)).then_inc(sem("x_in1"), 16)
            for b in range(1, B):
                sp.dma_start(X[:, b * TB:(b + 1) * TB, :], x[b].rearrange("(t p) d -> p t d", p=P)).then_inc(sem("x_in2"), 16)
            sp.dma_start(fraw[:, 0, :].rearrange("p (c n) -> p c n", c=KC), fw1.rearrange("(c p) n -> p c n", p=P)).then_inc(sem("fw_in"), 16)
            sp.dma_start(fraw[:, 1, :].rearrange("p (c n) -> p c n", c=MC), fw2.rearrange("(c p) n -> p c n", p=P)).then_inc(sem("fw_in"), 16)
            sp.wait_ge(sem("att_out"), 2 * NG)
            sp.dma_start(fb1c, fb1.partition_broadcast(P)).then_inc(sem("fb_in"), 16)
            sp.dma_start(fb2c, fb2.partition_broadcast(P)).then_inc(sem("fb_in"), 16)
            layer_loads(1)
            with sp.Fori(0, E - LATE) as e:
                e = sp.snap(e)
                for ch in range(4):
                    load_weights(sp, e, ch)
            sp.wait_ge(sem("att_out"), 4 * NG)
            sp.dma_start(wrr, wr.rearrange("(c p) e -> p c e", p=P)).then_inc(sem("wr_in"), 16)
            xout = out.rearrange("(t p) d -> p t d", p=P)
            rout = rowsd.rearrange("(t p) n -> p t n", p=P)
            for g in range(NG):
                t = slice(g * GT, (g + 1) * GT)
                sp.wait_ge(sem("rlo_ready"), g + 1)
                sp.dma_start(rout[:, t, 0:2 * D], xr[:, g % 2].bitcast(U16)).then_inc(sem(("rows_even", "rows_odd")[g % 2]), 16)
                sp.dma_start(xout[:, t, :], X[:, t, :]).then_inc(sem("x_out"), 16)
            sp.wait_ge(sem("gates_ready"), 1)
            sp.dma_start(rout[:, :, 2 * D:], gates.rearrange("p t e -> p (t e)").bitcast(U16).rearrange("p (t e) -> p t e", t=NT)).then_inc(sem("gates_out"), 16)
            sp.wait_ge(sem("onehot_used"), NPC + 2)
            sp.wait_ge(sem("x_out"), 16 * NG)
            sp.dma_start(b2t, eb2.partition_broadcast(P)).then_inc(sem("b2_in"), 16)
            sp.wait_ge(sem("scattered"), 16 * 2 * NST)

        KV_DMAS, PREP_DMAS = 4, 4

        @block.tensor
        def _(pe):
            T = nc.tensor

            def prep(l):
                if l:
                    pe.wait_ge(sem("ffn_out"), NT)
                pe.wait_ge(sem("kv_in"), 16 * KV_DMAS * (l + 1))
                for m in range(KC):
                    for c in range(KC):
                        last = T.matmul(ps[:, m, 0:B * NK], wraw[:, 1, c, m * P:(m + 1) * P], cxt[:, c, :],
                                        start=c == 0, stop=c == KC - 1)
                    last.then_inc(sem("kt_ps"), 1)
                pe.wait_ge(sem("one_set"), l + 1)
                for b in range(B):
                    o = ps[0:NK, 4 + b, 0:D]
                    for k in range(KC):
                        T.matmul(o, cxt[:, k, b * NK:(b + 1) * NK], wraw[:, 2, k, :], start=k == 0, stop=False)
                    T.matmul(o, one1[:, 0:NK], bvr, start=False, stop=True).then_inc(sem("v_ps"), 1)

            def select_values(l):
                pe.wait_ge(sem("prep_in"), 16 * PREP_DMAS * (l + 1))
                for b in range(B):
                    pe.wait_ge(sem("vlo_ready"), B * l + b + 1)
                    pe.wait_ge(sem("klo_ready"), KC * (l + 1))
                    if b >= 2:
                        pe.wait_ge(sem("v_ready"), KC * (B * l + b - 1))
                    for g in range(KC):
                        for c in range(NC5):
                            col = g * P + HD * HEAD0[c]
                            last = T.matmul(ps[0:ROWS[c], 2 * (b % 2) + g, c * 96:(c + 1) * 96].rearrange("p (a n) -> p a n", a=2),
                                            sel[0:NK, c * P:c * P + ROWS[c]], vs[0:NK, b, :, col:col + 48],
                                            start=True, stop=True)
                        last.then_inc(sem("vsel_ps"), 1)

            def transposes(bank, src, rows=GT):
                dst = ps[:, bank, :].bitcast(F16).rearrange("p (c n) -> p c n", c=KC)
                sv = src.rearrange("p (t c n) -> p t c n", t=GT, c=KC)
                for c in range(KC):
                    for t in range(GT):
                        last = T.transpose(dst[:, c, t * P:(t + 1) * P], sv[:, t, c, :], idf)
                return last

            def query_jobs(l, i, b, par, first=False):
                gi = i + NG * l

                def x_hi():
                    pe.wait_ge(sem("xhi_ready"), gi + 1)
                    transposes(WF, xs[0]).then_inc(sem("xT_ps"), 1)

                def x_lo():
                    pe.wait_ge(sem("xlo_ready"), gi + 1)
                    transposes(WF + 1, xs[1]).then_inc(sem("xT_ps"), 1)

                def query(m):
                    pe.wait_ge(sem("xThi_ready"), gi + 1)
                    cols = slice(m * P, (m + 1) * P)
                    T.matmul(ps[:, WF + m, :], WQ[:, 0, 0, cols], xT[:, 0, 0, :], start=True, stop=False)
                    T.matmul(ps[:, WF + m, :], WQ[:, 0, 1, cols], xT[:, 0, 1, :], start=False, stop=False)
                    T.matmul(ps[:, WF + m, :], WQ[:, 1, 0, cols], xT[:, 0, 0, :], start=False, stop=False)
                    T.matmul(ps[:, WF + m, :], WQ[:, 1, 1, cols], xT[:, 0, 1, :], start=False, stop=False)
                    pe.wait_ge(sem("xTlo_ready"), gi + 1)
                    T.matmul(ps[:, WF + m, :], WQ[:, 0, 0, cols], xT[:, 1, 0, :], start=False, stop=False)
                    T.matmul(ps[:, WF + m, :], WQ[:, 0, 1, cols], xT[:, 1, 1, :], start=False, stop=True).then_inc(sem("q_ps"), 1)

                def q0():
                    query(0)

                def q1():
                    query(1)
                    
                def max_scores(n, other=False):
                    base_ = WT if other and n % 2 else WF

                    def run():
                        t, g = n // KC, n % KC
                        if n == 0:
                            pe.wait_ge(sem("qhi_ready"), KC * (gi + 1))
                            pe.wait_ge(sem("qlo_ready"), KC * (gi + 1))
                        else:
                            after(pe, "max_done", GT * KC * gi + n - (1 if other else 0))
                        for h in range(2):
                            last = T.matmul(ps[:, base_ + h, 0:4 * NK], qT[:, par, 0, g, t * P:(t + 1) * P],
                                            KB[:, b, 0, g, h * 4 * NK:(h + 1) * 4 * NK], start=True, stop=True)
                        last.then_inc(sem("max_ps"), 1)
                    return run

                def max_t():
                    pe.wait_ge(sem("max_done"), GT * KC * (gi + 1))
                    dst = ps[0:H, WF, :].bitcast(BF16)
                    for t in range(GT):
                        last = T.transpose(dst[:, t * P:(t + 1) * P], mx[:, t, :], idb)
                    last.then_inc(sem("mxT_ps"), 1)
                return x_hi, x_lo, q0, q1, [max_scores(n, first) for n in range(GT * KC)], max_t

            def out_jobs(l, i):
                gi = i + NG * l

                def c_hi():
                    pe.wait_ge(sem("chi_ready"), gi + 1)
                    transposes(WT, cs[0]).then_inc(sem("cT_ps"), 1)

                def c_lo():
                    pe.wait_ge(sem("clo_ready"), gi + 1)
                    transposes(WT + 1, cs[1]).then_inc(sem("cT_ps"), 1)

                def project(u):
                    pe.wait_ge(sem("cThi_ready"), gi + 1)
                    pe.wait_ge(sem("cTlo_ready"), gi + 1)
                    for v in range(2):
                        t = 2 * u + v
                        o = ps[:, WT + u, v * D:(v + 1) * D]
                        n = 0
                        for a, w in ((0, 0), (0, 1), (1, 0)):
                            for c in range(KC):
                                last = T.matmul(o, cT[:, a, c, t * P:(t + 1) * P], WO[:, w, c, :],
                                                start=n == 0, stop=n == 5)
                                n += 1
                    last.then_inc(sem("o_ps"), 1)
                return c_hi, c_lo, lambda: project(0), lambda: project(1)

            PARTS = ((0, 0), (0, 1), (1, 0))

            def scores(l, i, b, par, n):
                N = NSLOT * (i + NG * l) + n
                g, c = n // NC5, n % NC5
                rows = ROWS[c]
                if n == 0:
                    pe.wait_ge(sem("mxT_ready"), i + NG * l + 1)
                pe.wait_ge(sem("p_ready"), N + 1)
                o = ps[0:rows, S0 + n % 2, :]
                cols = slice(c * P, c * P + rows)
                T.matmul(o, KB[:, b, 0, g, cols], qT[:, par, 0, g, :], start=True, stop=False)
                T.matmul(o, KB[:, b, 1, g, cols], qT[:, par, 0, g, :], start=False, stop=False)
                T.matmul(o, KB[:, b, 0, g, cols], qT[:, par, 1, g, :], start=False, stop=False)
                T.matmul(o, indb[:, g, cols], mxT[:, par, :], start=False, stop=True).then_inc(sem("s_ps"), 1)

            def values(l, i, b, par, n):
                gi = i + NG * l
                N = NSLOT * gi + n
                g, c = n // NC5, n % NC5
                if c == 0:
                    pe.wait_ge(sem("pv_free"), 4 * gi + 2 * g + 2)
                name, of, nth = lo_split(n)
                pe.wait_ge(sem(name), of * (gi + 1) + nth)
                rows, h0 = ROWS[c], HEAD0[c]
                for t in range(GT):
                    o = ps[:, PV0 + t // 2, (t % 2) * HG * VW + h0 * VW:(t % 2) * HG * VW + (h0 + 3) * VW]
                    for m, (a, w) in enumerate(PARTS):
                        last = T.matmul(o, PP[0:rows, (NSLOT * par + n) % NPB, a, t * P:(t + 1) * P], V[0:rows, b, n, w * 3 * VW:(w + 1) * 3 * VW],
                                        start=c == 0 and t % 2 == 0 and m == 0, stop=c == NC5 - 1 and m == 2,
                                        skip_group_check=True)
                last.then_inc(sem("pv_ps"), 1)

            def weight_sums():
                pe.wait_ge(sem("w_sums"), 1)
                T.matmul(ps[:, 7, 0:2], onef, wsm[:, 0:2], start=True, stop=True).then_inc(sem("w_tot"), 1)

            def half(l, i, b, par, before, behind, nxt):
                for n in range(NSLOT):
                    if n + 2 < NSLOT:
                        scores(l, i, b, par, n + 2)
                    for job in before.get(n, ()):
                        job()
                    values(l, i, b, par, n)
                    for job in behind.get(n, ()):
                        job()
                    if n + 2 >= NSLOT and nxt is not None:
                        scores(l, i + 1, nxt, 1 - par, n + 2 - NSLOT)

            def slots(front, back):
                before, behind = {}, {}

                def put(place, job):
                    (behind if place % 2 else before).setdefault(place // 2, []).append(job)
                at = SLOTS["pe"]
                if front:
                    xh, xl, q0, q1, mxs, mt = front
                    put(at["xh"], xh)
                    put(at["xl"], xl)
                    put(at["q0"], q0)
                    put(at["q1"], q1)
                    for n, job in enumerate(mxs):
                        put(at["max"][n], job)
                    put(at["mt"], mt)
                if back:
                    for name, job in zip(("ch", "cl", "p0", "p1"), back):
                        put(at[name], job)
                return before, behind

            def batch(l, b, first=False, last=False):
                before, behind = slots(query_jobs(l, 2 * b + 1, b, 1), None if first else out_jobs(l, 2 * b - 1))
                if first and l == 0:
                    behind.setdefault(5, []).append(weight_sums)
                half(l, 2 * b, b, 0, before, behind, b)
                front = None if last else query_jobs(l, 2 * b + 2, b + 1, 0)
                half(l, 2 * b + 1, b, 1, *slots(front, out_jobs(l, 2 * b)), None if last else b + 1)

            def attention(l):
                prep(l)
                pe.wait_ge(sem("c_in"), 96)
                pe.wait_ge(sem("vlo_ready"), B * (l + 1))
                xh, xl, q0, q1, mxs, mt = query_jobs(l, 0, 0, 0, first=True)
                xh()
                xl()
                pe.wait_ge(sem("wsplit"), 2 * (l + 1))
                q0()
                q1()
                select_values(l)
                pe.wait_ge(sem("kb0_ready"), l + 1)
                for job in (*mxs, mt):
                    job()
                pe.wait_ge(sem("kb_ready"), 3 * (l + 1))
                pe.wait_ge(sem("v_ready"), KC * B * (l + 1))
                scores(l, 0, 0, 0, 0)
                scores(l, 0, 0, 0, 1)
                batch(l, 0, first=True)
                with pe.Fori(1, B - 1) as b:
                    batch(l, pe.snap(b))
                batch(l, B - 1, last=True)
                for job in out_jobs(l, NG - 1):
                    job()
            HB, TQ, YB = (2, 4), 6, (7, 0)

            def ffn():
                pe.wait_ge(sem("wq_ready"), 2)

                def xq_t(b, v):
                    if v == 0:
                        pe.wait_ge(sem("z_ready"), b + 1)
                    else:
                        pe.wait_ge(sem("xqT_ready"), 2 * b + 1)
                    dst = ps[:, 1, :].bitcast(F16).rearrange("p (c n) -> p c n", c=KC)
                    for c in range(KC):
                        for t in range(GT):
                            last = T.transpose(dst[:, c, t * P:(t + 1) * P], low_halves(y8[:, GT * v + t, c * P:(c + 1) * P]), idf)
                    last.then_inc(sem("xqT_ps"), 1)

                def hidden(b, t):
                    if t % GT == 0:
                        pe.wait_ge(sem("xqT_ready"), 2 * b + t // GT + 1)
                    pe.wait_ge(sem("hpre_ready"), TB * b + t + 1)
                    for h in range(2):
                        for c in range(KC):
                            last = T.matmul(ps[:, HB[t % 2] + h, :], xqT[:, c, t * P:(t + 1) * P],
                                            w1q[:, c, h * 512:(h + 1) * 512], start=c == 0, stop=c == KC - 1)
                    last.then_inc(sem("h_ps"), 1)

                def hidden_t(k, t):
                    pe.wait_ge(sem("zz_ready"), k + 1)
                    pe.wait_ge(sem("hqT_ready"), k + 1)
                    dst = ps[:, TQ, :].bitcast(F16)
                    for c in range(MC):
                        last = T.transpose(dst[:, c * P:(c + 1) * P], low_halves(gl[:, t % 4, c * P:(c + 1) * P]), idf)
                    last.then_inc(sem("hqT_ps"), 1)

                def project(k, t):
                    pe.wait_ge(sem("hqT_ready"), k + 2)
                    after(pe, "ffn_out", k - 1)
                    for c in range(MC):
                        last = T.matmul(ps[:, YB[t % 2], 0:D], hqT[:, t % 2, c, :], w2q[:, c, :], start=c == 0, stop=c == MC - 1)
                    last.then_inc(sem("y_ps"), 1)

                def batch(b, first=False, last=False):
                    for t in range(TB):
                        k = TB * b + t
                        hidden(b, t)
                        if t == 0:
                            xq_t(b, 1)
                        if not last and t == TB - 2:
                            xq_t(b + 1, 0)
                        behind(k, t, first)

                def behind(k, t, first=False):
                    for name, job in (("transpose", hidden_t), ("project", project)):
                        lag = LAGS[name]
                        if due(t, lag, first):
                            job(k - lag, (t - lag) % TB)
                xq_t(0, 0)
                batch(0, first=True)
                with pe.Fori(1, B - 1) as b:
                    batch(pe.snap(b))
                batch(B - 1, last=True)
                for n in range(LAGS["project"]):
                    behind(NT + n, TB + n)

            RT, LGB, RK = (6, 7), 5, 4

            def router():
                pe.wait_ge(sem("wr_split"), 1)

                def group(g, par):
                    pe.wait_ge(sem("rlo_ready"), g + 1)
                    for a in range(2):
                        dst = ps[:, RT[a], :].bitcast(F16).rearrange("p (c n) -> p c n", c=KC)
                        for c in range(KC):
                            for t in range(GT):
                                last = T.transpose(dst[:, c, t * P:(t + 1) * P], xr[:, par, t, a * D + c * P:a * D + (c + 1) * P], idf)
                        last.then_inc(sem("rT_ps"), 1)
                    pe.wait_ge(sem("rThi_ready"), g + 1)
                    pe.wait_ge(sem("rTlo_ready"), g + 1)
                    pe.wait_ge(sem("lg_ready"), g + 1)
                    for t in range(GT):
                        n = 0
                        for a, w in ((0, 0), (0, 1), (1, 0)):
                            for c in range(KC):
                                last = T.matmul(ps[:, LGB, t * E:(t + 1) * E], xrT[:, a, c, t * P:(t + 1) * P], wrs[:, w, c, :],
                                                start=n == 0, stop=n == 5)
                                n += 1
                    last.then_inc(sem("lg_ps"), 1)
                with pe.Fori(0, NG // 2) as r:
                    r = pe.snap(r)
                    for u in range(2):
                        group(2 * r + u, u)

            def dispatch():
                pe.wait_ge(sem("m_ready"), 1)
                T.matmul(ps[:, RK, 0:NT * E], upper, Mb.rearrange("p t e -> p (t e)"), start=True, stop=False, skip_group_check=True)
                for t in range(NT):
                    last = T.matmul(ps[:, RK, (t + 1) * E:(NT + 1) * E].rearrange("p (t e) -> p t e", e=E), onesb,
                                    Mb[:, t, :].unsqueeze(1).to_broadcast([P, NT - t, E]), start=False, stop=t == NT - 1, skip_group_check=True)
                last.then_inc(sem("rank_ps"), 1)
                for n in range(NPC):
                    pe.wait_ge(sem("onehot_codes"), n + 1)
                    for i in range(PC):
                        last = T.matmul(ps[:, 6, 0:NSC], ohL[n % 2][:, i, :], ohH[n % 2][:, i, :],
                                        start=n == 0 and i == 0, stop=n == NPC - 1 and i == PC - 1)
                    last.then_inc(sem("onehot_used"), 1)

            XTB, H1, YB2 = 0, 1, (5, 6)

            def experts():
                pe.wait_ge(sem("ex_ready"), 1)
                pe.wait_ge(sem("wlo_done"), 4 * E + 4)

                def expert_of(j):
                    return pe.value_load(exi[0:1, j:j + 1] if isinstance(j, int) else exi[0:1, bass.ds(j, 1)], min_val=0, max_val=E - 1)

                def rows_t(j, par, jh):
                    pe.wait_ge(sem(("gathered_even", "gathered_odd")[par]), 32 * (jh + 1))
                    pe.wait_ge(sem("xsT_ready"), j + 1)
                    dst = ps[:, XTB, :].bitcast(F16).rearrange("p (w c n) -> p w c n", w=2, c=KC)
                    for w in range(2):
                        for c in range(KC):
                            for s_ in range(2):
                                last = T.transpose(dst[:, w, c, s_ * P:(s_ + 1) * P], xgat[:, par, s_, w * D + c * P:w * D + (c + 1) * P], idf)
                    last.then_inc(sem("xsT_ps"), 1)

                def hidden(j, par, e):
                    pe.wait_ge(sem("xsT_ready"), j + 2)
                    for q in range(4):
                        pe.wait_ge(sem("gelu_done"), 4 * j + q + 1)
                        for m in (2 * q, 2 * q + 1):
                            n = 0
                            for a, w in ((0, 0), (1, 0), (0, 1)):
                                for c in range(KC):
                                    lw = WE[:, bass.ds(e, 1), a * 2 * M + c * M + m * P:a * 2 * M + c * M + (m + 1) * P].rearrange("p a n -> p (a n)")
                                    last = T.matmul(ps[:, H1 + q, (m % 2) * ST:(m % 2 + 1) * ST], lw, xsT[:, par, w, c, :],
                                                    start=n == 0, stop=n == 5)
                                    n += 1
                        last.then_inc(sem("eh_ps"), 1)

                def project(j, par, e):
                    for s_ in range(2):
                        pe.wait_ge(sem("ey_done"), 2 * j + s_ + 1)
                        n = 0
                        for m in range(MC):
                            if s_ == 0 and m % 2 == 0:
                                pe.wait_ge(sem("hlo_ready"), 4 * j + m // 2 + 5)
                            for a, w in ((0, 0), (0, 1), (1, 0)):
                                rw = WE[:, bass.ds(e, 1), 4 * M + a * 2 * M + m * D:4 * M + a * 2 * M + (m + 1) * D].rearrange("p a n -> p (a n)")
                                last = T.matmul(ps[:, YB2[s_], 0:D], hid[:, par, w, m * ST + s_ * P:m * ST + (s_ + 1) * P], rw,
                                                start=n == 0, stop=n == 3 * MC - 1)
                                n += 1
                        last.then_inc(sem("ey_ps"), 1)
                rows_t(0, 0, 0)
                hidden(0, 0, expert_of(0))
                rows_t(1, 1, 0)
                with pe.Fori(0, (NST - 1) // 2) as r:
                    r = pe.snap(r)
                    for u in range(2):
                        this, ahead = expert_of(2 * r + u), expert_of(2 * r + u + 1)
                        hidden(2 * r + u + 1, 1 - u, ahead)
                        rows_t(2 * r + u + 2, u, r + 1)
                        project(2 * r + u, u, this)
                project(NST - 1, (NST - 1) % 2, expert_of(NST - 1))
            attention(0)
            ffn()
            attention(1)
            router()
            dispatch()
            experts()

        @block.scalar
        def _(act):
            A = nc.scalar

            def prep(l):
                act.wait_ge(sem("half_set"), 1)
                A.activation(warm[:], mhalf[:, 0:1], ACT.Exp)
                if l:
                    act.wait_ge(sem("ffn_out"), NT)
                act.wait_ge(sem("kv_in"), 16 * KV_DMAS * (l + 1))
                for m in range(KC):
                    act.wait_ge(sem("kt_ps"), KC * l + m + 1)
                    A.activation(KT[:, 0, m, :], ps[:, m, 0:B * NK], ACT.Identity, bias=bcol[:, 2 + m:3 + m]).then_inc(sem("khi_ready"), 1)

                for b in range(B):
                    act.wait_ge(sem("v_ps"), B * l + b + 1)
                    A.copy(vs[0:NK, b, 0, :], ps[0:NK, 4 + b, 0:D]).then_inc(sem("vhi_ready"), 1)
                act.wait_ge(sem("prep_in"), 16 * PREP_DMAS * (l + 1))
                for w, dst in ((0, WQ), (3, WO)):
                    A.mul(dst[:, 0, :, :], wraw[:, w, :, :], WS).then_inc(sem("whi_ready"), 1)

            def late_keys():
                b0 = B // 2
                for g in range(KC):
                    for h in range(HG):
                        last = A.mul(KB[:, b0:, 0, g, h * NK:(h + 1) * NK],
                                     KT[:, 0, g, b0 * NK:].rearrange("p (b k) -> p b k", k=NK), maskk[:, h:h + 1])
                last.then_inc(sem("kb_ready"), 1)

            def half(l, i, par, front, back):
                gi = i + NG * l
                qp = 1 - par

                def exp(n):
                    N = NSLOT * gi + n
                    rows = ROWS[n % NC5]
                    act.wait_ge(sem("s_ps"), N + 1)
                    act.wait_ge(sem("pv_ps"), N + 1)
                    src = ps[0:rows, S0 + n % 2, :]
                    A.activation(PP[0:rows, (NSLOT * par + n) % NPB, 0, :], src, ACT.Exp, scale=HD ** -0.5 / WS)
                    name, of, nth = lo_split((n - 2) % NSLOT)
                    act.wait_ge(sem(name), of * (gi + (n >= 2)) + nth)
                    A.activation(PT[0:rows, n % 2, :], src, ACT.Exp, scale=HD ** -0.5 / WS).then_inc(sem("p_ready"), 1)
                at = SLOTS["act"]
                for n in range(NSLOT):
                    exp(n)
                    if front and n == at["x"]:
                        x_hi(gi + 1)
                    for m in range(KC):
                        if front and n == at[f"q{m}"]:
                            q_hi(gi + 1, qp, m)
                    if back and n == at["c"]:
                        c_hi(gi - 1)
                    if front and n == at["mt"]:
                        m_t(gi + 1, qp)

            def x_hi(gi):
                act.wait_ge(sem("xT_ps"), 2 * gi + 1)
                A.copy(xT[:, 0, :, :], ps[:, WF, :].bitcast(F16).rearrange("p (c n) -> p c n", c=KC)).then_inc(sem("xThi_ready"), 1)

            def q_hi(gi, par, m):
                act.wait_ge(sem("q_ps"), KC * gi + m + 1)
                A.activation(qT[:, par, 0, m, :], ps[:, WF + m, :], ACT.Identity, bias=bcol[:, m:m + 1]).then_inc(sem("qhi_ready"), 1)

            def m_t(gi, par):
                act.wait_ge(sem("mxT_ps"), gi + 1)
                A.copy(mxT[:, par, :], ps[0:H, WF, :].bitcast(BF16)[:, 0:GN]).then_inc(sem("mxT_ready"), 1)

            def c_hi(gi):
                act.wait_ge(sem("cT_ps"), 2 * gi + 1)
                A.copy(cT[:, 0, :, :], ps[:, WT, :].bitcast(F16).rearrange("p (c n) -> p c n", c=KC)).then_inc(sem("cThi_ready"), 1)

            def batch(l, b, first=False, last=False):
                half(l, 2 * b, 0, True, not first)
                half(l, 2 * b + 1, 1, not last, True)

            def attention(l):
                prep(l)
                act.wait_ge(sem("bq_ready"), l + 1)
                g0 = NG * l
                x_hi(g0)
                q_hi(g0, 0, 0)
                q_hi(g0, 0, 1)
                late_keys()
                m_t(g0, 0)
                batch(l, 0, first=True)
                with act.Fori(1, B - 1) as b:
                    batch(l, act.snap(b))
                batch(l, B - 1, last=True)
                c_hi(NG * (l + 1) - 1)
            def ffn():
                def xq_copy(b, v):
                    act.wait_ge(sem("xqT_ps"), 2 * b + v + 1)
                    A.activation(xqT[:, :, v * GN:(v + 1) * GN], ps[:, 1, :].bitcast(F16).rearrange("p (c n) -> p c n", c=KC), ACT.Copy,
                                 bias=-HALF).then_inc(sem("xqT_ready"), 1)

                def gelu(k, t):
                    act.wait_ge(sem("hpre_ready"), k + 3)
                    after(act, "hqT_ps", k - 3)
                    A.activation(gl[:, t % 4, :], hpre[:, t % 2, :], ACT.Gelu).then_inc(sem("gl_ready"), 1)
                    act.wait_ge(sem("gl_ready"), k + 1)
                    A.activation(fsq, gl[:, t % 4, :], ACT.Square, scale=M ** -0.5,
                                 accum_out=MS[:, t % 4:t % 4 + 1]).then_inc(sem("ms_ready"), 1)

                def hidden_t(k, t):
                    act.wait_ge(sem("hqT_ps"), k + 1)
                    A.activation(hqT[:, t % 2, :, :], ps[:, 6, :].bitcast(F16).rearrange("p (c n) -> p c n", c=MC), ACT.Copy,
                                 bias=-HALF).then_inc(sem("hqT_ready"), 1)

                def multiple(k, t):
                    act.wait_ge(sem("s2_ready"), k + 1)
                    g = gl[:, t % 4, :]
                    A.activation(g, g, ACT.Copy, bias=MAGIC_H, scale=S2[:, t % 4:t % 4 + 1]).then_inc(sem("zz_ready"), 1)

                def batch(b, first=False, last=False):
                    for t in range(TB):
                        k = TB * b + t
                        if t == 0:
                            xq_copy(b, 1)
                        if not last and t == TB - 2:
                            xq_copy(b + 1, 0)
                        evacuate(k, t, first)
                        gelu(k, t)
                        multiply(k, t, first)
                        if t % 2 == 0 and (not first or t):
                            split(b if t else b - 1, t // 2 - 1 if t else 3)

                def evacuate(k, t, first=False):
                    lag = LAGS["evacuate"]
                    if due(t, lag, first):
                        hidden_t(k - lag, (t - lag) % TB)

                def multiply(k, t, first=False):
                    lag = LAGS["multiple"]
                    if due(t, lag, first):
                        multiple(k - lag, (t - lag) % TB)
                xq_copy(0, 0)
                batch(0, first=True)
                with act.Fori(1, B - 1) as b:
                    batch(act.snap(b))
                batch(B - 1, last=True)
                split(E - LATE - 1, 3)
                for n in range(LAGS["evacuate"]):
                    evacuate(NT + n, TB + n)
                    multiply(NT + n, TB + n)

            def split(e, ch):
                act.wait_ge(sem("w_scaled"), 4 * e + ch + 1)
                c0 = (ch // 2) * 4 * M + (ch % 2) * M
                A.copy(WE[:, e, c0:c0 + M] if isinstance(e, int) else WE[:, bass.ds(e, 1), c0:c0 + M].rearrange("p a n -> p (a n)"),
                       wstg[:, ch, :]).then_inc(sem("whi_done"), 1)

            def router():
                act.wait_ge(sem("att_out"), 4 * NG)
                e0 = E - LATE
                load_weights(act, e0, 0)
                load_weights(act, e0, 1)

                def expert(e, g, last=False):
                    for ch in range(4):
                        if ch % 2 == 0:
                            act.wait_ge(sem("rT_ps"), 2 * (g + ch // 2) + 1)
                            A.copy(xrT[:, 0], ps[:, 6, :].bitcast(F16).rearrange("p (c n) -> p c n", c=KC)).then_inc(sem("rThi_ready"), 1)
                        if not last or ch < 2:
                            load_weights(act, e + (ch + 2) // 4, (ch + 2) % 4)
                        act.wait_ge(sem(f"w_in{ch}"), 16 * (e + 1))
                        A.mul(wstg[:, ch, :], wstg[:, ch, :], WS).then_inc(sem("w_scaled"), 1)
                        split(e, ch)
                with act.Fori(0, LATE - 1) as r:
                    r = act.snap(r)
                    expert(e0 + r, 2 * r)
                expert(E - 1, NG - 2, last=True)
                act.wait_ge(sem("tops_ready"), 1)
                A.activation(wts[:, 0, :], wts[:, 0, :], ACT.Exp).then_inc(sem("exp_ready"), 1)
                A.activation(warm[:], mhalf[:, 0:1], ACT.Gelu)

            def experts():
                act.wait_ge(sem("ex_ready"), 1)

                def gelu(j):
                    e = act.value_load(exi[0:1, j:j + 1] if isinstance(j, int) else exi[0:1, bass.ds(j, 1)], min_val=0, max_val=E - 1)
                    for q in range(4):
                        act.wait_ge(sem("eh_ps"), 4 * j + q + 1)
                        act.wait_ge(sem("hlo_ready"), 4 * j + q + 1)
                        for v in range(2):
                            last = A.activation(gel[:, q, v * ST:(v + 1) * ST], ps[:, 1 + q, v * ST:(v + 1) * ST], ACT.Gelu,
                                                bias=b1t[:, bass.ds(e * MC + 2 * q + v, 1)], scale=1.0 / WS)
                        last.then_inc(sem("gelu_done"), 1)
                gelu(0)
                with act.Fori(0, (NST - 1) // 2) as r:
                    r = act.snap(r)
                    for u in range(2):
                        gelu(2 * r + u + 1)
            act.sem_inc(sem("gelu_done"), 4)
            act.sem_inc(sem("p_ready"), 2)
            act.wait_ge(sem("c_in"), 96)
            A.activation(gsc[:, 2:4], gsr[:, 2:4], ACT.Tanh).then_inc(sem("tanh"), 1)
            A.activation(gsc[:, 4:6], gsr[:, 0:2], ACT.Tanh).then_inc(sem("tanh"), 1)
            attention(0)
            ffn()
            attention(1)
            router()
            experts()

        @block.vector
        def _(dve):
            V_ = nc.vector
            base = [0, 0]

            def link(ins, wait=after):
                base[1] += 1
                ins.then_inc(sem("dve_link"), 1)
                wait(dve, "dve_link", base[0] + base[1])

            def loop(lo, hi, links, body):
                start = base[0] + base[1]
                with dve.Fori(lo, hi) as r:
                    r = dve.snap(r)
                    base[0], base[1] = r * links + (start - lo * links), 0
                    body(r)
                    assert base[1] == links, base[1]
                base[0], base[1] = start + (hi - lo) * links, 0

            def prep(l):
                dve.wait_ge(sem("kv_in"), 16 * KV_DMAS * (l + 1))
                link(V_.tensor_scalar(bcol[:, 0:KC], bcol[:, 0:KC], WS, None, ALU.mult))
                for m in range(KC):
                    dve.wait_ge(sem("khi_ready"), KC * l + m + 1)
                    ins = V_.scalar_tensor_tensor(KT[:, 1, m, :], ps[:, m, 0:B * NK], bcol[:, 2 + m:3 + m],
                                                  KT[:, 0, m, :], ALU.add, ALU.subtract)
                    ins.then_inc(sem("klo_ready"), 1)
                for b in range(B):
                    dve.wait_ge(sem("vhi_ready"), B * l + b + 1)
                    V_.tensor_tensor(vs[0:NK, b, 1, :], ps[0:NK, 4 + b, 0:D], vs[0:NK, b, 0, :], ALU.subtract).then_inc(sem("vlo_ready"), 1)
                dve.wait_ge(sem("prep_in"), 16 * PREP_DMAS * (l + 1))
                V_.tensor_scalar(gbo, bosr, gsc[:, GX[l]:GX[l] + 1], None, ALU.mult).then_inc(sem("bq_ready"), 1)
                for n, (w, dst) in enumerate(((0, WQ), (3, WO))):
                    dve.wait_ge(sem("whi_ready"), 2 * l + n + 1)
                    V_.scalar_tensor_tensor(dst[:, 1, :, :], wraw[:, w, :, :], WS, dst[:, 0, :, :],
                                            ALU.mult, ALU.subtract).then_inc(sem("wsplit"), 1)
                x_lo(NG * l)
                for b in range(B // 2):
                    for g in range(KC):
                        last = V_.tensor_tensor(KB[:, b, 0, g, :].rearrange("p (h k) -> p h k", k=NK),
                                                KT[:, 0, g, b * NK:(b + 1) * NK].unsqueeze(1).to_broadcast([P, HG, NK]),
                                                maskk.unsqueeze(2).to_broadcast([P, HG, NK]), ALU.mult)
                    if b == 0:
                        last.then_inc(sem("kb0_ready"), 1)
                last.then_inc(sem("kb_ready"), 1)
                q_lo(NG * l, 0, 0)
                q_lo(NG * l, 0, 1)
                for b in range(B):
                    for g in range(KC):
                        dve.wait_ge(sem("vsel_ps"), KC * (B * l + b) + g + 1)
                        n4 = NC5 - 1
                        for r, c0, nc_ in ((P, 0, n4), (ROWS[n4], n4, 1)):
                            dst = V[0:r, b, g * NC5 + c0:g * NC5 + c0 + nc_, :].rearrange("p c (j v) -> p (c j) v", v=VW)
                            V_.tensor_tensor(dst[:, :, 0:HD],
                                             ps[0:r, 2 * (b % 2) + g, c0 * 96:(c0 + nc_) * 96].rearrange("p (j v) -> p j v", v=HD),
                                             maskv[0:r, 6 * c0:6 * (c0 + nc_)].unsqueeze(2).to_broadcast([r, 6 * nc_, HD]), ALU.mult)
                            last = V_.tensor_copy(dst[:, :, HD], maskone[0:r, 6 * c0:6 * (c0 + nc_)])
                        last.then_inc(sem("v_ready"), 1)

            def norm_stats(gi, i):
                for t in range(GT):
                    ins = V_.bn_stats(stats[:, t, :], X[:, t + GT * i, :] if isinstance(i, int) else X[:, bass.ds(i * GT + t, 1), :])
                link(ins, hold)
                for t in range(GT):
                    ins = V_.bn_aggr(mv[:, t, :], stats[:, t, :])
                ins.then_inc(sem("var_ready"), 1)

            def norm(gi, i):
                dve.wait_ge(sem("rstd_ready"), gi + 1)
                for t in range(GT):
                    xt = X[:, t + GT * i, :] if isinstance(i, int) else X[:, bass.ds(i * GT + t, 1), :]
                    ins = V_.tensor_scalar(xn[:, t, :], xt, mv[:, t, 0:1], rstd[:, t:t + 1], ALU.subtract, ALU.mult)
                link(ins)
                V_.tensor_copy(xs[0], xn.rearrange("p t d -> p (t d)")).then_inc(sem("xhi_ready"), 1)

            def x_lo(gi):
                dve.wait_ge(sem("xT_ps"), 2 * gi + 2)
                V_.tensor_copy(xT[:, 1, :, :], ps[:, WF + 1, :].bitcast(F16).rearrange("p (c n) -> p c n", c=KC)).then_inc(sem("xTlo_ready"), 1)

            def q_lo(gi, par, m):
                dve.wait_ge(sem("qhi_ready"), KC * gi + m + 1)
                V_.scalar_tensor_tensor(qT[:, par, 1, m, :], ps[:, WF + m, :], bcol[:, m:m + 1], qT[:, par, 0, m, :],
                                        ALU.add, ALU.subtract).then_inc(sem("qlo_ready"), 1)

            def maxima(gi, n, other=False):
                t, g = n // KC, n % KC
                bank = WT if other and n % 2 else WF
                dve.wait_ge(sem("max_ps"), GT * KC * gi + n + 1)
                V_.tensor_reduce(mx[:, t, g * HG:(g + 1) * HG],
                                 ps[:, bank:bank + 2, 0:4 * NK].rearrange("p a (h k) -> p a h k", k=NK),
                                 AX.X, ALU.max, negate=True).then_inc(sem("max_done"), 1)

            def attend(gi, g):
                dve.wait_ge(sem("pv_ps"), NPB + NSLOT * gi + NC5 * (g + 1))
                pv = [ps[:, PV0 + u, 0:2 * HG * VW].rearrange("p (t h v) -> p t h v", t=2, v=VW) for u in range(2)]
                dve.wait_ge(sem("pv_free"), 2 + 4 * gi + 2 * g)
                for u in range(2):
                    ins = V_.reciprocal(rec[:, u], pv[u][:, :, :, HD])
                link(ins)
                for u in range(2):
                    dst = cx[:, 2 * u:2 * u + 2, g * P:(g + 1) * P].rearrange("p t (h v) -> p t h v", v=HD)
                    for t in range(2):
                        ins = V_.tensor_tensor(dst[:, t], pv[u][:, t, :, 0:HD],
                                               rec[:, u, t, :].unsqueeze(2).to_broadcast([P, HG, HD]), ALU.mult)
                    ins.then_inc(sem("pv_free"), 1)

            def ctx_hi(gi):
                dve.wait_ge(sem("pv_free"), 4 * gi + 4 + 2)
                V_.tensor_copy(cs[0], cx.rearrange("p t d -> p (t d)")).then_inc(sem("chi_ready"), 1)

            def ctx_lo(gi):
                dve.wait_ge(sem("cT_ps"), 2 * gi + 2)
                V_.tensor_copy(cT[:, 1, :, :], ps[:, WT + 1, :].bitcast(F16).rearrange("p (c n) -> p c n", c=KC)).then_inc(sem("cTlo_ready"), 1)

            def add_out(l, gi, i, u):
                dve.wait_ge(sem("o_ps"), 2 * gi + u + 1)
                dve.wait_ge(sem("xb_ready"), gi + 1)
                xt = X[:, bass.ds(i * GT + 2 * u, 2), :]
                V_.scalar_tensor_tensor(xt, ps[:, WT + u, :].rearrange("p (t d) -> p t d", t=2), gsc[:, GA[l]:GA[l] + 1], xt,
                                        ALU.mult, ALU.add).then_inc(sem("att_out"), 1)

            def router_stats(gi, i):
                dve.wait_ge(sem("att_out"), 2 * gi + 2)
                for t in range(GT):
                    ins = V_.bn_stats(rst[:, t + GT * i, :] if isinstance(i, int) else rst[:, bass.ds(i * GT + t, 1), :],
                                      X[:, t + GT * i, :] if isinstance(i, int) else X[:, bass.ds(i * GT + t, 1), :])
                ins.then_inc(sem("rst_ready"), 1)

            def p_lo(gi, par, n):
                rows = ROWS[n % NC5]
                dve.wait_ge(sem("p_ready"), NSLOT * gi + n + 3)
                buf = (NSLOT * par + n) % NPB
                V_.tensor_tensor(PP[0:rows, buf, 1, :], PT[0:rows, n % 2, :], PP[0:rows, buf, 0, :],
                                 ALU.subtract).then_inc(sem("plo_dve"), 1)

            def ternary():
                def sums():
                    dve.wait_ge(sem("fw_in"), 32)
                    V_.tensor_reduce(wsm[:, 0:1], fraw[:, 0, :], AX.X, ALU.add, apply_absolute_value=True)
                    V_.memset(onef, 1.0)

                def sums_end():
                    V_.tensor_reduce(wsm[:, 1:2], fraw[:, 1, :], AX.X, ALU.add, apply_absolute_value=True).then_inc(sem("w_sums"), 1)

                def means():
                    dve.wait_ge(sem("w_tot"), 1)
                    link(V_.tensor_scalar(wsm[:, 2:4], ps[:, 7, 0:2], 1.0 / (D * M), Q_EPS, ALU.mult, ALU.max))
                    link(V_.reciprocal(wsm[:, 4:6], wsm[:, 2:4]))

                def rounded(w):
                    link(V_.tensor_scalar(fraw[:, w, :], fraw[:, w, :], wsm[:, 4 + w:5 + w], MAGIC, ALU.mult, ALU.add))

                def clipped(w):
                    link(V_.tensor_scalar(fraw[:, w, :], fraw[:, w, :], MAGIC + 1, MAGIC - 1, ALU.min, ALU.max))

                def stored(w):
                    dst = (w1q, w2q)[w].rearrange("p c n -> p (c n)")
                    V_.tensor_scalar(dst, fraw[:, w, :], MAGIC, None, ALU.subtract).then_inc(sem("wq_ready"), 1)
                return {(0, 2): [sums], (0, 3): [sums_end], (0, 6): [means], (0, 7): [lambda: rounded(0)], (0, 8): [lambda: rounded(1)],
                        (1, 0): [lambda: clipped(0)], (1, 1): [lambda: clipped(1)], (1, 2): [lambda: stored(0)], (1, 4): [lambda: stored(1)]}

            def rows(b, t):
                return X[:, b * TB + t, :] if isinstance(b, int) else X[:, bass.ds(b * TB + t, 1), :]

            def front(b, part):
                if part == 0:
                    for t in range(TB):
                        ins = V_.bn_stats(fst[:, t, :], rows(b, t))
                    link(ins, hold)
                    for t in range(TB):
                        ins = V_.bn_aggr(fmv[:, t, :], fst[:, t, :])
                    ins.then_inc(sem("fvar_ready"), 1)
                elif part == 1:
                    dve.wait_ge(sem("frs_ready"), b + 1)
                    after(dve, "xqT_ps", 2 * b)
                    for t in range(TB):
                        ins = V_.tensor_scalar(y8[:, t, :], rows(b, t), fmv[:, t, 0:1], RS_[:, t:t + 1], ALU.subtract, ALU.mult)
                    link(ins)
                elif part == 2:
                    link(V_.tensor_reduce(AM, y8, AX.X, ALU.max, apply_absolute_value=True))
                    link(V_.tensor_tensor(AM, AM, R2, ALU.mult))
                    link(V_.tensor_scalar(AM, AM, Q_EPS, None, ALU.max))
                    V_.tensor_scalar(DN, AM, wsm[:, 2:3], 1.0 / 127, ALU.mult, ALU.mult)
                    link(V_.reciprocal(INV, AM))
                    link(V_.scalar_tensor_tensor(SC, INV, 127.0, R2, ALU.mult, ALU.mult))
                else:
                    for t in range(TB):
                        ins = V_.tensor_scalar(y8[:, t, :], y8[:, t, :], SC[:, t:t + 1], MAGIC_H, ALU.mult, ALU.add)
                    ins.then_inc(sem("z_ready"), 1)
            FRONT_LINKS = 7


            def half(l, i, par, front, stats_next, back, extra=None):
                gi = i + NG * l
                at = SLOTS["dve"]
                for n in range(NSLOT):
                    if n not in SLOTS["pool"]["lo"]:
                        p_lo(gi, par, n)
                    if front and n == at["x"]:
                        x_lo(gi + 1)
                    for m in range(KC):
                        if front and n == at[f"q{m}"]:
                            q_lo(gi + 1, 1 - par, m)
                    for m in range(GT * KC):
                        if front and n == at["max"][m]:
                            maxima(gi + 1, m)
                    if stats_next and n == at["stats"]:
                        norm_stats(gi + 2, i + 2)
                    if n == at["attend"]:
                        if back:
                            dve.wait_ge(sem("clo_ready"), gi)
                        attend(gi, 0)
                    if back and n == at["c"]:
                        ctx_lo(gi - 1)
                    if back and n == at["out"]:
                        add_out(l, gi - 1, i - 1, 0)
                        add_out(l, gi - 1, i - 1, 1)
                        if l:
                            router_stats(gi - 1, i - 1)
                    if stats_next and n == at["norm"]:
                        norm(gi + 2, i + 2)
                    for job in (extra or {}).get((par, n), ()):
                        job()
                attend(gi, 1)
                ctx_hi(gi)

            def batch(l, b, first=False, last=False):
                extra = ternary() if first and l == 0 else {}
                if last and l == 0:
                    extra = {(0, 3): [lambda: front(0, 0)], (0, 8): [lambda: front(0, 1)], (1, 1): [lambda: front(0, 2)], (1, 4): [lambda: front(0, 3)]}
                half(l, 2 * b, 0, True, not last, not first, extra)
                half(l, 2 * b + 1, 1, not last, not last, True, extra)

            def attention(l):
                V_.memset(one1, 1.0).then_inc(sem("one_set"), 1)
                if l == 0:
                    dve.wait_ge(sem("x_in"), 16)
                norm_stats(NG * l, 0)
                norm(NG * l, 0)
                prep(l)
                for n in range(KC * GT):
                    maxima(NG * l, n, other=True)
                if l == 0:
                    dve.wait_ge(sem("x_in1"), 16)
                norm_stats(NG * l + 1, 1)
                norm(NG * l + 1, 1)
                if l == 0:
                    dve.wait_ge(sem("x_in2"), 48)
                batch(l, 0, first=True)
                loop(1, B - 1, 8, lambda b: batch(l, b))
                batch(l, B - 1, last=True)
                gi = NG * (l + 1) - 1
                ctx_lo(gi)
                add_out(l, gi, NG - 1, 0)
                add_out(l, gi, NG - 1, 1)
                if l:
                    router_stats(gi, NG - 1)

            def ffn():
                dve.wait_ge(sem("att_out"), 2 * NG)
                dve.wait_ge(sem("fb_in"), 32)
                link(V_.tensor_scalar(wsm[:, 3:4], wsm[:, 3:4], gsc[:, 2:3], 1.0 / 127, ALU.mult, ALU.mult))
                V_.tensor_scalar(fb2c, fb2c, gsc[:, 2:3], None, ALU.mult).then_inc(sem("fb2_ready"), 1)

                def pre(k, b, t):
                    dve.wait_ge(sem("h_ps"), k + 1)
                    after(dve, "gl_ready", k - 1)
                    h = (2, 4)[t % 2]
                    V_.scalar_tensor_tensor(hpre[:, t % 2, :].rearrange("p (a n) -> p a n", a=2), ps[:, h:h + 2, :], D1[:, t:t + 1],
                                            fb1c.rearrange("p (a n) -> p a n", a=2), ALU.mult, ALU.add).then_inc(sem("hpre_ready"), 1)

                def small(k, t):
                    c = slice(t % 4, t % 4 + 1)
                    dve.wait_ge(sem("gl_ready"), k + 1)
                    link(V_.tensor_reduce(A2[:, c], gl[:, t % 4, :], AX.X, ALU.max, apply_absolute_value=True))
                    dve.wait_ge(sem("rr_ready"), k + 1)
                    link(V_.tensor_scalar(A2[:, c], A2[:, c], RR[:, c], Q_EPS, ALU.mult, ALU.max))
                    V_.tensor_scalar(D2[:, c], A2[:, c], wsm[:, 3:4], None, ALU.mult)
                    link(V_.reciprocal(IV2[:, c], A2[:, c]))
                    V_.tensor_scalar(S2[:, c], IV2[:, c], 127.0, RR[:, c], ALU.mult, ALU.mult).then_inc(sem("s2_ready"), 1)

                def add(k, t, b):
                    dve.wait_ge(sem("xb2_ready"), b + 1)
                    dve.wait_ge(sem("y_ps"), k + 1)
                    xt = X[:, bass.ds(k, 1), :].rearrange("p a d -> p (a d)")
                    V_.scalar_tensor_tensor(xt, ps[:, (7, 0)[t % 2], 0:D], D2[:, t % 4:t % 4 + 1], xt, ALU.mult, ALU.add).then_inc(sem("ffn_out"), 1)

                def batch(b, first=False, last=False):
                    link(V_.tensor_copy(D1, DN))
                    for t in range(TB):
                        k = TB * b + t
                        pre(k, b, t)
                        behind(k, t, b, first)
                        if t % 2:
                            ch = t // 2
                            dve.wait_ge(sem(f"w_in{ch}"), 16 * (b + 1))
                            V_.tensor_scalar(wstg[:, ch, :], wstg[:, ch, :], WS, None, ALU.mult).then_inc(sem("w_scaled"), 1)
                        if not last and t in (0, 2, 3, 4):
                            front(b + 1, (0, 2, 3, 4).index(t))

                def behind(k, t, b, first=False):
                    lag = LAGS["small"]
                    if due(t, lag, first):
                        small(k - lag, (t - lag) % TB)
                    lag = LAGS["add"]
                    if due(t, lag, first):
                        add(k - lag, (t - lag) % TB, b if t >= lag else b - 1)
                dve.sem_inc(sem("hpre_ready"), 2)
                dve.sem_inc(sem("hqT_ready"), 1)
                batch(0, first=True)
                loop(1, B - 1, 1 + 3 * TB + FRONT_LINKS, lambda b: batch(b))
                batch(B - 1, last=True)
                for n in range(LAGS["add"]):
                    behind(NT + n, TB + n, B - 1)

            def router():
                dve.wait_ge(sem("att_out"), 4 * NG)
                dve.wait_ge(sem("wr_in"), 16)
                link(V_.tensor_scalar(wrr, wrr, WS, None, ALU.mult))
                link(V_.tensor_copy(wrs[:, 0], wrr))
                V_.tensor_tensor(wrs[:, 1], wrr, wrs[:, 0], ALU.subtract).then_inc(sem("wr_split"), 1)

                dve.wait_ge(sem("rst_ready"), NG)
                for t0, t1 in ((0, GT), (GT, NT)):
                    for t in range(t0, t1):
                        ins = V_.bn_aggr(rmv[:, t, :], rst[:, t, :])
                    ins.then_inc(sem("rvar_ready"), 1)
                dve.wait_ge(sem("rrs_ready"), 1)

                def rows(g, par, r, between=lambda: None):
                    after(dve, "rlo_ready", g)
                    for t in range(GT):
                        ins = V_.tensor_scalar(rxn[:, t, :], X[:, bass.ds(g * GT + t, 1), :].rearrange("p a d -> p (a d)"),
                                               rmv[:, bass.ds(g * GT + t, 1), 0:1].rearrange("p a d -> p (a d)"), rrs[:, bass.ds(g * GT + t, 1)],
                                               ALU.subtract, ALU.mult)
                    ins.then_inc(sem("rxn_ready"), 1)
                    between()
                    dve.wait_ge(sem("rxn_ready"), g + 1)
                    dve.wait_ge(sem(("rows_even", "rows_odd")[par]), 16 * (r + 1))
                    V_.tensor_copy(xr[:, par, :, 0:D], rxn).then_inc(sem("rhi_ready"), 1)
                    dve.wait_ge(sem("rhi_ready"), g + 1)
                    V_.tensor_tensor(xr[:, par, :, D:], rxn, xr[:, par, :, 0:D], ALU.subtract).then_inc(sem("rlo_ready"), 1)

                def row_lo_t(g):
                    dve.wait_ge(sem("rT_ps"), 2 * g + 2)
                    V_.tensor_copy(xrT[:, 1], ps[:, 7, :].bitcast(F16).rearrange("p (c n) -> p c n", c=KC)).then_inc(sem("rTlo_ready"), 1)

                def logits(g):
                    dve.wait_ge(sem("lg_ps"), g + 1)
                    V_.tensor_scalar(lg[:, bass.ds(g * GT, GT), :], ps[:, 5, 0:GT * E].rearrange("p (t e) -> p t e", e=E), 1.0 / WS, None,
                                     ALU.mult).then_inc(sem("lg_ready"), 1)
                rows(0, 0, 0)
                dve.wait_ge(sem("rrs_ready"), 2)
                with dve.Fori(0, NG // 2 - 1) as r:
                    r = dve.snap(r)
                    rows(2 * r + 1, 1, r, lambda: row_lo_t(2 * r))
                    logits(2 * r)
                    rows(2 * r + 2, 0, r + 1, lambda: row_lo_t(2 * r + 1))
                    logits(2 * r + 1)
                rows(NG - 1, 1, NG // 2 - 1, lambda: row_lo_t(NG - 2))
                logits(NG - 2)
                row_lo_t(NG - 1)
                logits(NG - 1)

            def tiles(ap):
                return ap.unsqueeze(1).to_broadcast([P, NT, E])

            def choices(ap):
                return ap.unsqueeze(2).to_broadcast([P, NT, E])

            def whole(ap):
                link(V_.tensor_scalar(ap, ap, MAGIC, None, ALU.add))
                link(V_.tensor_scalar(ap, ap, MAGIC, None, ALU.subtract))

            def dispatch():
                link(V_.tensor_scalar(desc, iota[:, 0:E], -1.0, float(E), ALU.mult, ALU.add))
                dve.wait_ge(sem("lg_ready"), NG + 1)
                for k in range(TOPK):
                    link(V_.tensor_reduce(top[:, k], lg, AX.X, ALU.max))
                    link(V_.tensor_tensor(ta, lg, choices(top[:, k]), ALU.is_equal))
                    link(V_.tensor_tensor(ta, ta, tiles(desc), ALU.mult))
                    link(V_.tensor_reduce(top_s, ta, AX.X, ALU.max))
                    link(V_.tensor_tensor(oh[:, k], ta, choices(top_s), ALU.is_equal))
                    if k == 0:
                        link(V_.scalar_tensor_tensor(lg, oh[:, 0], -1e37, lg, ALU.mult, ALU.add))
                V_.tensor_tensor(Mb, oh[:, 0], oh[:, 1], ALU.add).then_inc(sem("m_ready"), 1)
                V_.tensor_tensor(wts[:, 0], top[:, 1], top[:, 0], ALU.subtract).then_inc(sem("tops_ready"), 1)
                dve.wait_ge(sem("exp_ready"), 1)
                link(V_.tensor_scalar(wts[:, 1], wts[:, 0], 1.0, None, ALU.add))
                link(V_.reciprocal(wts[:, 1], wts[:, 1]))
                link(V_.tensor_scalar(wts[:, 1], wts[:, 1], gsc[:, 3:4], None, ALU.mult))
                link(V_.tensor_tensor(wts[:, 2], wts[:, 0], wts[:, 1], ALU.mult))
                link(V_.tensor_tensor(gates, oh[:, 0], choices(wts[:, 1]), ALU.mult))
                link(V_.tensor_tensor(ta, oh[:, 1], choices(wts[:, 2]), ALU.mult))
                V_.tensor_tensor(gates, gates, ta, ALU.add).then_inc(sem("gates_ready"), 1)
                dve.wait_ge(sem("rank_ps"), 1)
                link(V_.tensor_copy(cnt, ps[:, 4, NT * E:(NT + 1) * E]))
                link(V_.tensor_scalar(nb, cnt, 1.0 / ST, 0.5 - 0.5 / ST, ALU.mult, ALU.add))
                whole(nb)
                link(V_.tensor_copy(ce, nb))
                src, dst = ce, ce2
                for step in (1, 2, 4):
                    link(V_.tensor_copy(dst[:, 0:step], src[:, 0:step]))
                    link(V_.tensor_tensor(dst[:, step:E], src[:, step:E], src[:, 0:E - step], ALU.add))
                    src, dst = dst, src
                ends = src
                link(V_.tensor_tensor(base_e, ends, nb, ALU.subtract))
                link(V_.tensor_scalar(base_e, base_e, float(ST), None, ALU.mult))
                link(V_.tensor_tensor(ta, ps[:, 4, 0:NT * E].rearrange("p (t e) -> p t e", e=E), tiles(base_e), ALU.add))
                for k in range(TOPK):
                    link(V_.tensor_tensor(tb, oh[:, k], ta, ALU.mult))
                    link(V_.tensor_reduce(pos[:, k * NT:(k + 1) * NT], tb, AX.X, ALU.add))
                link(V_.tensor_scalar(phi, pos, 1.0 / P, -(0.5 - 0.5 / P), ALU.mult, ALU.add))
                whole(phi)
                ins = V_.scalar_tensor_tensor(pos, phi, -float(P), pos, ALU.mult, ALU.add)
                ins.then_inc(sem("pos_ready"), 1)
                dve.wait_ge(sem("pos_ready"), 1)
                dve.wait_ge(sem("x_out"), 16 * NG)
                for n in range(NPC):
                    dve.wait_ge(sem("onehot_used"), n + 1)
                    V_.tensor_tensor(ohL[n % 2], iota.unsqueeze(1).to_broadcast([P, PC, P]),
                                     pos[:, n * PC:(n + 1) * PC].unsqueeze(2).to_broadcast([P, PC, P]), ALU.is_equal)
                    V_.tensor_tensor(ohH[n % 2], iota[:, 0:NSC].unsqueeze(1).to_broadcast([P, PC, NSC]),
                                     phi[:, n * PC:(n + 1) * PC].unsqueeze(2).to_broadcast([P, PC, NSC]), ALU.is_equal).then_inc(sem("onehot_ready"), 1)
                link(V_.tensor_tensor(cmpb, ends.unsqueeze(1).to_broadcast([P, NSP, E]), iota[:, 0:NSP].unsqueeze(2).to_broadcast([P, NSP, E]), ALU.is_le))
                link(V_.tensor_reduce(exf, cmpb, AX.X, ALU.add))
                V_.tensor_scalar(exi, exf, float(E - 1), None, ALU.min).then_inc(sem("ex_ready"), 1)
                dve.wait_ge(sem("onehot_used"), NPC + 2)
                link(V_.tensor_copy(idh, ps[:, 6, 0:NSC]))
                link(V_.tensor_copy(idn, idh.bitcast(U16)))
                link(V_.tensor_scalar(idn, idn, float(CODE0), None, ALU.subtract))
                V_.tensor_scalar(gidx, idn, 0.0, None, ALU.max)
                link(V_.tensor_scalar(idt, idn, 0.0, FAR, ALU.is_lt, ALU.mult))
                link(V_.tensor_tensor(sidx, idn, idt, ALU.add))

            def experts():
                def cols(ap, j):
                    return ap[:, bass.ds(2 * j, 2)]

                def rows_t(j, par):
                    dve.wait_ge(sem("xsT_ps"), j + 1)
                    after(dve, "eh_ps", 4 * j - 4)
                    V_.tensor_copy(xsT[:, par], ps[:, 0, :].bitcast(F16).rearrange("p (w c n) -> p w c n", w=2, c=KC)).then_inc(sem("xsT_ready"), 1)

                def take_gates(j, par, e):
                    after(dve, "ey_out", 2 * j - 2)
                    V_.tensor_copy(gcur[:, par].unsqueeze(2), xgf[:, par, :, bass.ds(e + D, 1)]).then_inc(sem("gate_ready"), 1)

                def expert_of(j):
                    return dve.value_load(exi[0:1, j:j + 1] if isinstance(j, int) else exi[0:1, bass.ds(j, 1)], min_val=0, max_val=E - 1)

                def split(j, par):
                    def hi(q):
                        dve.wait_ge(sem("gelu_done"), 4 * j + q + 5)
                        if q == 0:
                            after(dve, "ey_ps", 2 * j)
                        V_.tensor_copy(hid[:, par, 0, q * 512:(q + 1) * 512], gel[:, q, :]).then_inc(sem("hhi_ready"), 1)

                    def lo(q):
                        dve.wait_ge(sem("hhi_ready"), 4 * j + q + 1)
                        V_.tensor_tensor(hid[:, par, 1, q * 512:(q + 1) * 512], gel[:, q, :], hid[:, par, 0, q * 512:(q + 1) * 512],
                                         ALU.subtract).then_inc(sem("hlo_ready"), 1)
                    for q in range(4):
                        hi(q)
                        lo(q)

                def output(j, par, e):
                    for s_ in range(2):
                        dve.wait_ge(sem("ey_ps"), 2 * j + s_ + 3)
                        after(dve, "scattered", 16 * (2 * j + s_ - 3))
                        V_.tensor_copy(scatter_now[:, par, s_:s_ + 1], sidx[:, bass.ds(2 * j + s_, 1)])
                        y = yb[:, par, s_, :]
                        V_.scalar_tensor_tensor(y, ps[:, 5 + s_, 0:D], 1.0 / WS, b2t[:, bass.ds(e, 1), :].rearrange("p a n -> p (a n)"),
                                                ALU.mult, ALU.add).then_inc(sem("ey_done"), 1)
                        dve.wait_ge(sem("ey_done"), 2 * j + s_ + 3)
                        V_.tensor_scalar(y, y, gcur[:, par, s_:s_ + 1], None, ALU.mult).then_inc(sem("ey_out"), 1)
                for j in range(2):
                    V_.tensor_copy(gather_now[:, j], cols(gidx, j)).then_inc(sem("gidx_ready"), 1)
                e0 = expert_of(0)
                rows_t(0, 0)
                take_gates(0, 0, e0)
                V_.tensor_copy(gather_now[:, 0], cols(gidx, 2)).then_inc(sem("gidx_ready"), 1)
                split(0, 0)
                rows_t(1, 1)
                take_gates(1, 1, expert_of(1))
                V_.tensor_copy(gather_now[:, 1], cols(gidx, 3)).then_inc(sem("gidx_ready"), 1)

                def pair(r):
                    for u in range(2):
                        j = 2 * r + u
                        split(j + 1, 1 - u)
                        rows_t(j + 2, u)
                        V_.tensor_copy(gather_now[:, u], cols(gidx, j + 4)).then_inc(sem("gidx_ready"), 1)
                        output(j, u, expert_of(j))
                        take_gates(j + 2, u, expert_of(j + 2))
                dve.wait_ge(sem("b2_in"), 16)
                pair(0)
                with dve.Fori(1, (NST - 1) // 2) as r:
                    pair(dve.snap(r))
                output(NST - 1, (NST - 1) % 2, expert_of(NST - 1))

            dve.sem_inc(sem("rows_even"), 16)
            dve.sem_inc(sem("rows_odd"), 16)
            dve.sem_inc(sem("lg_ready"), 1)
            dve.sem_inc(sem("onehot_used"), 2)
            dve.sem_inc(sem("xsT_ready"), 1)
            dve.sem_inc(sem("ey_done"), 2)
            dve.sem_inc(sem("ey_ps"), 2)
            dve.sem_inc(sem("hlo_ready"), 4)
            dve.sem_inc(sem("pv_free"), 2)
            for n in sorted({lo_split(n)[:2] for n in range(NSLOT)}):
                dve.sem_inc(sem(n[0]), n[1])
            dve.sem_inc(sem("pv_ps"), NPB)
            V_.memset(mhalf[:], -0.5).then_inc(sem("half_set"), 1)
            dve.wait_ge(sem("tanh"), 2)
            link(V_.tensor_scalar(gsc[:, 0:2], gsc[:, 4:6], 1.0 / WS, None, ALU.mult))
            attention(0)
            ffn()
            attention(1)
            router()
            dispatch()
            experts()

        @block.gpsimd
        def _(pool):
            G = nc.gpsimd
            base = [0, 0]

            def link(ins):
                base[1] += 1
                ins.then_inc(sem("pool_link"), 1)
                hold(pool, "pool_link", base[0] + base[1])

            def loop(lo, hi, links, body):
                start = base[0] + base[1]
                with pool.Fori(lo, hi) as r:
                    r = pool.snap(r)
                    base[0], base[1] = r * links + (start - lo * links), 0
                    body(r)
                    assert base[1] == links, base[1]
                base[0], base[1] = start + (hi - lo) * links, 0

            def prep(l):
                for b in range(B):
                    pool.wait_ge(sem("klo_ready"), KC * (l + 1))
                    for g in range(KC):
                        last = G.tensor_tensor(KB[:, b, 1, g, :].rearrange("p (h k) -> p h k", k=NK),
                                               KT[:, 1, g, b * NK:(b + 1) * NK].unsqueeze(1).to_broadcast([P, HG, NK]),
                                               maskk.unsqueeze(2).to_broadcast([P, HG, NK]), ALU.mult)
                last.then_inc(sem("kb_ready"), 1)

            def rsqrt(gi):
                hold(pool, "var_ready", gi + 1)
                link(G.tensor_scalar(rstd[:, 0:GT], mv[:, 0:GT, 1], LN_EPS, None, ALU.add))
                G.tensor_tensor(rstd[:, 0:GT], rstd[:, 0:GT], mhalf[:, 0:GT], ALU.pow).then_inc(sem("rstd_ready"), 1)

            def x_lo(gi):
                hold(pool, "xhi_ready", gi + 1)
                G.tensor_tensor(xs[1], xn.rearrange("p t d -> p (t d)"), xs[0], ALU.subtract).then_inc(sem("xlo_ready"), 1)

            def c_lo(gi):
                hold(pool, "chi_ready", gi + 1)
                G.tensor_tensor(cs[1], cx.rearrange("p t d -> p (t d)"), cs[0], ALU.subtract).then_inc(sem("clo_ready"), 1)

            def add_bias(gi, i):
                xt = X[:, bass.ds(i * GT, GT), :]
                G.tensor_tensor(xt, xt, gbo.unsqueeze(1).to_broadcast([P, GT, D]), ALU.add).then_inc(sem("xb_ready"), 1)

            def scales(b):
                hold(pool, "fvar_ready", b + 1)
                var = fmv[:, :, 1]
                link(G.tensor_scalar(VE, var, LN_EPS, None, ALU.add))
                link(G.tensor_tensor(RS_, VE, mhalf[:], ALU.pow))
                link(G.tensor_tensor(R2, RS_, RS_, ALU.mult))
                link(G.tensor_tensor(R2, R2, var, ALU.mult))
                link(G.tensor_scalar(R2, R2, RMS_EPS, None, ALU.add))
                G.tensor_tensor(R2, R2, mhalf[:], ALU.pow).then_inc(sem("frs_ready"), 1)

            def half(l, i, par, stats_next, back, extra=None):
                gi = i + NG * l
                at = SLOTS["pool"]
                for n in range(NSLOT):
                    if n in at["lo"]:
                        rows = ROWS[n % NC5]
                        hold(pool, "p_ready", NSLOT * gi + n + 3)
                        buf = (NSLOT * par + n) % NPB
                        G.tensor_tensor(PP[0:rows, buf, 1, :], PT[0:rows, n % 2, :], PP[0:rows, buf, 0, :],
                                        ALU.subtract).then_inc(sem("plo_pool"), 1)
                    if back and n == at["c"]:
                        c_lo(gi - 1)
                    if stats_next and n == at["rsqrt"]:
                        rsqrt(gi + 2)
                    if back and n == at["bias"]:
                        add_bias(gi - 1, i - 1)
                    if stats_next and n == at["x"]:
                        x_lo(gi + 2)
                    for job in (extra or {}).get((par, n), ()):
                        job()

            def batch(l, b, first=False, last=False):
                extra = {(0, 5): [lambda: scales(0)]} if last and l == 0 else {}
                half(l, 2 * b, 0, not last, not first, extra)
                half(l, 2 * b + 1, 1, not last, True, extra)

            def attention(l):
                pool.wait_ge(sem("half_set"), 1)
                rsqrt(NG * l)
                x_lo(NG * l)
                prep(l)
                rsqrt(NG * l + 1)
                x_lo(NG * l + 1)
                batch(l, 0, first=True)
                loop(1, B - 1, 2, lambda b: batch(l, b))
                batch(l, B - 1, last=True)
                c_lo(NG * (l + 1) - 1)
                add_bias(NG * (l + 1) - 1, NG - 1)

            def weights_lo(e, ch):
                hold(pool, "whi_done", 4 * e + ch + 1)
                c0 = (ch // 2) * 4 * M + (ch % 2) * M
                hi, lo = (WE[:, e, c:c + M] if isinstance(e, int) else WE[:, bass.ds(e, 1), c:c + M].rearrange("p a n -> p (a n)")
                          for c in (c0, c0 + 2 * M))
                G.tensor_tensor(lo, wstg[:, ch, :], hi, ALU.subtract).then_inc(sem("wlo_done"), 1)

            def ffn():
                pool.wait_ge(sem("fb2_ready"), 1)

                def bias(b):
                    pool.wait_ge(sem("z_ready"), b + 1)
                    xb = X[:, b * TB:(b + 1) * TB, :] if isinstance(b, int) else X[:, bass.ds(b * TB, TB), :]
                    G.tensor_tensor(xb, xb, fb2c.unsqueeze(1).to_broadcast([P, TB, D]), ALU.add).then_inc(sem("xb2_ready"), 1)

                def hidden_rsqrt(k, t):
                    c = slice(t % 4, t % 4 + 1)
                    hold(pool, "ms_ready", k + 1)
                    link(G.tensor_scalar(RR[:, c], MS[:, c], RMS_EPS, None, ALU.add))
                    G.tensor_tensor(RR[:, c], RR[:, c], mhalf[:, 0:1], ALU.pow).then_inc(sem("rr_ready"), 1)

                def batch(b, first=False, last=False):
                    for t in range(TB):
                        hidden_rsqrt(TB * b + t, t)
                        if not last and t == 1:
                            scales(b + 1)
                        if not last and t == 5:
                            bias(b + 1)
                        if t % 2 and (t > 1 or not first):
                            weights_lo(b if t > 1 else b - 1, t // 2 - 1 if t > 1 else 3)
                bias(0)
                batch(0, first=True)
                loop(1, B - 1, TB + 5, lambda b: batch(b))
                batch(B - 1, last=True)
                weights_lo(E - LATE - 1, 3)

            def router():
                for n, (t0, t1) in enumerate(((0, GT), (GT, NT))):
                    pool.wait_ge(sem("rvar_ready"), n + 1)
                    link(G.tensor_scalar(rrs[:, t0:t1], rmv[:, t0:t1, 1], LN_EPS, None, ALU.add))
                    G.tensor_tensor(rrs[:, t0:t1], rrs[:, t0:t1], mhalf[:, 0:1].to_broadcast([P, t1 - t0]), ALU.pow).then_inc(sem("rrs_ready"), 1)
                with pool.Fori(E - LATE, E) as e:
                    e = pool.snap(e)
                    for ch in range(4):
                        weights_lo(e, ch)
                for n in range(NPC):
                    pool.wait_ge(sem("onehot_ready"), n + 1)
                    t0 = n * PC % NT
                    G.tensor_tensor(ohH[n % 2], ohH[n % 2], code[:, t0:t0 + PC].unsqueeze(2).to_broadcast([P, PC, NSC]),
                                    ALU.mult).then_inc(sem("onehot_codes"), 1)

            def experts():
                def gather(j, par):
                    hold(pool, "gidx_ready", j + 1)
                    hold(pool, "xsT_ps", j - 1)
                    hold(pool, "gate_ready", j - 1)
                    for s_ in range(2):
                        G.indirect_dma_start(xgat[:, par, s_, :].bitcast(U16), None, rowsd, bass.IndirectOffsetOnAxis(ap=gather_now[:, par, s_:s_ + 1], axis=0)
                                             ).then_inc(sem(("gathered_even", "gathered_odd")[par]), 16)

                def scatter(j, par):
                    for s_ in range(2):
                        n = 2 * j + s_
                        hold(pool, "ey_out", n + 1)
                        hold(pool, "scattered", 16 * n)
                        G.indirect_dma_start(out, bass.IndirectOffsetOnAxis(ap=scatter_now[:, par, s_:s_ + 1], axis=0), yb[:, par, s_, :], None,
                                             bounds_check=B * S - 1, oob_is_err=False, compute_op=ALU.add).then_inc(sem("scattered"), 16)
                pool.wait_ge(sem("rows_even"), 16 * (NG // 2 + 1))
                pool.wait_ge(sem("rows_odd"), 16 * (NG // 2 + 1))
                pool.wait_ge(sem("gates_out"), 16)
                pool.wait_ge(sem("x_out"), 16 * NG)
                gather(0, 0)
                gather(1, 1)
                gather(2, 0)

                def pair(r):
                    for u in range(2):
                        gather(2 * r + u + 3, 1 - u)
                        scatter(2 * r + u, u)
                pair(0)
                with pool.Fori(1, (NST - 1) // 2) as r:
                    pair(pool.snap(r))
                scatter(NST - 1, (NST - 1) % 2)
            pool.sem_inc(sem("wlo_done"), 4)
            pool.wait_ge(sem("c_in"), 96)
            attention(0)
            ffn()
            attention(1)
            router()
            experts()


def constants():
    p = np.arange(P)
    c32 = np.zeros((P, C_END), np.float32)
    c32[:, C_MASKK:C_MASKK + HG] = p[:, None] // HD == np.arange(HG)
    for c in range(NC5):
        for j in range(3):
            own = (P * c + p) // NK == HEAD0[c] + j
            c32[:, C_MASKV + 6 * c + j] = c32[:, C_MASKV + 6 * c + 3 + j] = own
            c32[:, C_ONE + 6 * c + j] = own
    ids = CODE0 + np.arange(NT) * P + p[:, None]
    c32[:, C_CODE:C_CODE + NT] = ids.astype(np.uint16).view(np.float16)
    c32[:, C_IOTA:] = np.arange(P)
    one_f, one_b = 0x3C00, 0x3F80
    c16 = np.zeros((P, H_END), np.uint16)
    c16[:, H_IDF:H_IDF + P] = np.eye(P) * one_f
    c16[:, H_IDB:H_IDB + P] = np.eye(P) * one_b
    c16[:, H_UP:H_UP + P] = (p[:, None] < p) * one_b
    c16[:, H_ONES:] = one_b
    ind = (np.arange(H)[:, None] == np.arange(KC * FK) // NK) * one_b
    selk = (p[:, None] == np.arange(FK) % NK) * one_f
    return c32, c16, ind.astype(np.uint16), selk.astype(np.uint16)


def kernel(**inputs):
    import concourse.bacc as _bacc
    from concourse.bass_utils import run_bass_kernel_spmd as _run
    a = {k: np.asarray(v) for k, v in inputs.items()}
    c = np.ascontiguousarray
    zero = np.zeros(D, np.float32)
    L1 = {k: a[f"L1_xattn_{k}"] for k in ("Wq", "Wk", "Wv", "Wo", "bq", "bk", "bv", "bo")}
    bcol = [np.stack([q.reshape(KC, P), k.reshape(KC, P)]).reshape(2 * KC, P).T
            for q, k in ((zero, zero), (L1["bq"], L1["bk"]))]
    c32, c16, ind, selk = constants()
    arrays = {
        "x": c(a["x"]),
        "ctxT": c(a["ctx_1024"].reshape(B * NK, D).T),
        "g_att": c(a["g_xattn"]), "g_ffn": c(a["g_ffn"]),
        "attn_w": np.stack([np.stack([a[f"L0_xattn_{w}"] for w in ("Wq", "Wk", "Wv", "Wo")]),
                            np.stack([L1[w].T for w in ("Wq", "Wk", "Wv", "Wo")])]),
        "attn_bcol": c(np.stack(bcol)),
        "attn_brow": np.stack([np.stack([zero, a["L0_xattn_bo"]]), np.stack([L1["bv"], L1["bo"]])]),
        "fw1": c(a["L0_ffn_w1"].T), "fb1": c(a["L0_ffn_b1"]),
        "fw2": c(a["L0_ffn_w2"].T), "fb2": c(a["L0_ffn_b2"]),
        "wr": c(a["L1_ffn_Wr"].T),
        "ew1": c(a["L1_ffn_W1"].transpose(0, 2, 1)),
        "eb1": c(a["L1_ffn_b1"].reshape(E, MC, P).transpose(2, 0, 1).reshape(P, E * MC)),
        "ew2": c(a["L1_ffn_W2"].transpose(0, 2, 1)),
        "eb2": c(a["L1_ffn_b2"]),
        "c32": c32, "c16": c16, "ind": ind, "selk": selk,
    }
    nc = _bacc.Bacc("TRN2", target_bir_lowering=False, num_devices=1)
    args = {k: nc.dram_tensor(k, v.shape, mybir.dt.from_np(v.dtype), kind="ExternalInput").ap() for k, v in arrays.items()}
    args["out"] = nc.dram_tensor("out", (B * S, D), F32, kind="ExternalOutput").ap()
    build(nc, **args)
    r = _run(nc, [arrays], core_ids=[0])
    return r.results[0]["out"].reshape(B, S, D)
```
